# Optimizing a Trainium2 kernel written in Bass

```python
import numpy as np
import jax
import jax.numpy as jnp

def _softmax(x, axis=-1):
    return jax.nn.softmax(x, axis=axis)

def _gelu(x):
    return jax.nn.gelu(x, approximate=True)

def _silu(x):
    return jax.nn.silu(x)

def _sigmoid(x):
    return jax.nn.sigmoid(x)

def _layernorm(x, axis=-1, eps=1e-05):
    m = jnp.mean(x, axis=axis, keepdims=True)
    v = jnp.var(x, axis=axis, keepdims=True)
    return (x - m) / jnp.sqrt(v + eps)

def _scatter_add(tgt, idx, src, axis=0):
    return tgt.at[idx].add(src)

def _segment_sum(src, seg, n):
    return jax.ops.segment_sum(src, seg, n)
kernel_name = 'mk_gnn_preln_d4_gnn_r8_7a5aea'

def setup_inputs(seed: int=0):
    np.random.seed(seed)
    _w = jnp.asarray

    def _rec_inputs():
        import jax
        import jax.numpy as jnp
        _gk = jax.random.key(seed)
        x = -0.0003713 + 1 * jax.random.normal(jax.random.fold_in(_gk, 1), (6250, 256), jnp.float32)
        src = jax.random.randint(jax.random.fold_in(_gk, 2), (100000,), 0, 6250, jnp.int32)
        dst = jax.random.randint(jax.random.fold_in(_gk, 3), (100000,), 0, 6250, jnp.int32)
        _o = jnp.argsort(dst, stable=True)
        src = src[_o]
        dst = dst[_o]
        edge_type_16 = jax.random.randint(jax.random.fold_in(_gk, 13), (100000,), 0, 16, jnp.int32)
        edge_weight = jax.random.uniform(jax.random.fold_in(_gk, 14), (100000,), jnp.float32, 0.0, 1)
        edge_weight1 = jax.random.uniform(jax.random.fold_in(_gk, 15), (100000, 1), jnp.float32, 0.0, 1)
        return (x, src, dst, edge_type_16, edge_weight, edge_weight1)
    x, src, dst, edge_type_16, edge_weight, edge_weight1 = _rec_inputs()

    def _L0_gnn_setup():
        import jax, jax.numpy as jnp
        import numpy as np
        N_NODES = 6250
        N_EDGES = 200000
        D = 256

        def spmm(edge_row, edge_col, edge_val, dense):
            msgs = edge_val[:, None] * dense[edge_col]
            return jax.ops.segment_sum(msgs, edge_row, num_segments=N_NODES)
        key = jax.random.key(seed)
        k1, k2, k3, k4, k5, k6 = jax.random.split(key, 6)
        x = jax.random.normal(k1, (N_NODES, D), dtype=jnp.float32)
        weight = jax.random.normal(k2, (D, D), dtype=jnp.float32) * (1.0 / np.sqrt(D))
        hop_logits = jnp.array([1.2, 0.0], dtype=jnp.float32)
        edge_row = jax.random.randint(k4, (N_EDGES,), 0, N_NODES, dtype=jnp.int32)
        edge_col = jax.random.randint(k5, (N_EDGES,), 0, N_NODES, dtype=jnp.int32)
        edge_val = jax.random.uniform(k6, (N_EDGES,), dtype=jnp.float32)
        return {'x': x, 'weight': weight, 'hop_logits': hop_logits, 'edge_row': edge_row, 'edge_col': edge_col, 'edge_val': edge_val}
    _L0_gnn_all = _L0_gnn_setup()
    _L0_gnn_in = {k: v for k, v in _L0_gnn_all.items() if k in ('weight', 'hop_logits')}
    del _L0_gnn_all

    def _L1_gnn_setup():
        import jax, jax.numpy as jnp
        import numpy as np
        N_NODES = 6250
        N_EDGES = 100000
        D = 256
        L = 3
        key = jax.random.key(seed)
        k1, k2, k3, k4, k5 = jax.random.split(key, 5)
        features = jax.random.normal(k1, (N_NODES, D), dtype=jnp.float32)
        scale = 1.0 / np.sqrt(D)
        W_self = jax.random.normal(k2, (L, D, D), dtype=jnp.float32) * scale
        W_neigh = jax.random.normal(k3, (L, D, D), dtype=jnp.float32) * scale
        bias = jnp.zeros((L, D), dtype=jnp.float32)
        src = jax.random.randint(k4, (N_EDGES,), 0, N_NODES, dtype=jnp.int32)
        dst = jax.random.randint(k5, (N_EDGES,), 0, N_NODES, dtype=jnp.int32)
        return {'features': features, 'W_self': W_self, 'W_neigh': W_neigh, 'bias': bias, 'src': src, 'dst': dst}
    _L1_gnn_all = _L1_gnn_setup()
    _L1_gnn_in = {k: v for k, v in _L1_gnn_all.items() if k in ('W_self', 'W_neigh', 'bias')}
    del _L1_gnn_all

    def _L2_gnn_setup():
        import jax, jax.numpy as jnp
        import numpy as np
        N_NODES = 12500
        N_EDGES = 400000
        D_FEAT = 256
        LEAKY_ALPHA = 0.2
        key = jax.random.key(seed)
        k1, k2, k3 = jax.random.split(key, 3)
        x = jax.random.normal(k1, (N_NODES, D_FEAT), dtype=jnp.float32)
        edge_index = jax.random.randint(k2, (2, N_EDGES), 0, N_NODES, dtype=jnp.int32)
        W = jax.random.normal(k3, (D_FEAT, D_FEAT), dtype=jnp.float32) * (1.0 / np.sqrt(D_FEAT))
        b = jnp.zeros((D_FEAT,), dtype=jnp.float32)
        return {'x': x, 'edge_index': edge_index, 'W': W, 'b': b}
    _L2_gnn_all = _L2_gnn_setup()
    _L2_gnn_in = {k: v for k, v in _L2_gnn_all.items() if k in ('W', 'b')}
    del _L2_gnn_all

    def _L3_gnn_setup():
        import jax, jax.numpy as jnp
        import numpy as np
        N_NODES = 6250
        N_EDGES = 100000
        NUM_RELS = 16
        FEAT = 256
        OUT = 256
        key = jax.random.key(seed)
        ks = jax.random.split(key, 7)
        h = jax.random.normal(ks[0], (N_NODES, FEAT), dtype=jnp.float32)
        norm = jax.random.uniform(ks[1], (N_EDGES, 1), dtype=jnp.float32)
        weight = jax.random.normal(ks[2], (NUM_RELS, FEAT, OUT), dtype=jnp.float32) * 0.05
        gate_weight = jax.random.normal(ks[3], (NUM_RELS, FEAT, 1), dtype=jnp.float32) * 0.05
        src = jax.random.randint(ks[4], (N_EDGES,), 0, N_NODES)
        dst = jax.random.randint(ks[5], (N_EDGES,), 0, N_NODES)
        rel_type = jax.random.randint(ks[6], (N_EDGES,), 0, NUM_RELS)
        return {'h': h, 'norm': norm, 'weight': weight, 'gate_weight': gate_weight, 'src': src, 'dst': dst, 'rel_type': rel_type}
    _L3_gnn_all = _L3_gnn_setup()
    _L3_gnn_in = {k: v for k, v in _L3_gnn_all.items() if k in ('weight', 'gate_weight')}
    del _L3_gnn_all
    return {'x': x, 'src': src, 'dst': dst, 'edge_type_16': edge_type_16, 'edge_weight': edge_weight, 'edge_weight1': edge_weight1, 'L0_gnn_weight': _L0_gnn_in['weight'], 'L0_gnn_hop_logits': _L0_gnn_in['hop_logits'], 'L1_gnn_W_self': _L1_gnn_in['W_self'], 'L1_gnn_W_neigh': _L1_gnn_in['W_neigh'], 'L1_gnn_bias': _L1_gnn_in['bias'], 'L2_gnn_W': _L2_gnn_in['W'], 'L2_gnn_b': _L2_gnn_in['b'], 'L3_gnn_weight': _L3_gnn_in['weight'], 'L3_gnn_gate_weight': _L3_gnn_in['gate_weight']}

def reference(x, src, dst, edge_type_16, edge_weight, edge_weight1, L0_gnn_weight, L0_gnn_hop_logits, L1_gnn_W_self, L1_gnn_W_neigh, L1_gnn_bias, L2_gnn_W, L2_gnn_b, L3_gnn_weight, L3_gnn_gate_weight):
    import jax
    import jax.numpy as jnp

    def _L0_gnn_ref(x, weight, hop_logits, edge_row, edge_col, edge_val):
        import jax, jax.numpy as jnp
        import numpy as np
        N_NODES = 6250
        N_EDGES = 200000
        D = 256

        def spmm(edge_row, edge_col, edge_val, dense):
            msgs = edge_val[:, None] * dense[edge_col]
            return jax.ops.segment_sum(msgs, edge_row, num_segments=N_NODES)
        residual = x
        support = x @ weight
        hop_w = jax.nn.softmax(hop_logits)
        h1 = spmm(edge_row, edge_col, edge_val, support)
        h2 = spmm(edge_row, edge_col, edge_val, h1)
        out = hop_w[0] * h1 + hop_w[1] * h2 + residual
        return jax.nn.relu(out)

    def _L1_gnn_ref(features, W_self, W_neigh, bias, src, dst):
        import jax, jax.numpy as jnp
        import numpy as np
        N_NODES = 6250
        N_EDGES = 100000
        D = 256
        L = 3
        "3-layer GraphSAGE encoder (DGL SAGEConv, mean aggregator), eval mode.\n\n            Per layer: h_neigh = mean over in-neighbors of h (messages src -> dst);\n                       out = h @ W_self + h_neigh @ W_neigh + bias; relu except last.\n            feat_drop / wrapper dropout are identity in eval mode. The wrapper's relu\n            after layers 0,1 is idempotent with SAGEConv's internal relu.\n            "
        n = features.shape[0]
        ones = jnp.ones(src.shape[0], dtype=features.dtype)
        deg = jax.ops.segment_sum(ones, dst, num_segments=n)
        inv_deg = jnp.where(deg > 0, 1.0 / jnp.maximum(deg, 1.0), 0.0)[:, None]
        h = features
        for l in range(L):
            agg = jax.ops.segment_sum(h[src], dst, num_segments=n) * inv_deg
            h = h @ W_self[l] + agg @ W_neigh[l] + bias[l]
            if l < L - 1:
                h = jax.nn.relu(h)
        return h

    def _L2_gnn_ref(x, edge_index, W, b):
        import jax, jax.numpy as jnp
        import numpy as np
        N_NODES = 12500
        N_EDGES = 400000
        D_FEAT = 256
        LEAKY_ALPHA = 0.2
        N = x.shape[0]
        row = edge_index[0]
        col = edge_index[1]
        ones = jnp.ones(row.shape[0], dtype=x.dtype)
        deg = jax.ops.segment_sum(ones, row, num_segments=N)
        deg_safe = jnp.where(deg > 0, deg, 1.0)
        dinv_sqrt = jnp.where(deg > 0, jax.lax.rsqrt(deg_safe), 0.0)
        w = dinv_sqrt[row] * dinv_sqrt[col]
        h = jax.ops.segment_sum(w[:, None] * x[col], row, num_segments=N)
        h = h @ W + b
        return jnp.where(h >= 0, h, LEAKY_ALPHA * h)

    def _L3_gnn_ref(h, norm, weight, gate_weight, src, dst, rel_type):
        import jax, jax.numpy as jnp
        import numpy as np
        N_NODES = 6250
        N_EDGES = 100000
        NUM_RELS = 16
        FEAT = 256
        OUT = 256
        n_nodes = h.shape[0]
        all_msg = jnp.einsum('nf,rfo->rno', h, weight)
        msg = all_msg[rel_type, src] * norm
        all_gate = jnp.einsum('nf,rf->rn', h, gate_weight[..., 0])
        gate = jax.nn.sigmoid(all_gate[rel_type, src])[:, None]
        msg = msg * gate
        agg = jax.ops.segment_sum(msg, dst, num_segments=n_nodes)
        return jax.nn.relu(agg)
    edge_index = jnp.stack([src, dst])
    h = jnp.maximum(_layernorm(x, axis=-1), 0.0)
    x = x + _L0_gnn_ref(h, L0_gnn_weight, L0_gnn_hop_logits, src, dst, edge_weight)
    h = jnp.maximum(_layernorm(x, axis=-1), 0.0)
    x = x + _L1_gnn_ref(h, L1_gnn_W_self, L1_gnn_W_neigh, L1_gnn_bias, src, dst)
    h = jnp.maximum(_layernorm(x, axis=-1), 0.0)
    x = x + _L2_gnn_ref(h, edge_index, L2_gnn_W, L2_gnn_b)
    h = jnp.maximum(_layernorm(x, axis=-1), 0.0)
    x = x + _L3_gnn_ref(h, edge_weight1, L3_gnn_weight, L3_gnn_gate_weight, src, dst, edge_type_16)
    return x

_drawn_inputs = setup_inputs


def setup_inputs(seed=0):
    import zlib

    import numpy as np

    out = dict(_drawn_inputs(seed))
    spreads = {'L1_gnn_bias': (0.0, 0.285), 'L2_gnn_b': (0.0, 0.715)}
    factors = {}
    for name, (base, spread) in spreads.items():
        noise = np.random.default_rng([zlib.crc32(name.encode()), seed]).standard_normal(out[name].shape)
        drawn = base * np.exp(spread * noise) if base else spread * noise
        out[name] = jnp.asarray(drawn.astype(out[name].dtype))
    for name, factor in factors.items():
        out[name] = (out[name] * factor).astype(out[name].dtype)
    return out
```

```python
import concourse.bass as bass
from concourse import mybir
from contextlib import ExitStack

P = 128
N = 6250
E = 100000
D = 256
RELS = 16
TILES = -(-N // P)
NP = TILES * P
LAST_ROWS = N - (TILES - 1) * P
CHUNKS = -(-E // P)
STEP_TILES = -(-(CHUNKS + TILES) // P)
TAB = STEP_TILES * P
GROUP = 8
LAP = 4
LAPS = -(-(CHUNKS + TILES - 1) // (GROUP * LAP))
GROUPS = LAPS * LAP
STEPS = GROUPS * GROUP
HALF = GROUP // 2
HIST_ROWS = 125
HIST_COLS = E // HIST_ROWS
NO_NODE = 1 << 20
SORT_SLOTS = 32
SORT_LAPS = HIST_COLS // SORT_SLOTS
COL_BLOCKS = -(-HIST_COLS // P)
FIELDS = 3
LN_EPS = 1e-5
LEAK = 0.2

F32 = mybir.dt.float32
I32 = mybir.dt.int32
BF16 = mybir.dt.bfloat16
ALU = mybir.AluOpType
ACT = mybir.ActivationFunctionType
AX = mybir.AxisListType
ds = bass.ds


class Steps:

    def __init__(self, sem, names):
        self.sem, self.names = sem, names

    def at(self, name, t):
        return len(self.names) * t + self.names.index(name) + 1


def over_tiles(eng, body):
    body(0, 0, 0)
    body(1, 0, 1)
    with eng.Fori(1, TILES // 2) as i:
        body(2 * i, i, 0)
        body(2 * i + 1, i, 1)
    body(TILES - 1, TILES // 2, 0)


def gnn(nc, x, src, dst, edge_type, w0, w1, L0_w, L0_hop, L1_ws, L1_wn, L1_b, L2_w, L2_b, L3_w, L3_g, out):
    ctx = ExitStack()
    with ctx:
        def sb(name, shape, dt=F32):
            return ctx.enter_context(nc.sbuf_tensor(name, shape, dt))

        def pb(name, shape, dt=F32):
            return ctx.enter_context(nc.psum_tensor(name, shape, dt))

        def sem(name):
            return ctx.enter_context(nc.semaphore(name))

        def dram(name, shape, dt=F32):
            return nc.dram_tensor(name, shape, dt).ap()

        srcD, dstD, typD = (dram(n, [TAB, P], I32) for n in ("srcD", "dstD", "typD"))
        w1D = dram("w1D", [TAB, P])
        by_srcD = dram("by_srcD", [TAB * P, FIELDS])
        tileD = [dram(f"tileD{k}", [STEP_TILES, P], I32) for k in range(2)]
        tables = [dram(f"table{l}", [NP, D]) for l in range(6)]
        rel_table = dram("rel_table", [RELS * NP, D])
        x1D = dram("x1D", [NP, D])

        acc = sb("acc", [P, TILES, D])
        keep = sb("keep", [P, TILES, D])
        ring = sb("ring", [P, LAP * GROUP, D])
        D_idx = sb("D_idx", [P, TAB], I32)
        D_rel = sb("D_rel", [P, TAB], I32)
        D_key = sb("D_key", [P, TAB])
        D_w = sb("D_w", [P, TAB])
        early = sb("early", [P, 3 * TAB + 2 * STEPS + HIST_COLS])
        S_idx = early[:, 0:TAB].bitcast(I32)
        S_key = early[:, TAB:2 * TAB]
        S_w = early[:, 2 * TAB:3 * TAB]
        hist_lo = early[0:HIST_ROWS, 3 * TAB:3 * TAB + STEPS]
        hist_hi = early[0:HIST_ROWS, 3 * TAB + STEPS:3 * TAB + 2 * STEPS]
        hist_dst = early[0:HIST_ROWS, 3 * TAB + 2 * STEPS:3 * TAB + 2 * STEPS + HIST_COLS].bitcast(I32)
        tile_row = [sb(f"tile_row{k}", [1, TAB], I32) for k in range(2)]
        onehot = sb("onehot", [P, 2 * GROUP, P])
        lo_hot = sb("lo_hot", [HIST_ROWS, GROUP, P], BF16)
        hi_hot = sb("hi_hot", [HIST_ROWS, GROUP, TILES], BF16)
        stage = sb("stage", [P, LAP * GROUP], I32)
        W = [sb(f"W{b}", [P, 2, 2 * D]) for b in range(2)]
        gw = sb("gw", [P, 2, RELS])
        bias = sb("bias", [P, 4, D])
        ident = sb("ident", [P, P])
        iota = sb("iota", [P, P])
        ones_b = sb("ones_b", [P, 1], BF16)
        zeros = sb("zeros", [P, D])
        deg_src = sb("deg_src", [P, TILES])
        dinv = sb("dinv", [P, TILES])
        inv_deg = sb("inv_deg", [P, TILES])
        dtmp = sb("dtmp", [P, TILES])
        hop = sb("hop", [P, 8])
        eps = sb("eps", [P, 1])
        part = sb("part", [P, 1])
        nx = [sb(f"nx{b}", [P, D]) for b in range(2)]
        ny = [sb(f"ny{b}", [P, D]) for b in range(2)]
        nh = [sb(f"nh{b}", [P, D]) for b in range(2)]
        nhT = [sb(f"nhT{b}", [P, 2, P]) for b in range(2)]
        nt = [sb(f"nt{b}", [P, D]) for b in range(2)]
        st6 = sb("st6", [P, 2, 6])
        mv = sb("mv", [P, 2, 4])
        gate = sb("gate", [P, 2, RELS])
        keep_row = keep[:, :, :].rearrange("p a b -> p (a b)")
        acc_row = acc[:, :, :].rearrange("p a b -> p (a b)")
        ring_row = ring[:, :, :].rearrange("p a b -> p (a b)")

        class Room:

            def __init__(self, row):
                self.row, self.at = row, 0

            def take(self, n, dt=F32):
                a = self.row[:, self.at:self.at + n]
                self.at += n
                return a if dt == F32 else a.bitcast(dt)

        cells = STEP_TILES * P
        room = Room(keep_row)
        raw_i = room.take(3 * cells, I32).rearrange("p (k i e) -> p k i e", k=3, e=P)
        raw_f = room.take(4 * cells).rearrange("p (k i e) -> p k i e", k=4, e=P)
        raw_s = room.take(FIELDS * cells).rearrange("p (i e f) -> p i e f", f=FIELDS, e=P)
        raw_k = room.take(cells).rearrange("p (i e) -> p i e", e=P)
        room = Room(acc_row)
        last_i, last_f = room.take(STEP_TILES, I32), room.take(STEP_TILES)
        thr, tnum = room.take(TILES - 1), room.take(TILES - 1)
        snum = room.take(STEP_TILES)
        step_tile, step_base = room.take(STEP_TILES), room.take(STEP_TILES)
        step_chunk = room.take(STEP_TILES, I32)
        cnt, first_step = room.take(TILES - 1), room.take(TILES - 1)
        cmp = room.take(STEP_TILES * (TILES - 1)).rearrange("p (i t) -> p i t", i=STEP_TILES)
        pad_i = room.take(3 * P, I32).rearrange("p (k e) -> p k e", e=P)
        pad_s = room.take(FIELDS * P).rearrange("p (e f) -> p e f", f=FIELDS)
        tile_i = room.take(P, I32)[0:STEP_TILES, :]
        columns = room.take(HIST_COLS)
        ones = room.take(P)
        before = room.take(HIST_COLS // 2, BF16)
        masks = [room.take(COL_BLOCKS * P // 2, BF16)[0:HIST_ROWS, :] for b in range(2)]
        picked = room.take(HIST_COLS)[0:HIST_ROWS, :]
        rank = room.take(HIST_COLS)[0:HIST_ROWS, :]
        rank_i = room.take(HIST_COLS, I32)[0:HIST_ROWS, :]
        begin = room.take(TILES + 1)[0:HIST_ROWS, :]
        in_block = room.take(8, BF16)
        hist_src = room.take(HIST_COLS, I32)[0:HIST_ROWS, :]
        hist_w = room.take(HIST_COLS)[0:HIST_ROWS, :]
        room = Room(ring_row)
        record = room.take(FIELDS * HIST_COLS)[0:HIST_ROWS, :].rearrange("p (c f) -> p c f", f=FIELDS)
        rec_stage = room.take(FIELDS * SORT_SLOTS)[0:HIST_ROWS, :].rearrange("p (c f) -> p c f", f=FIELDS)
        W3 = [ring[:, RELS:2 * RELS, :], early[:, 0:RELS * D].rearrange("p (r d) -> p r d", d=D)]
        msg = ring[:, 0:RELS, :]

        ps_sum = pb("ps_sum", [P, GROUP, D])
        ps_T = pb("ps_T", [P, 2, 2, P])
        ps_M = pb("ps_M", [P, 2, 2 * D])
        ps_h = pb("ps_h", [P, 2 * D])

        prep = {}

        def psem(name):
            if name not in prep:
                prep[name] = sem("p_" + name)
            return prep[name]

        copied = sem("inputs_copied")
        padded = sem("pads_ready")
        loaded = sem("prep_loaded")
        gath = sem("step_rows_gathered")
        weights_in = [sem(f"weights_in{n}") for n in range(5)]
        consts = sem("consts_ready")
        prep_dve = sem("prep_vector")
        prep_pe = sem("prep_tensor")
        tile_out = sem("tile_row_out")
        tile_in = sem("tile_row_in")
        sort_masks = sem("sort_masks_ready")
        sort_counts = sem("sort_counts_ready")
        sort_blocks = sem("sort_counts_out")
        sort_totals = sem("sort_totals_ready")
        sort_begins = sem("sort_begins_ready")
        sort_ranks = sem("sort_ranks_ready")
        sort_picks = sem("sort_picks")
        sort_staged = sem("sort_slots_staged")
        sorted_out = [sem(f"sorted_rows_out{h}") for h in range(2)]
        hist_in = sem("hist_in")
        misc_act = sem("small_scalar")
        misc_dve = sem("small_vector")

        passed = sem("waits_passed")
        staged = sem("indices_staged")
        gathered = [sem(f"rows_gathered{k}") for k in range(LAP)]
        hots = sem("onehots_ready")
        hist_hots = sem("hist_onehots_ready")
        half_sums = sem("half_sums_ready")
        added = sem("steps_added")
        acc_ready = sem("acc_ready")
        table_out = [sem(f"table_out{b}") for b in range(2)]

        block = ctx.enter_context(nc.Block())
        SUMS = 7

        class NodeStage:

            def __init__(self, name, kind, vector, scalar, tensor, pool):
                self.name, self.kind = name, kind
                self.v = Steps(sem(name + "_vector"), vector) if vector else None
                self.s = Steps(sem(name + "_scalar"), scalar) if scalar else None
                self.t = Steps(sem(name + "_tensor"), tensor) if tensor else None
                self.p = Steps(sem(name + "_pool"), pool) if pool else None
                self.load = [sem(f"{name}_loaded{b}") for b in range(2)]
                self.store = [sem(f"{name}_stored{b}") for b in range(2)]

        LN_V = ["stats", "moments", "rstd", "norm"]
        A = NodeStage("in", "A", LN_V + ["table"], ["std", "relu", "hT"], ["hT", "prod"], ["keep"])
        C = NodeStage("hop", "C", ["sum", "resid"] + LN_V + ["self"], ["std", "relu", "hT", "table"],
                      ["hT", "prod"], ["clear"])
        D1 = NodeStage("sage1", "D", ["sum", "self"], ["relu", "hT", "table"], ["hT", "prod"], ["clear"])
        D2 = NodeStage("sage2", "D", ["sum", "self"], ["relu", "hT", "table"], ["hT", "prod"], ["clear"])
        Es = NodeStage("sage3", "E", ["sum", "resid"] + LN_V, ["std", "relu", "scaled"], None, ["keep", "clear"])
        Fs = NodeStage("conv", "F", ["biased", "leaky", "resid"] + LN_V + [f"m{r}" for r in range(RELS) if r % 4 < 2],
                       ["dinv", "aT", "std", "relu", "hT", "gate"] + [f"m{r}" for r in range(RELS) if r % 4 >= 2],
                       ["aT", "prod", "hT", "gate"] + [f"m{r}" for r in range(0, RELS, 2)], ["keep"])
        Gs = NodeStage("out", "G", ["sum"], None, None, None)
        def wide(a):
            return a[:, :].rearrange("p (o d) -> p o d", o=1)

        def rows_of(t):
            return LAST_ROWS if isinstance(t, int) and t == TILES - 1 else P

        def node_rows(a, t, n=P):
            return a[ds(t * P, n), :] if not isinstance(t, int) else a[t * P:t * P + n, :]

        TABLE_TILES = [(TILES + 1) // 2, TILES // 2]

        @block.sync
        def _(sp):
            for a, o in ((src, srcD), (dst, dstD), (edge_type, typD), (w1, w1D)):
                flat = o.rearrange("a b -> (a b)")[0:E].rearrange("(a b) -> a b", a=16)
                sp.dma_start(flat, a.rearrange("(a b) -> a b", a=16)).then_inc(copied, 16)
            sp.wait_ge(padded, 2)
            full, part_row = TAB - CHUNKS, E % P
            for o, rows in ((srcD, pad_i[:, 0, :]), (dstD, pad_i[:, 1, :]), (typD, pad_i[:, 2, :]),
                            (w1D, zeros[:, 0:P]),
                            (by_srcD.rearrange("(a b) f -> a (b f)", b=P), pad_s.rearrange("p e f -> p (e f)"))):
                w = rows.shape[1] // P
                sp.dma_start(o[CHUNKS:TAB, :], rows[0:full, :]).then_inc(copied, 16)
                sp.dma_start(o[CHUNKS - 1:CHUNKS, part_row * w:P * w], rows[0:1, part_row * w:P * w]).then_inc(copied, 16)
            sp.wait_ge(copied, 16 * 14)
            for k in range(2):
                if k == 0:
                    sp.dma_start(last_i, dstD.rearrange("(i p) e -> p i e", p=P)[:, :, P - 1],
                                 allow_slow_non_contiguous=True).then_inc(loaded, 16)
                else:
                    for h in range(2):
                        sp.wait_ge(sorted_out[h], 16 * (SORT_SLOTS // 2) * SORT_LAPS)
                    sp.wait_ge(psem("step_chunk"), 1)
                    sp.dma_start(last_f, by_srcD.rearrange("(i p e) f -> p i (e f)", p=P, e=P)[:, :, FIELDS * P - 2],
                                 allow_slow_non_contiguous=True).then_inc(loaded, 16)
                sp.wait_ge(psem("tile_i"), k + 1)
                sp.dma_start(tileD[k], tile_i).then_inc(tile_out, 16)
                sp.wait_ge(tile_out, 16 * (k + 1))
                sp.dma_start(tile_row[k][:, :], tileD[k].rearrange("(o a) b -> o (a b)", o=1)).then_inc(tile_in, 16)

            def stores(S, buf, dest, ready):
                def at(t, i, b):
                    n = rows_of(t) if dest is out else P
                    sp.dma_start(node_rows(dest, t, n), buf[b][0:n, :]).then_inc(S.store[b], 16)
                return at

            def body(t, i, b):
                n = rows_of(t)
                if not (isinstance(t, int) and t < 2):
                    sp.wait_ge(A.v.sem, A.v.at("norm", t - 2))
                sp.dma_start(nx[b][0:n, :], node_rows(x, t, n)).then_inc(A.load[b], 16)
                if not (isinstance(t, int) and t < 1):
                    sp.wait_ge(A.v.sem, A.v.at("table", t - 1))
                    sp.dma_start(node_rows(tables[0], t - 1), nt[1 - b][:, :]).then_inc(A.store[1 - b], 16)
            sp.wait_ge(consts, 1)
            over_tiles(sp, body)
            sp.wait_ge(A.v.sem, A.v.at("table", TILES - 1))
            sp.dma_start(node_rows(tables[0], TILES - 1), nt[0][:, :]).then_inc(A.store[0], 16)

            sp.wait_ge(added, GROUP + STEPS)
            sp.dma_start(tables[1].rearrange("(t p) d -> p t d", p=P), acc[:, :, :]).then_inc(table_out[0], 16)

            sp.wait_ge(added, GROUP + 2 * STEPS)
            def body(t, i, b):
                n = rows_of(t)
                if not (isinstance(t, int) and t < 2):
                    sp.wait_ge(C.v.sem, C.v.at("resid", t - 2))
                sp.dma_start(nx[b][0:n, :], node_rows(x, t, n)).then_inc(C.load[b], 16)
                sp.wait_ge(C.v.sem, C.v.at("resid", t))
                sp.dma_start(node_rows(x1D, t), ny[b][:, :]).then_inc(C.store[b], 16)
                if not (isinstance(t, int) and t < 1):
                    sp.wait_ge(C.s.sem, C.s.at("table", t - 1))
                    sp.dma_start(node_rows(tables[2], t - 1), nt[1 - b][:, :]).then_inc(C.store[1 - b], 16)
            over_tiles(sp, body)
            sp.wait_ge(C.s.sem, C.s.at("table", TILES - 1))
            sp.dma_start(node_rows(tables[2], TILES - 1), nt[0][:, :]).then_inc(C.store[0], 16)

            for S, tab in ((D1, tables[3]), (D2, tables[4])):
                def body(t, i, b):
                    sp.wait_ge(S.s.sem, S.s.at("table", t))
                    sp.dma_start(node_rows(tab, t), nt[b][:, :]).then_inc(S.store[b], 16)
                over_tiles(sp, body)

            sp.wait_ge(C.store[0], 32 * TABLE_TILES[0])
            sp.wait_ge(C.store[1], 32 * TABLE_TILES[1])
            sp.wait_ge(D2.v.sem, D2.v.at("self", TILES - 1))
            def body(t, i, b):
                if not (isinstance(t, int) and t < 2):
                    sp.wait_ge(Es.v.sem, Es.v.at("resid", t - 2))
                sp.dma_start(nx[b][:, :], node_rows(x1D, t)).then_inc(Es.load[b], 16)
                if not (isinstance(t, int) and t < 1):
                    sp.wait_ge(Es.s.sem, Es.s.at("scaled", t - 1))
                    sp.dma_start(node_rows(tables[5], t - 1), nt[1 - b][:, :]).then_inc(Es.store[1 - b], 16)
            over_tiles(sp, body)
            sp.wait_ge(Es.s.sem, Es.s.at("scaled", TILES - 1))
            sp.dma_start(node_rows(tables[5], TILES - 1), nt[0][:, :]).then_inc(Es.store[0], 16)

            dest = rel_table.rearrange("(r n) d -> n r d", r=RELS)
            def body(t, i, b):
                sp.wait_ge(Fs.v.sem, Fs.v.at(f"m{RELS - 3}", t))
                sp.wait_ge(Fs.s.sem, Fs.s.at(f"m{RELS - 1}", t))
                to = dest[t * P:(t + 1) * P, :, :] if isinstance(t, int) else dest[ds(t * P, P), :, :]
                sp.dma_start(to, msg).then_inc(Fs.store[b], 16)
            over_tiles(sp, body)

            def body(t, i, b):
                n = rows_of(t)
                sp.wait_ge(Gs.v.sem, Gs.v.at("sum", t))
                sp.dma_start(node_rows(out, t, n), nt[b][0:n, :]).then_inc(Gs.store[b], 16)
            over_tiles(sp, body)
            for b in range(2):
                sp.wait_ge(Gs.store[b], 16 * TABLE_TILES[b])

        @block.scalar
        def _(act):
            act.dma_start(W[0][:, :, 0:D], L0_w.rearrange("(k p) n -> p k n", p=P)).then_inc(weights_in[0], 16)

            def load_sage(l, n):
                act.dma_start(W[n % 2][:, :, 0:D], L1_ws[l].rearrange("(k p) n -> p k n", p=P)).then_inc(weights_in[n], 16)
                act.dma_start(W[n % 2][:, :, D:2 * D], L1_wn[l].rearrange("(k p) n -> p k n", p=P)).then_inc(weights_in[n], 16)
            load_sage(0, 1)
            for l in range(3):
                act.dma_start(bias[:, l, :], L1_b[l:l + 1, :].to_broadcast([P, D])).then_inc(hist_in, 16)
            act.dma_start(bias[:, 3, :], L2_b.rearrange("(o d) -> o d", o=1).to_broadcast([P, D])).then_inc(hist_in, 16)
            act.dma_start(hop[:, 0:2], L0_hop.rearrange("(o d) -> o d", o=1).to_broadcast([P, 2])).then_inc(hist_in, 16)
            act.dma_start(hist_src, src.rearrange("(p c) -> p c", p=HIST_ROWS)).then_inc(hist_in, 16)
            act.dma_start(hist_dst, dst.rearrange("(p c) -> p c", p=HIST_ROWS)).then_inc(hist_in, 16)
            act.dma_start(hist_w, w0.rearrange("(p c) -> p c", p=HIST_ROWS)).then_inc(hist_in, 16)
            for k in range(2):
                act.dma_start(gw[:, k, :], L3_g[:, k * P:(k + 1) * P, 0].rearrange("r p -> p r"),
                              allow_slow_non_contiguous=True).then_inc(hist_in, 16)
            act.wait_ge(psem("sort_start"), 1)
            def body(k):
                act.wait_ge(sort_counts, k + 1)
                if not isinstance(k, int):
                    act.wait_ge(sort_ranks, k)
                nc.scalar.copy(in_block[:, 0:COL_BLOCKS], ps_h[:, 0:COL_BLOCKS]).then_inc(sort_blocks, 1)
                act.wait_ge(sort_totals, k + 1)
                if not isinstance(k, int):
                    act.wait_ge(sort_begins, k)
                nc.scalar.activation(begin[:, ds(k + 1, 1)], ps_T[0:HIST_ROWS, 0, 0, 0:1], ACT.Identity,
                                     bias=begin[:, ds(k, 1)]).then_inc(sort_begins, 1)
            body(0)
            with act.Fori(1, TILES) as k:
                body(k)
            def body(i):
                for h in range(2):
                    if not isinstance(i, int):
                        act.wait_ge(sorted_out[h], 16 * (SORT_SLOTS // 2) * i)
                    n, at = SORT_SLOTS // 2, SORT_SLOTS * i + SORT_SLOTS // 2 * h
                    nc.scalar.copy(stage[0:HIST_ROWS, n * h:n * (h + 1)], rank_i[:, ds(at, n)]).then_inc(sort_staged, 1)
                    nc.scalar.copy(rec_stage[:, n * h:n * (h + 1), :], record[:, ds(at, n), :]).then_inc(sort_staged, 1)
            act.wait_ge(psem("records"), 1)
            body(0)
            with act.Fori(1, SORT_LAPS) as i:
                body(i)
            act.wait_ge(misc_dve, 12)
            nc.scalar.activation(hop[:, 3:5], hop[:, 3:5], ACT.Exp).then_inc(misc_act, 1)

            def ln_scalar(S, t, b):
                act.wait_ge(S.v.sem, S.v.at("moments", t))
                nc.scalar.activation(mv[:, b, 2:3], mv[:, b, 1:2], ACT.Sqrt, bias=eps[:, :]).then_inc(S.s.sem, 1)
                act.wait_ge(S.v.sem, S.v.at("norm", t))

            def transposed(S, b, t, step="hT"):
                act.wait_ge(S.t.sem, S.t.at(step, t))
                nc.scalar.copy(nhT[b][:, :, :], ps_T[:, b, :, :]).then_inc(S.s.sem, 1)

            def stage_indices(table, l):
                with act.Fori(0, LAPS) as i:
                    for k in range(LAP):
                        act.wait_ge(half_sums, 2 * (l * GROUPS + LAP * i + k + 1))
                        nc.scalar.copy(stage[:, GROUP * k:GROUP * (k + 1)],
                                       table[:, ds(GROUP * LAP * i + GROUP * k, GROUP)]).then_inc(staged, 1)

            def body(t, i, b):
                ln_scalar(A, t, b)
                if not (isinstance(t, int) and t < 2):
                    act.wait_ge(A.p.sem, A.p.at("keep", t - 2))
                    act.wait_ge(A.t.sem, A.t.at("hT", t - 2))
                nc.scalar.activation(nh[b][:, :], ny[b][:, :], ACT.Relu).then_inc(A.s.sem, 1)
                if not (isinstance(t, int) and t < 2):
                    act.wait_ge(A.t.sem, A.t.at("prod", t - 2))
                transposed(A, b, t)
            act.wait_ge(consts, 1)
            over_tiles(act, body)
            act.wait_ge(psem("tables"), 1)
            stage_indices(S_idx, 0)
            stage_indices(S_idx, 1)
            act.wait_ge(A.t.sem, A.t.at("prod", TILES - 1))

            act.wait_ge(misc_dve, 200)
            nc.scalar.activation(dinv[:, :], dinv[:, :], ACT.Sqrt).then_inc(misc_act, 1)

            def body(t, i, b):
                ln_scalar(C, t, b)
                if not (isinstance(t, int) and t < 2):
                    act.wait_ge(C.t.sem, C.t.at("hT", t - 2))
                nc.scalar.activation(nh[b][:, :], nh[b][:, :], ACT.Relu).then_inc(C.s.sem, 1)
                if not (isinstance(t, int) and t < 2):
                    act.wait_ge(C.t.sem, C.t.at("prod", t - 2))
                transposed(C, b, t)
                act.wait_ge(C.t.sem, C.t.at("prod", t))
                if not (isinstance(t, int) and t < 2):
                    act.wait_ge(C.store[b], 32 * i)
                nc.scalar.copy(nt[b][:, :], ps_sum[:, 2 * b, :]).then_inc(C.s.sem, 1)
            over_tiles(act, body)
            load_sage(1, 2)
            act.wait_ge(C.t.sem, C.t.at("prod", TILES - 1))
            load_sage(2, 3)
            stage_indices(D_idx, 2)

            for l, S in ((3, D1), (4, D2)):
                if l == 4:
                    act.wait_ge(D1.t.sem, D1.t.at("prod", TILES - 1))
                    act.dma_start(W[0][:, :, 0:D], L2_w.rearrange("(k p) n -> p k n", p=P)).then_inc(weights_in[4], 16)
                def body(t, i, b):
                    act.wait_ge(S.v.sem, S.v.at("sum", t))
                    if not (isinstance(t, int) and t < 2):
                        act.wait_ge(S.t.sem, S.t.at("hT", t - 2))
                    nc.scalar.activation(nh[b][:, :], ny[b][:, :], ACT.Relu).then_inc(S.s.sem, 1)
                    if not (isinstance(t, int) and t < 2):
                        act.wait_ge(S.t.sem, S.t.at("prod", t - 2))
                    transposed(S, b, t)
                    act.wait_ge(S.t.sem, S.t.at("prod", t))
                    if not (isinstance(t, int) and t < 2):
                        act.wait_ge(S.store[b], 16 * i)
                    nc.scalar.copy(nt[b][:, :], ps_sum[:, 2 * b, :]).then_inc(S.s.sem, 1)
                over_tiles(act, body)
                stage_indices(D_idx, l)

            def body(t, i, b):
                ln_scalar(Es, t, b)
                nc.scalar.activation(nh[b][:, :], nh[b][:, :], ACT.Relu).then_inc(Es.s.sem, 1)
                act.wait_ge(Es.s.sem, Es.s.at("relu", t))
                if not (isinstance(t, int) and t < 2):
                    act.wait_ge(Es.store[b], 16 * i)
                nc.scalar.activation(nt[b][:, :], nh[b][:, :], ACT.Copy, scale=dinv[:, ds(t, 1)]).then_inc(Es.s.sem, 1)
            over_tiles(act, body)
            stage_indices(S_idx, 5)

            act.wait_ge(half_sums, 2 * (LAP + 6 * GROUPS))
            act.wait_ge(added, GROUP + 6 * STEPS)
            for k in range(2):
                act.dma_start(W3[k], L3_w[:, k * P:(k + 1) * P, :].rearrange("r p n -> p r n")
                              ).then_inc(weights_in[4], 16)
            def body(t, i, b):
                nc.scalar.activation(wide(nh[b]), acc[:, ds(t, 1), :], ACT.Copy, scale=dinv[:, ds(t, 1)]
                                     ).then_inc(Fs.s.sem, 1)
                transposed(Fs, b, t, "aT")
                ln_scalar(Fs, t, b)
                nc.scalar.activation(nh[b][:, :], nh[b][:, :], ACT.Relu).then_inc(Fs.s.sem, 1)
                transposed(Fs, b, t, "hT")
                act.wait_ge(Fs.t.sem, Fs.t.at("gate", t))
                nc.scalar.activation(gate[:, b, :], ps_h[:, 0:RELS], ACT.Sigmoid).then_inc(Fs.s.sem, 1)
                act.wait_ge(Fs.s.sem, Fs.s.at("gate", t))
                if not (isinstance(t, int) and t < 1):
                    act.wait_ge(Fs.store[1 - b], 16 * (i + b))
                for r in [r for r in range(RELS) if r % 4 >= 2]:
                    act.wait_ge(Fs.t.sem, Fs.t.at(f"m{r // 2 * 2}", t))
                    nc.scalar.activation(msg[:, r, :], ps_sum[:, r % 8, :], ACT.Copy,
                                         scale=gate[:, b, r:r + 1]).then_inc(Fs.s.sem, 1)
            over_tiles(act, body)
            stage_indices(D_rel, 6)

        @block.gpsimd
        def _(pool):
            nc.gpsimd.memset(zeros[:, :], 0.0).then_inc(padded, 1)
            nc.gpsimd.iota(iota[:, :], pattern=[[1, P]], base=0, channel_multiplier=0,
                           allow_small_or_imprecise_dtypes=True).then_inc(psem("iota"), 1)
            nc.gpsimd.iota(thr, pattern=[[P, TILES - 1]], base=P, channel_multiplier=0,
                           allow_small_or_imprecise_dtypes=True).then_inc(psem("iota"), 1)
            nc.gpsimd.iota(tnum, pattern=[[1, TILES - 1]], base=1, channel_multiplier=0,
                           allow_small_or_imprecise_dtypes=True).then_inc(psem("iota"), 1)
            nc.gpsimd.iota(snum, pattern=[[P, STEP_TILES]], base=0, channel_multiplier=1,
                           allow_small_or_imprecise_dtypes=True).then_inc(psem("iota"), 1)
            nc.gpsimd.iota(part[:, :], pattern=[[0, 1]], base=0, channel_multiplier=1,
                           allow_small_or_imprecise_dtypes=True).then_inc(psem("iota"), 1)
            nc.gpsimd.iota(columns, pattern=[[1, HIST_COLS]], base=0, channel_multiplier=0,
                           allow_small_or_imprecise_dtypes=True).then_inc(psem("iota"), 1)
            nc.gpsimd.memset(ones[:, :], 1.0).then_inc(psem("ones"), 1)
            pool.wait_ge(psem("ones"), 1)
            nc.gpsimd.affine_select(out=ident[:, :], in_=ones[:, :], compare_op=ALU.is_equal, fill=0.0, base=0,
                                    pattern=[[-1, P]], channel_multiplier=1).then_inc(psem("iota"), 1)
            pool.wait_ge(copied, 16 * 14)
            pool.wait_ge(psem("step_chunk"), 1)
            for i in range(STEP_TILES):
                for to, table in ((raw_i[:, 0, i, :], srcD), (raw_i[:, 1, i, :], dstD), (raw_i[:, 2, i, :], typD),
                                  (raw_f[:, 3, i, :], w1D)):
                    nc.gpsimd.indirect_dma_start(
                        out=to, out_offset=None, in_=table,
                        in_offset=bass.IndirectOffsetOnAxis(ap=step_chunk[:, i:i + 1], axis=0)).then_inc(gath, 16)
            with pool.Fori(0, SORT_LAPS) as i:
                for h in range(2):
                    pool.wait_ge(sort_staged, 4 * i + 2 * h + 2)
                    pool.sem_inc(passed, 1)
                    for j in range(h * SORT_SLOTS // 2, (h + 1) * SORT_SLOTS // 2):
                        nc.gpsimd.indirect_dma_start(
                            out=by_srcD, out_offset=bass.IndirectOffsetOnAxis(ap=stage[0:HIST_ROWS, j:j + 1], axis=0),
                            in_=rec_stage[:, j, :], in_offset=None).then_inc(sorted_out[h], 16)
            for h in range(2):
                pool.wait_ge(sorted_out[h], 16 * (SORT_SLOTS // 2) * SORT_LAPS)
            pool.wait_ge(psem("step_chunk"), 2)
            for i in range(STEP_TILES):
                nc.gpsimd.indirect_dma_start(
                    out=raw_s[:, i, :, :].rearrange("p e f -> p (e f)"), out_offset=None,
                    in_=by_srcD.rearrange("(a b) f -> a (b f)", b=P),
                    in_offset=bass.IndirectOffsetOnAxis(ap=step_chunk[:, i:i + 1], axis=0)).then_inc(gath, 16)

            def body(t, i, b):
                pool.wait_ge(A.s.sem, A.s.at("relu", t))
                nc.gpsimd.tensor_copy(keep[:, ds(t, 1), :], nh[b][:, :].rearrange("p (o d) -> p o d", o=1)
                                      ).then_inc(A.p.sem, 1)
            pool.wait_ge(psem("tables"), 1)
            over_tiles(pool, body)

            def gathers(table, l, ready):
                for s, v in ready:
                    pool.wait_ge(s, v)
                with pool.Fori(0, LAPS) as i:
                    for k in range(LAP):
                        pool.wait_ge(staged, l * GROUPS + LAP * i + k + 1)
                        pool.sem_inc(passed, 1)
                        for j in range(GROUP):
                            slot = GROUP * k + j
                            nc.gpsimd.indirect_dma_start(
                                out=ring[:, slot, :], out_offset=None, in_=table,
                                in_offset=bass.IndirectOffsetOnAxis(ap=stage[:, slot:slot + 1], axis=0)
                            ).then_inc(gathered[k], 16)

            def stored(S, n=1):
                return [(S.store[b], 16 * n * TABLE_TILES[b]) for b in range(2)]

            def clear(S, step):
                def body(t, i, b):
                    pool.wait_ge(S.v.sem, S.v.at(step, t))
                    nc.gpsimd.tensor_copy(acc[:, ds(t, 1), :], zeros[:, :].rearrange("p (o d) -> p o d", o=1)
                                          ).then_inc(S.p.sem, 1)
                over_tiles(pool, body)

            gathers(tables[0], 0, stored(A))
            gathers(tables[1], 1, [(table_out[0], 16)])
            clear(C, "sum")
            gathers(tables[2], 2, stored(C, 2))
            clear(D1, "sum")
            gathers(tables[3], 3, stored(D1))
            clear(D2, "sum")
            gathers(tables[4], 4, stored(D2))
            def body(t, i, b):
                pool.wait_ge(Es.v.sem, Es.v.at("resid", t))
                nc.gpsimd.tensor_copy(keep[:, ds(t, 1), :], wide(ny[b])).then_inc(Es.p.sem, 1)
                nc.gpsimd.tensor_copy(acc[:, ds(t, 1), :], wide(zeros)).then_inc(Es.p.sem, 1)
            over_tiles(pool, body)
            gathers(tables[5], 5, stored(Es))
            def body(t, i, b):
                pool.wait_ge(Fs.v.sem, Fs.v.at("resid", t))
                nc.gpsimd.tensor_copy(keep[:, ds(t, 1), :], wide(ny[b])).then_inc(Fs.p.sem, 1)
            over_tiles(pool, body)
            gathers(rel_table, 6, stored(Fs))

        @block.vector
        def _(dve):
            n = [0]

            def step(ins):
                n[0] += 1
                ins.then_inc(prep_dve, 1)
                dve.wait_ge(prep_dve, n[0])

            step(nc.vector.memset(pad_i[:, 0, :], N))
            step(nc.vector.memset(pad_i[:, 1, :], NO_NODE))
            step(nc.vector.memset(pad_i[:, 2, :], 0))
            step(nc.vector.memset(pad_s[:, :, 0], float(N)))
            step(nc.vector.memset(pad_s[:, :, 1], float(NO_NODE)))
            step(nc.vector.memset(pad_s[:, :, 2], 0.0))
            dve.sem_inc(padded, 1)
            step(nc.vector.memset(eps[:, :], LN_EPS))
            step(nc.vector.memset(ones_b[:, :], 1.0))
            step(nc.vector.memset(nx[0][:, :], 0.0))
            step(nc.vector.memset(rank, 0.0))
            step(nc.vector.memset(begin, 0.0))
            for b in range(2):
                step(nc.vector.memset(masks[b], 0.0))
            dve.wait_ge(psem("iota"), 7)
            step(nc.vector.tensor_scalar(before, columns, part[:, 0:1], None, ALU.is_gt))
            m = [0]

            def small(ins):
                m[0] += 1
                ins.then_inc(misc_dve, 1)
                dve.wait_ge(misc_dve, m[0])

            def split(nodes):
                for half, op, by in ((hist_hi, ALU.logical_shift_right, 7), (hist_lo, ALU.bitwise_and, P - 1)):
                    small(nc.vector.tensor_scalar(half[:, 0:HIST_COLS].bitcast(I32), nodes, by, None, op))
                    small(nc.vector.tensor_copy(half[:, 0:HIST_COLS], half[:, 0:HIST_COLS].bitcast(I32)))
            dve.wait_ge(hist_in, 16 * 10)
            small(nc.vector.memset(hist_lo[:, HIST_COLS:STEPS], -1.0))
            small(nc.vector.memset(hist_hi[:, HIST_COLS:STEPS], -1.0))
            split(hist_src)
            dve.sem_inc(psem("sort_start"), 1)

            def mask(k, b):
                nc.vector.tensor_scalar(masks[b][:, 0:HIST_COLS], hist_hi[:, 0:HIST_COLS], iota[0:HIST_ROWS, ds(k, 1)],
                                        None, ALU.is_equal).then_inc(sort_masks, 1)

            def pick(k, b):
                dve.wait_ge(sort_ranks, k + 1)
                dve.wait_ge(sort_masks, k + 1)
                if not (isinstance(k, int) and k < 1):
                    dve.wait_ge(sort_begins, k)
                    dve.wait_ge(sort_picks, 2 * k)
                ranks = ps_sum[0:HIST_ROWS, 4 * b:4 * b + 4, :].rearrange("p a b -> p (a b)")[:, 0:HIST_COLS]
                nc.vector.scalar_tensor_tensor(picked, ranks, begin[:, ds(k, 1)], masks[b][:, 0:HIST_COLS], ALU.add,
                                               ALU.mult).then_inc(sort_picks, 1)
                dve.wait_ge(sort_picks, 2 * k + 1)
                nc.vector.tensor_tensor(rank, rank, picked, ALU.add).then_inc(sort_picks, 1)
            mask(0, 0)
            mask(1, 1)

            def body(k, b):
                pick(k, b)
                dve.wait_ge(sort_picks, 2 * k + 2)
                mask(k + 2, b)
            body(0, 0)
            body(1, 1)
            with dve.Fori(1, (TILES - 1) // 2) as i:
                body(2 * i, 0)
                body(2 * i + 1, 1)
            pick(TILES - 1, 0)
            dve.wait_ge(sort_picks, 2 * TILES)
            small(nc.vector.tensor_copy(rank_i, rank))
            small(nc.vector.tensor_copy(record[:, :, 0], hist_dst))
            small(nc.vector.tensor_copy(record[:, :, 1], hist_src))
            small(nc.vector.tensor_copy(record[:, :, 2], hist_w))
            dve.sem_inc(psem("records"), 1)

            def find_steps(k):
                dve.wait_ge(loaded, 16 * (k + 1))
                if k == 0:
                    step(nc.vector.tensor_copy(last_f, last_i))
                step(nc.vector.memset(cnt, 0.0))
                for i in range(STEP_TILES):
                    step(nc.vector.scalar_tensor_tensor(cnt, thr, last_f[:, i:i + 1], cnt, ALU.is_gt, ALU.add))
                dve.sem_inc(psem("cnt"), 1)
                dve.wait_ge(prep_pe, (STEP_TILES + 2) * k + 1)
                step(nc.vector.tensor_tensor(first_step, ps_h[:, 0:TILES - 1], tnum, ALU.add))
                for i in range(STEP_TILES):
                    step(nc.vector.tensor_scalar(cmp[:, i, :], first_step, snum[:, i:i + 1], None, ALU.is_le))
                step(nc.vector.tensor_reduce(step_tile, cmp, AX.X, ALU.add))
                step(nc.vector.tensor_tensor(step_chunk, snum, step_tile, ALU.subtract))
                step(nc.vector.tensor_scalar(step_base, step_tile, float(P), None, ALU.mult))
                dve.sem_inc(psem("step_chunk"), 1)
                dve.wait_ge(prep_pe, (STEP_TILES + 2) * k + 2)
                if k:
                    dve.wait_ge(tile_out, 16)
                nc.vector.tensor_copy(tile_i, ps_h[0:STEP_TILES, 128:128 + P]).then_inc(psem("tile_i"), 1)

            def turned(k, tables):
                for i in range(STEP_TILES):
                    dve.wait_ge(prep_pe, (STEP_TILES + 2) * k + 3 + i)
                    for q, table in enumerate(tables):
                        ins = nc.vector.tensor_copy(table[:, i * P:(i + 1) * P], ps_M[:, i % 2, q * P:(q + 1) * P])
                    ins.then_inc(psem("turned"), 1)
            find_steps(0)
            dve.wait_ge(gath, 16 * 4 * STEP_TILES)
            for i in range(STEP_TILES):
                step(nc.vector.tensor_copy(raw_f[:, 0, i, :], raw_i[:, 0, i, :]))
                step(nc.vector.tensor_scalar(raw_f[:, 1, i, :], raw_i[:, 1, i, :], step_base[:, i:i + 1], None,
                                             ALU.subtract))
                step(nc.vector.scalar_tensor_tensor(raw_f[:, 2, i, :], raw_i[:, 2, i, :], float(NP),
                                                    raw_f[:, 0, i, :], ALU.mult, ALU.add))
            dve.sem_inc(psem("step_rows"), 1)
            turned(0, (D_idx, D_key, D_rel, D_w))
            find_steps(1)
            dve.wait_ge(gath, 16 * 5 * STEP_TILES)
            for i in range(STEP_TILES):
                step(nc.vector.tensor_scalar(raw_k[:, i, :], raw_s[:, i, :, 1], step_base[:, i:i + 1], None,
                                             ALU.subtract))
            dve.sem_inc(psem("step_rows"), 1)
            turned(1, (S_idx, S_key, S_w))
            dve.wait_ge(psem("turned"), 2 * STEP_TILES)

            small(nc.vector.tensor_tensor(hop[:, 2:3], hop[:, 0:1], hop[:, 1:2], ALU.max))
            small(nc.vector.tensor_scalar(hop[:, 3:5], hop[:, 0:2], hop[:, 2:3], None, ALU.subtract))
            dve.wait_ge(misc_act, 1)
            small(nc.vector.tensor_tensor(hop[:, 5:6], hop[:, 3:4], hop[:, 4:5], ALU.add))
            small(nc.vector.reciprocal(hop[:, 5:6], hop[:, 5:6]))
            small(nc.vector.tensor_scalar(hop[:, 3:5], hop[:, 3:5], hop[:, 5:6], None, ALU.mult))

            dve.sem_inc(psem("tables"), 1)
            dve.sem_inc(consts, 1)

            def norm(S, t, b, xin, to):
                nc.vector.bn_stats(st6[:, b, :], xin[b][:, :]).then_inc(S.v.sem, 1)
                dve.wait_ge(S.v.sem, S.v.at("stats", t))
                dve.sem_inc(passed, 1)
                nc.vector.bn_aggr(mv[:, b, 0:2], st6[:, b, :]).then_inc(S.v.sem, 1)
                dve.wait_ge(S.s.sem, S.s.at("std", t))
                nc.vector.reciprocal(mv[:, b, 3:4], mv[:, b, 2:3]).then_inc(S.v.sem, 1)
                dve.wait_ge(S.v.sem, S.v.at("rstd", t))
                nc.vector.tensor_scalar(to[b][:, :], xin[b][:, :], mv[:, b, 0:1], mv[:, b, 3:4], ALU.subtract,
                                        ALU.mult).then_inc(S.v.sem, 1)

            def body(t, i, b):
                dve.wait_ge(A.load[b], 16 * i + 16)
                if not (isinstance(t, int) and t < 2):
                    dve.wait_ge(A.s.sem, A.s.at("relu", t - 2))
                norm(A, t, b, nx, ny)
                dve.wait_ge(A.t.sem, A.t.at("prod", t))
                if not (isinstance(t, int) and t < 2):
                    dve.wait_ge(A.store[b], 16 * i)
                nc.vector.tensor_copy(nt[b][:, :], ps_M[:, b, 0:D]).then_inc(A.v.sem, 1)
            over_tiles(dve, body)
            nc.vector.memset(acc[:, :, :].rearrange("p a b -> p (a b)"), 0.0).then_inc(acc_ready, 1)
            dve.sem_inc(added, GROUP)
            dve.wait_ge(acc_ready, 1)

            tiles_r = [dve.alloc_register(f"step_tile{j}") for j in range(GROUP)]

            def sums(l, key, weight, hist):
                row = tile_row[1 if key is S_key else 0]
                with dve.Fori(0, GROUPS // 2) as i:
                    for k in range(2):
                        g = 2 * i + k
                        dve.wait_ge(half_sums, 2 * (l * GROUPS + g + LAP - 1))
                        for j in range(GROUP):
                            o, s = onehot[:, GROUP * k + j, :], GROUP * g + j
                            if weight is None:
                                ins = nc.vector.tensor_scalar(o, iota[:, :], key[:, ds(s, 1)], None, ALU.is_equal)
                            else:
                                ins = nc.vector.tensor_scalar(o, iota[:, :], key[:, ds(s, 1)], weight[:, ds(s, 1)],
                                                              ALU.is_equal, ALU.mult)
                            ins.then_inc(hots, 1)
                        if hist:
                            dve.wait_ge(half_sums, 2 * (l * GROUPS + g + LAP))
                            for j in range(GROUP):
                                s = GROUP * g + j
                                nc.vector.tensor_scalar(lo_hot[:, j, :], iota[0:HIST_ROWS, :], hist_lo[:, ds(s, 1)],
                                                        None, ALU.is_equal).then_inc(hist_hots, 1)
                                nc.vector.tensor_scalar(hi_hot[:, j, :], iota[0:HIST_ROWS, 0:TILES],
                                                        hist_hi[:, ds(s, 1)], None, ALU.is_equal
                                                        ).then_inc(hist_hots, 1)
                        dve.load(tiles_r, row[0:1, ds(GROUP * g, GROUP)])
                        for h in range(2):
                            dve.wait_ge(half_sums, 2 * (LAP + l * GROUPS + g) + h + 1)
                            for j in range(h * HALF, (h + 1) * HALF):
                                t = dve.snap(tiles_r[j], min_val=0, max_val=TILES - 1)
                                dve.wait_ge(added, GROUP + l * STEPS + GROUP * g + j)
                                a = acc[:, ds(t, 1), :]
                                nc.vector.tensor_tensor(a, a, ps_sum[:, j:j + 1, :], ALU.add).then_inc(added, 1)

            def to_small(v):
                dve.sem_inc(misc_dve, v - m[0])
                m[0] = v
                dve.wait_ge(misc_dve, v)

            dve.wait_ge(tile_in, 32)
            dve.wait_ge(psem("hist_clear"), 1)
            sums(0, S_key, S_w, True)
            dve.wait_ge(half_sums, 2 * (LAP + GROUPS))
            small(nc.vector.tensor_copy(deg_src[:, :], ps_h[:, 0:TILES]))
            to_small(100)
            split(hist_dst)
            dve.wait_ge(added, GROUP + STEPS)
            dve.wait_ge(A.p.sem, A.p.at("keep", TILES - 1))
            small(nc.vector.scalar_tensor_tensor(keep[:, :, :].rearrange("p a b -> p (a b)"),
                                                 acc[:, :, :].rearrange("p a b -> p (a b)"), hop[:, 3:4],
                                                 keep[:, :, :].rearrange("p a b -> p (a b)"), ALU.mult, ALU.add))
            small(nc.vector.tensor_scalar(S_w, S_w, hop[:, 4:5], None, ALU.mult))
            dve.wait_ge(table_out[0], 16)
            nc.vector.memset(acc[:, :, :].rearrange("p a b -> p (a b)"), 0.0).then_inc(acc_ready, 1)
            dve.wait_ge(acc_ready, 2)
            dve.wait_ge(psem("hist_clear"), 2)
            sums(1, S_key, S_w, True)
            dve.wait_ge(half_sums, 2 * (LAP + 2 * GROUPS))
            small(nc.vector.tensor_copy(dtmp[:, :], ps_h[:, 0:TILES]))
            small(nc.vector.tensor_scalar(inv_deg[:, :], dtmp[:, :], 1.0, None, ALU.max))
            small(nc.vector.reciprocal(inv_deg[:, :], inv_deg[:, :]))
            small(nc.vector.scalar_tensor_tensor(inv_deg[:, :], dtmp[:, :], 0.5, inv_deg[:, :], ALU.is_gt, ALU.mult))
            small(nc.vector.tensor_scalar(dinv[:, :], deg_src[:, :], 1.0, None, ALU.max))
            to_small(200)
            dve.wait_ge(misc_act, 2)
            small(nc.vector.reciprocal(dinv[:, :], dinv[:, :]))
            small(nc.vector.scalar_tensor_tensor(dinv[:, :], deg_src[:, :], 0.5, dinv[:, :], ALU.is_gt, ALU.mult))
            dve.wait_ge(added, GROUP + 2 * STEPS)

            def tile(a, t):
                return a[:, ds(t, 1), :]

            def body(t, i, b):
                if not (isinstance(t, int) and t < 2):
                    dve.wait_ge(C.store[b], 32 * i)
                nc.vector.tensor_tensor(wide(ny[b]), tile(acc, t), tile(keep, t), ALU.add).then_inc(C.v.sem, 1)
                dve.wait_ge(C.v.sem, C.v.at("sum", t))
                dve.wait_ge(C.load[b], 16 * i + 16)
                nc.vector.scalar_tensor_tensor(ny[b][:, :], ny[b][:, :], 0.0, nx[b][:, :], ALU.max, ALU.add
                                               ).then_inc(C.v.sem, 1)
                dve.wait_ge(C.v.sem, C.v.at("resid", t))
                if not (isinstance(t, int) and t < 2):
                    dve.wait_ge(C.t.sem, C.t.at("hT", t - 2))
                norm(C, t, b, ny, nh)
                dve.wait_ge(C.t.sem, C.t.at("prod", t))
                nc.vector.tensor_tensor(tile(keep, t), ps_M[:, b:b + 1, 0:D], bias[:, 0:1, :], ALU.add
                                        ).then_inc(C.v.sem, 1)
            over_tiles(dve, body)
            dve.wait_ge(C.p.sem, C.p.at("clear", TILES - 1))
            sums(2, D_key, None, False)

            for l, S in ((3, D1), (4, D2)):
                dve.wait_ge(added, GROUP + l * STEPS)
                def body(t, i, b):
                    if not (isinstance(t, int) and t < 2):
                        dve.wait_ge(S.s.sem, S.s.at("relu", t - 2))
                    nc.vector.scalar_tensor_tensor(wide(ny[b]), tile(acc, t), inv_deg[:, ds(t, 1)], tile(keep, t),
                                                   ALU.mult, ALU.add).then_inc(S.v.sem, 1)
                    dve.wait_ge(S.v.sem, S.v.at("sum", t))
                    dve.wait_ge(S.t.sem, S.t.at("prod", t))
                    nc.vector.tensor_tensor(tile(keep, t), ps_M[:, b:b + 1, 0:D], bias[:, l - 2:l - 1, :], ALU.add
                                            ).then_inc(S.v.sem, 1)
                over_tiles(dve, body)
                dve.wait_ge(S.p.sem, S.p.at("clear", TILES - 1))
                sums(l, D_key, None, False)

            dve.wait_ge(added, GROUP + 5 * STEPS)
            def body(t, i, b):
                if not (isinstance(t, int) and t < 2):
                    dve.wait_ge(Es.p.sem, Es.p.at("keep", t - 2))
                nc.vector.scalar_tensor_tensor(wide(ny[b]), tile(acc, t), inv_deg[:, ds(t, 1)], tile(keep, t),
                                               ALU.mult, ALU.add).then_inc(Es.v.sem, 1)
                dve.wait_ge(Es.v.sem, Es.v.at("sum", t))
                dve.wait_ge(Es.load[b], 16 * i + 16)
                nc.vector.tensor_tensor(ny[b][:, :], ny[b][:, :], nx[b][:, :], ALU.add).then_inc(Es.v.sem, 1)
                dve.wait_ge(Es.v.sem, Es.v.at("resid", t))
                if not (isinstance(t, int) and t < 2):
                    dve.wait_ge(Es.s.sem, Es.s.at("scaled", t - 2))
                norm(Es, t, b, ny, nh)
            over_tiles(dve, body)

            dve.wait_ge(Es.p.sem, Es.p.at("clear", TILES - 1))
            sums(5, S_key, None, False)

            dve.wait_ge(Es.p.sem, Es.p.at("keep", TILES - 1))
            def body(t, i, b):
                dve.wait_ge(Fs.t.sem, Fs.t.at("prod", t))
                nc.vector.tensor_tensor(nx[b][:, :], ps_M[:, b, 0:D], bias[:, 3, :], ALU.add).then_inc(Fs.v.sem, 1)
                dve.wait_ge(Fs.v.sem, Fs.v.at("biased", t))
                nc.vector.scalar_tensor_tensor(nx[b][:, :], nx[b][:, :], LEAK, nx[b][:, :], ALU.mult, ALU.max
                                               ).then_inc(Fs.v.sem, 1)
                dve.wait_ge(Fs.v.sem, Fs.v.at("leaky", t))
                if not (isinstance(t, int) and t < 2):
                    dve.wait_ge(Fs.p.sem, Fs.p.at("keep", t - 2))
                nc.vector.tensor_tensor(wide(ny[b]), wide(nx[b]), tile(keep, t), ALU.add).then_inc(Fs.v.sem, 1)
                dve.wait_ge(Fs.v.sem, Fs.v.at("resid", t))
                norm(Fs, t, b, ny, nh)
                dve.wait_ge(Fs.s.sem, Fs.s.at("gate", t))
                if not (isinstance(t, int) and t < 1):
                    dve.wait_ge(Fs.store[1 - b], 16 * (i + b))
                for r in [r for r in range(RELS) if r % 4 < 2]:
                    dve.wait_ge(Fs.t.sem, Fs.t.at(f"m{r // 2 * 2}", t))
                    nc.vector.tensor_scalar(msg[:, r, :], ps_sum[:, r % 8, :], gate[:, b, r:r + 1], None, ALU.mult
                                            ).then_inc(Fs.v.sem, 1)
            over_tiles(dve, body)
            nc.vector.memset(acc[:, :, :].rearrange("p a b -> p (a b)"), 0.0).then_inc(acc_ready, 1)
            dve.wait_ge(acc_ready, 3)
            dve.wait_ge(Fs.p.sem, Fs.p.at("keep", TILES - 1))
            sums(6, D_key, D_w, False)

            dve.wait_ge(added, GROUP + 7 * STEPS)
            def body(t, i, b):
                if not (isinstance(t, int) and t < 2):
                    dve.wait_ge(Gs.store[b], 16 * i)
                nc.vector.scalar_tensor_tensor(wide(nt[b]), tile(acc, t), 0.0, tile(keep, t), ALU.max, ALU.add
                                               ).then_inc(Gs.v.sem, 1)
            over_tiles(dve, body)

        @block.tensor
        def _(pe):
            def body(k, b, first):
                pe.wait_ge(sort_masks, k + 1)
                if not first:
                    pe.wait_ge(sort_blocks, k)
                for i in range(COL_BLOCKS):
                    ins = nc.tensor.matmul(ps_h[:, i:i + 1], masks[b][:, i * P:(i + 1) * P], ones_b[0:HIST_ROWS, :],
                                           start=True, stop=True)
                ins.then_inc(sort_counts, 1)
                if not (isinstance(k, int) and k < 2):
                    pe.wait_ge(sort_picks, 2 * (k - 1))
                to = ps_sum[0:HIST_ROWS, 4 * b:4 * b + 4, :].rearrange("p a b -> p (a b)")
                parts = [(0, 512), (512, HIST_COLS)]
                for lo, hi in parts:
                    nc.tensor.matmul(to[:, lo:hi], before[0:HIST_ROWS, 0:HIST_ROWS], masks[b][:, lo:hi], start=True,
                                     stop=False)
                pe.wait_ge(sort_blocks, k + 1)
                for i in reversed(range(COL_BLOCKS)):
                    block_counts = in_block[:, i:i + 1].to_broadcast([P, HIST_ROWS])
                    for lo, hi in parts:
                        a = max(lo, i * P)
                        if a < hi:
                            ins = nc.tensor.matmul(to[:, a:hi], block_counts, before[:, a - i * P:hi - i * P],
                                                   start=False, stop=(i == 0))
                ins.then_inc(sort_ranks, 1)
                if not first:
                    pe.wait_ge(sort_begins, k)
                for i in range(COL_BLOCKS):
                    ins = nc.tensor.matmul(ps_T[0:HIST_ROWS, 0, 0, 0:1], in_block[:, i:i + 1].to_broadcast([P, HIST_ROWS]),
                                           ones_b[:, :], start=(i == 0), stop=(i == COL_BLOCKS - 1))
                ins.then_inc(sort_totals, 1)
            pe.wait_ge(psem("sort_start"), 1)
            body(0, 0, True)
            body(1, 1, False)
            with pe.Fori(1, TILES // 2) as i:
                body(2 * i, 0, False)
                body(2 * i + 1, 1, False)
            body(TILES - 1, 0, False)

            def find_steps(k):
                pe.wait_ge(psem("cnt"), k + 1)
                if k == 0:
                    pe.wait_ge(sort_blocks, TILES)
                nc.tensor.matmul(ps_h[:, 0:TILES - 1], ones[:, :], cnt, start=True, stop=True).then_inc(prep_pe, 1)
                pe.wait_ge(psem("step_chunk"), k + 1)
                nc.tensor.transpose(ps_h[0:STEP_TILES, P:2 * P], step_tile, ident[:, :]).then_inc(prep_pe, 1)

            def turn_rows(k, fields):
                pe.wait_ge(psem("step_rows"), k + 1)
                for i in range(STEP_TILES):
                    if i + k >= 2:
                        pe.wait_ge(psem("turned"), STEP_TILES * k + i - 1)
                    for q, field in enumerate(fields):
                        ins = nc.tensor.transpose(ps_M[:, i % 2, q * P:(q + 1) * P], field(i), ident[:, :])
                    ins.then_inc(prep_pe, 1)
            find_steps(0)
            turn_rows(0, [lambda i, q=q: raw_f[:, q, i, :] for q in range(4)])
            find_steps(1)
            turn_rows(1, [lambda i: raw_s[:, i, :, 0], lambda i: raw_k[:, i, :], lambda i: raw_s[:, i, :, 2]])

            def turn(S, t, b, source, step="hT"):
                for k in range(2):
                    ins = nc.tensor.transpose(ps_T[:, b, k, :], source[b][:, k * P:(k + 1) * P], ident[:, :])
                ins.then_inc(S.t.sem, 1)

            def product(S, t, b, w, n):
                for k in range(2):
                    ins = nc.tensor.matmul(ps_M[:, b, 0:n], nhT[b][:, k, :], w[:, k, 0:n], start=(k == 0), stop=(k == 1))
                ins.then_inc(S.t.sem, 1)

            pe.wait_ge(consts, 1)
            pe.wait_ge(weights_in[0], 16)
            def body(t, i, b):
                pe.wait_ge(A.s.sem, A.s.at("relu", t))
                turn(A, t, b, nh)
                pe.wait_ge(A.s.sem, A.s.at("hT", t))
                if not (isinstance(t, int) and t < 2):
                    pe.wait_ge(A.v.sem, A.v.at("table", t - 2))
                product(A, t, b, W[0], D)
            over_tiles(pe, body)

            def clear_hist(v):
                nc.tensor.matmul(ps_h[:, 0:TILES], zeros[:, 0:P], zeros[:, 0:TILES], start=True, stop=False,
                                 skip_group_check=True).then_inc(psem("hist_clear"), 1)
                pe.wait_ge(psem("hist_clear"), v)

            pe.sem_inc(half_sums, 2 * LAP)

            def sums(l, hist):
                with pe.Fori(0, LAPS) as i:
                    for k in range(LAP):
                        g = LAP * i + k
                        if hist:
                            pe.wait_ge(hist_hots, 2 * (l * STEPS + GROUP * (g + 1)))
                            for j in range(GROUP):
                                nc.tensor.matmul(ps_h[:, 0:TILES], lo_hot[:, j, :], hi_hot[:, j, :], start=False,
                                                 stop=False, skip_group_check=True)
                        pe.wait_ge(gathered[k], 16 * GROUP * (l * LAPS + i + 1))
                        for h in range(2):
                            pe.wait_ge(hots, l * STEPS + GROUP * g + HALF * (h + 1))
                            pe.wait_ge(added, l * STEPS + GROUP * g + HALF * (h + 1))
                            for j in range(h * HALF, (h + 1) * HALF):
                                ins = nc.tensor.matmul(ps_sum[:, j, :], onehot[:, GROUP * (k % 2) + j, :],
                                                       ring[:, GROUP * k + j, :], start=True, stop=True)
                            ins.then_inc(half_sums, 1)
            pe.wait_ge(psem("turned"), 2 * STEP_TILES)
            clear_hist(1)
            sums(0, True)
            pe.wait_ge(misc_dve, 100)
            clear_hist(2)
            sums(1, True)

            def sage(S, w):
                def body(t, i, b):
                    pe.wait_ge(S.s.sem, S.s.at("relu", t))
                    turn(S, t, b, nh)
                    pe.wait_ge(S.s.sem, S.s.at("hT", t))
                    if not (isinstance(t, int) and t < 2):
                        pe.wait_ge(S.v.sem, S.v.at("self", t - 2))
                        pe.wait_ge(S.s.sem, S.s.at("table", t - 2))
                    for to, half in ((ps_M[:, b, 0:D], 0), (ps_sum[:, 2 * b, :], D)):
                        for k in range(2):
                            ins = nc.tensor.matmul(to, nhT[b][:, k, :], w[:, k, half:half + D], start=(k == 0),
                                                   stop=(k == 1))
                    ins.then_inc(S.t.sem, 1)
                over_tiles(pe, body)
            pe.wait_ge(weights_in[1], 32)
            sage(C, W[1])
            sums(2, False)
            pe.wait_ge(weights_in[2], 32)
            sage(D1, W[0])
            sums(3, False)
            pe.wait_ge(weights_in[3], 32)
            sage(D2, W[1])
            sums(4, False)

            sums(5, False)

            pe.wait_ge(weights_in[4], 48)
            pe.wait_ge(hist_in, 16 * 10)
            pe.wait_ge(added, GROUP + 6 * STEPS)
            def body(t, i, b):
                pe.wait_ge(Fs.s.sem, Fs.s.at("dinv", t))
                turn(Fs, t, b, nh)
                pe.wait_ge(Fs.s.sem, Fs.s.at("aT", t))
                product(Fs, t, b, W[0], D)
                pe.wait_ge(Fs.s.sem, Fs.s.at("relu", t))
                turn(Fs, t, b, nh)
                pe.wait_ge(Fs.s.sem, Fs.s.at("hT", t))
                for k in range(2):
                    ins = nc.tensor.matmul(ps_h[:, 0:RELS], nhT[b][:, k, :], gw[:, k, :], start=(k == 0), stop=(k == 1))
                ins.then_inc(Fs.t.sem, 1)
                for r in range(0, RELS, 2):
                    out_by = Fs.v if r % 4 == 0 else Fs.s
                    if r >= 8:
                        pe.wait_ge(out_by.sem, out_by.at(f"m{r - 7}", t))
                    elif not (isinstance(t, int) and t < 1):
                        pe.wait_ge(out_by.sem, out_by.at(f"m{r + 9}", t - 1))
                    for k in range(2):
                        ins = nc.tensor.matmul(ps_sum[:, r % 8:r % 8 + 2, :], nhT[b][:, k, :], W3[k][:, r:r + 2, :],
                                               start=(k == 0), stop=(k == 1))
                    ins.then_inc(Fs.t.sem, 1)
            over_tiles(pe, body)
            sums(6, False)


_INS = ['x', 'src', 'dst', 'edge_type_16', 'edge_weight', 'edge_weight1', 'L0_gnn_weight', 'L0_gnn_hop_logits',
        'L1_gnn_W_self', 'L1_gnn_W_neigh', 'L1_gnn_bias', 'L2_gnn_W', 'L2_gnn_b', 'L3_gnn_weight',
        'L3_gnn_gate_weight']


def kernel(**inputs):
    import numpy as _np
    import concourse.bacc as _bacc
    from concourse import mybir as _mybir
    from concourse.bass_utils import run_bass_kernel_spmd as _run

    nc = _bacc.Bacc("TRN2", target_bir_lowering=False, num_devices=1)
    arrays, args = {}, []
    for name in _INS:
        a = _np.ascontiguousarray(inputs[name])
        if name == 'edge_weight1':
            a = a.reshape(-1)
        arrays[f"in_{name}_dram"] = a
        args.append(nc.dram_tensor(f"in_{name}_dram", a.shape, _mybir.dt.from_np(a.dtype), kind="ExternalInput").ap())
    args.append(nc.dram_tensor("out_0_dram", (N, D), _mybir.dt.float32, kind="ExternalOutput").ap())
    gnn(nc, *args)
    r = _run(nc, [arrays], core_ids=[0])
    return r.results[0]["out_0_dram"]
```

```python
import concourse.bass as bass
from concourse import mybir
from contextlib import ExitStack

P = 128
N = 6250
E = 100000
D = 256
RELS = 16
TILES = -(-N // P)
NP = TILES * P
LAST_ROWS = N - (TILES - 1) * P
CHUNKS = -(-E // P)
STEP_TILES = -(-(CHUNKS + TILES) // P)
TAB = STEP_TILES * P
GROUP = 8
LAP = 4
LAPS = -(-(CHUNKS + TILES - 1) // (GROUP * LAP))
GROUPS = LAPS * LAP
STEPS = GROUPS * GROUP
HALF = GROUP // 2
OUT_TILES = 7
HIST_ROWS = 125
HIST_COLS = E // HIST_ROWS
NO_NODE = 1 << 20
SORT_SLOTS = 32
SORT_LAPS = HIST_COLS // SORT_SLOTS
COL_BLOCKS = -(-HIST_COLS // P)
FIELDS = 3
LN_EPS = 1e-5
LEAK = 0.2

F32 = mybir.dt.float32
I32 = mybir.dt.int32
BF16 = mybir.dt.bfloat16
ALU = mybir.AluOpType
ACT = mybir.ActivationFunctionType
AX = mybir.AxisListType
ds = bass.ds


MATS = 8 + RELS
PAIRS = [(2, 0), (0, 2), (1, 1), (1, 0), (0, 1), (0, 0)]
LEAD = 3


class Steps:

    def __init__(self, sem, steps, lead=LEAD):
        self.sem, self.names, self.ahead, self.lead = sem, [n for n, _ in steps], dict(steps), lead

    def at(self, name, t):
        return len(self.names) * (t - self.ahead[name] + self.lead) + self.names.index(name) + 1

    def iteration(self, eng, do, it, i, c):
        for n, name in enumerate(self.names):
            a = self.ahead[name]
            t = it + a
            if isinstance(t, int) and not 0 <= t < TILES:
                if self.sem is not None:
                    before = len(self.names) * (it + self.lead) + n
                    if before:
                        eng.wait_ge(self.sem, before)
                    eng.sem_inc(self.sem, 1)
            else:
                do[name](t, i + (c + a) // 2, (c + a) % 2)


def walk(eng, steps, do):
    def iteration(it, i, c):
        steps.iteration(eng, do, it, i, c)
    for it in range(-LEAD, 4):
        iteration(it, it // 2, it % 2)
    with eng.Fori(2, TILES // 2 - 2) as i:
        for c in range(2):
            iteration(2 * i + c, i, c)
    for it in range(TILES - 5, TILES + 2):
        iteration(it, it // 2, it % 2)


def walk_pairs(eng, pair, steps=None, do=None, pair_first=False):
    def iteration(it, i, c):
        if pair_first:
            pair(it, i, c)
        if steps:
            steps.iteration(eng, do, it, i, c)
        if not pair_first:
            pair(it, i, c)
    head, tail = (6, TILES - 1) if steps else (0, GROUPS // 2 - 2)
    for it in range(head):
        iteration(it, it // 2, it % 2)
    with eng.Fori(head // 2, tail // 2) as i:
        for c in range(2):
            iteration(2 * i + c, i, c)
    for it in range(tail, GROUPS // 2):
        iteration(it, it // 2, it % 2)
    if steps:
        it = GROUPS // 2
        steps.iteration(eng, do, it, it // 2, it % 2)


def over_tiles(eng, body):
    walk(eng, Steps(None, [("body", 0)]), dict(body=body))


def first(t):
    return isinstance(t, int) and t < 2


def gnn(nc, x, src, dst, edge_type, w0, w1, L0_w, L0_hop, L1_ws, L1_wn, L1_b, L2_w, L2_b, L3_w, L3_g, out):
    ctx = ExitStack()
    with ctx:
        def sb(name, shape, dt=F32):
            return ctx.enter_context(nc.sbuf_tensor(name, shape, dt))

        def pb(name, shape, dt=F32):
            return ctx.enter_context(nc.psum_tensor(name, shape, dt))

        def sem(name):
            return ctx.enter_context(nc.semaphore(name))

        def dram(name, shape, dt=F32):
            return nc.dram_tensor(name, shape, dt).ap()

        srcD, dstD, typD = (dram(n, [TAB, P], I32) for n in ("srcD", "dstD", "typD"))
        w1D = dram("w1D", [TAB, P])
        by_srcD = dram("by_srcD", [TAB * P, FIELDS])
        tileD = [dram(f"tileD{k}", [STEP_TILES, P], I32) for k in range(2)]
        tables = [dram(f"table{l}", [NP, D]) for l in range(6)]
        rel_table = dram("rel_table", [RELS * NP, D])
        x1D = dram("x1D", [NP, D])
        matD = dram("matD", [MATS, D, D])
        splitD = dram("splitD", [MATS, P, 3, 2 * D], BF16)

        acc = sb("acc", [P, TILES, D])
        keep = sb("keep", [P, TILES, D])
        ring = sb("ring", [P, LAP * GROUP, D])
        D_idx = sb("D_idx", [P, TAB], I32)
        D_rel = sb("D_rel", [P, TAB], I32)
        D_key = sb("D_key", [P, TAB])
        D_w = sb("D_w", [P, TAB])
        early = sb("early", [P, RELS * D])
        S_idx = early[:, 0:TAB].bitcast(I32)
        S_key = early[:, TAB:2 * TAB]
        S_w = early[:, 2 * TAB:3 * TAB]
        tile_row = [sb("tile_row", [1, TAB], I32), early[0:1, 3 * TAB:4 * TAB].bitcast(I32)]
        onehot = sb("onehot", [P, 2 * GROUP, P])
        stage = sb("stage", [P, LAP * GROUP], I32)
        W = [sb(f"W{b}", [P, 3, 2, 2, D], BF16) for b in range(2)]
        gw = sb("gw", [P, 2, RELS])
        gw3 = sb("gw3", [P, 3, 2, RELS], BF16)
        bias = sb("bias", [P, 4, D])
        ident = sb("ident", [P, P])
        iota = sb("iota", [P, P])
        ones_b = sb("ones_b", [P, 1], BF16)
        zeros = sb("zeros", [P, D])
        deg_src = sb("deg_src", [P, TILES])
        dinv = sb("dinv", [P, TILES])
        inv_deg = sb("inv_deg", [P, TILES])
        dtmp = sb("dtmp", [P, TILES])
        hop = sb("hop", [P, 8])
        eps = sb("eps", [P, 1])
        part = sb("part", [P, 1])
        nx = [sb(f"nx{b}", [P, D]) for b in range(2)]
        ny = [sb(f"ny{b}", [P, D]) for b in range(2)]
        nh = [sb(f"nh{b}", [P, D]) for b in range(2)]
        nhT = [sb(f"nhT{b}", [P, 3, 2, P], BF16) for b in range(2)]
        naT = sb("naT", [P, 3, 2, P], BF16)
        nr = [sb(f"nr{b}", [P, 2, P]) for b in range(2)]
        nt = [sb(f"nt{b}", [P, D]) for b in range(2)]
        st6 = sb("st6", [P, 2, 6])
        mv = sb("mv", [P, 2, 4])
        gate = sb("gate", [P, 2, RELS])
        keep_row = keep[:, :, :].rearrange("p a b -> p (a b)")
        acc_row = acc[:, :, :].rearrange("p a b -> p (a b)")
        ring_row = ring[:, :, :].rearrange("p a b -> p (a b)")

        class Room:

            def __init__(self, row):
                self.row, self.at = row, 0

            def take(self, n, dt=F32):
                a = self.row[:, self.at:self.at + n]
                self.at += n
                return a if dt == F32 else a.bitcast(dt)

        cells = STEP_TILES * P
        room = Room(keep_row)
        raw_i = room.take(3 * cells, I32).rearrange("p (k i e) -> p k i e", k=3, e=P)
        raw_f = room.take(4 * cells).rearrange("p (k i e) -> p k i e", k=4, e=P)
        gate_rest = room.take(2 * RELS).rearrange("p (k r) -> p k r", k=2)
        room = Room(acc_row)
        last_i, last_f = room.take(STEP_TILES, I32), room.take(STEP_TILES)
        thr, tnum = room.take(TILES - 1), room.take(TILES - 1)
        snum = room.take(STEP_TILES)
        step_tile, step_base = room.take(STEP_TILES), room.take(STEP_TILES)
        step_chunk = room.take(STEP_TILES, I32)
        cnt, first_step = room.take(TILES - 1), room.take(TILES - 1)
        cmp = room.take(STEP_TILES * (TILES - 1)).rearrange("p (i t) -> p i t", i=STEP_TILES)
        pad_i = room.take(3 * P, I32).rearrange("p (k e) -> p k e", e=P)
        pad_s = room.take(FIELDS * P).rearrange("p (e f) -> p e f", f=FIELDS)
        tile_i = room.take(P, I32)[0:STEP_TILES, :]
        columns = room.take(HIST_COLS)
        ones = room.take(P)
        before = room.take(HIST_COLS // 2, BF16)
        masks = [room.take(COL_BLOCKS * P // 2, BF16)[0:HIST_ROWS, :] for b in range(2)]
        picked = room.take(HIST_COLS)[0:HIST_ROWS, :]
        rank = room.take(HIST_COLS)[0:HIST_ROWS, :]
        rank_i = room.take(HIST_COLS, I32)[0:HIST_ROWS, :]
        begin = room.take(TILES + 1)[0:HIST_ROWS, :]
        in_block = room.take(8, BF16)
        hist_src = room.take(HIST_COLS, I32)[0:HIST_ROWS, :]
        hist_w = room.take(HIST_COLS)[0:HIST_ROWS, :]
        hist_lo, hist_hi = (room.take(HIST_COLS)[0:HIST_ROWS, :] for _ in range(2))
        hist_dst = room.take(HIST_COLS, I32)[0:HIST_ROWS, :]
        room = Room(ring_row)
        record = room.take(FIELDS * HIST_COLS)[0:HIST_ROWS, :].rearrange("p (c f) -> p c f", f=FIELDS)
        rec_stage = room.take(FIELDS * SORT_SLOTS)[0:HIST_ROWS, :].rearrange("p (c f) -> p c f", f=FIELDS)
        lo_hot = room.take(GROUP * P, BF16)[0:HIST_ROWS, :].rearrange("p (b j e) -> p b j e", b=2, e=P)
        hi_hot = room.take(GROUP * TILES, BF16)[0:HIST_ROWS, :].rearrange("p (b j e) -> p b j e", b=2, e=TILES)
        mat = [room.take(2 * D) for b in range(2)]
        mat_rest = room.take(2 * D)
        mat3 = room.take(3 * D, BF16).rearrange("p (s c) -> p s c", s=3)
        room = Room(ring_row)
        raw_s = room.take(FIELDS * cells).rearrange("p (i e f) -> p i e f", f=FIELDS, e=P)
        raw_k = room.take(cells).rearrange("p (i e) -> p i e", e=P)
        ring_b = ring_row.bitcast(BF16).rearrange("p (s r k d) -> p s r k d", s=2, r=RELS, k=2)
        W3 = [ring_b[:, 0], ring_b[:, 1],
              early[:, :].bitcast(BF16).rearrange("p (r k d) -> p r k d", r=RELS, k=2)]
        msg = onehot[:, :, :].rearrange("p a b -> p (a b)").rearrange("p (u r d) -> p u r d", u=4, r=2)

        ps_sum = pb("ps_sum", [P, GROUP, D])
        ps_T = pb("ps_T", [P, 2 * D])
        ps_M = pb("ps_M", [P, 2, 2 * D])
        ps_h = pb("ps_h", [P, 2 * D])
        TT = [a[:, 0:D].rearrange("p (k e) -> p k e", k=2) for a in (ps_T, ps_h)]

        prep = {}

        def psem(name):
            if name not in prep:
                prep[name] = sem("p_" + name)
            return prep[name]

        copied = sem("inputs_copied")
        padded = sem("pads_ready")
        loaded = sem("prep_loaded")
        gath = sem("step_rows_gathered")
        weights_in = [sem(f"weights_in{n}") for n in range(5)]
        conv_weights_in = sem("conv_weights_in")
        consts = sem("consts_ready")
        prep_dve = sem("prep_vector")
        prep_pe = sem("prep_tensor")
        tile_out = sem("tile_row_out")
        tile_in = sem("tile_row_in")
        sort_masks = sem("sort_masks_ready")
        sort_counts = sem("sort_counts_ready")
        sort_blocks = sem("sort_counts_out")
        sort_totals = sem("sort_totals_ready")
        sort_begins = sem("sort_begins_ready")
        sort_ranks = sem("sort_ranks_ready")
        sort_picks = sem("sort_picks")
        sort_staged = sem("sort_slots_staged")
        sorted_out = [sem(f"sorted_rows_out{h}") for h in range(2)]
        hist_in = sem("hist_in")
        hist_used = sem("hist_onehots_used")
        misc_act = sem("small_scalar")
        misc_dve = sem("small_vector")

        passed = sem("waits_passed")
        staged = sem("indices_staged")
        gathered = [sem(f"rows_gathered{k}") for k in range(LAP)]
        hots = sem("onehots_ready")
        hist_hots = sem("hist_onehots_ready")
        half_sums = sem("half_sums_ready")
        added = sem("steps_added")
        acc_ready = sem("acc_ready")
        x1_out = [sem(f"x1_out{b}") for b in range(2)]
        msgs_out = [sem(f"messages_out{j}") for j in range(4)]
        mat_copied, mat_in, mat_out = sem("mats_copied"), [sem(f"mat_in{b}") for b in range(2)], sem("mat_parts_out")
        mat_steps, mat_used = sem("mat_parts_ready"), sem("mat_used")
        table_out = [sem(f"table_out{b}") for b in range(2)]

        block = ctx.enter_context(nc.Block())
        SUMS = 7

        class NodeStage:

            def __init__(self, name, kind, vector, scalar, tensor, pool):
                self.name, self.kind = name, kind
                self.v = Steps(sem(name + "_vector"), vector) if vector else None
                self.s = Steps(sem(name + "_scalar"), scalar) if scalar else None
                self.t = Steps(sem(name + "_tensor"), tensor) if tensor else None
                self.p = Steps(sem(name + "_pool"), pool) if pool else None
                self.load = [sem(f"{name}_loaded{b}") for b in range(2)]
                self.store = [sem(f"{name}_stored{b}") for b in range(2)]

        def ln(*more):
            return ([("rstd", 2), ("norm", 2)], [(n, 3) for n in more] + [("stats", 3), ("moments", 3)])
        A = NodeStage("in", "A", ln()[0] + [("rest", 1)] + ln()[1] + [("low", 1), ("table", -1)],
                      [("hT", 1), ("relu", 2), ("keep", 2), ("mid", 1), ("std", 3)], [("prod", 0), ("hT", 2)], None)
        C = NodeStage("hop", "C",
                      [("rstd", 1), ("stats", 2), ("rest", 0), ("norm", 1), ("moments", 2), ("resid", 3), ("low", 0)],
                      [("hT", 0), ("table", -2), ("mid", 0), ("relu", 1), ("std", 2), ("keep", 1)],
                      [("prod", -1), ("hT", 1)], [("clear", 3)])
        D_V = [("rest", 0), ("sum", 3), ("low", 0)]
        D_S = [("hT", 0), ("table", -2), ("mid", 0), ("relu", 2), ("keep", 2)]
        D1 = NodeStage("sage1", "D", D_V, D_S, [("prod", -1), ("hT", 1)], [("clear", 3)])
        D2 = NodeStage("sage2", "D", D_V, D_S, [("prod", -1), ("hT", 1)], [("clear", 3)])
        Es = NodeStage("sage3", "E", 
                       [("rstd", 1), ("stats", 2), ("sum", 3), ("moments", 2), ("norm", 1), ("resid", 3)],
                       [("std", 2), ("scaled", 1)], None, [("clear", 3)])
        Fs = NodeStage("conv", "F",
                       [("arest", 1), ("alow", 1), ("m0", 0), ("biased", 1), ("leaky", 1), ("resid", 1), ("stats", 1),
                        ("moments", 1), ("m2", 0), ("rstd", 1), ("norm", 1), ("m4", 0), ("rest", 1), ("low", 1),
                        ("m6", 0)],
                       [("aT", 1), ("amid", 1), ("m1", 0), ("std", 1), ("relu", 1), ("agg", 2), ("m3", 0), ("hT", 1),
                        ("mid", 1), ("m5", 0), ("gate", 1), ("m7", 0)],
                       [("aT", 1), ("m0", 0), ("m1", 0), ("prod", 1), ("m2", 0), ("m3", 0), ("m4", 0), ("hT", 1),
                        ("m5", 0), ("m6", 0), ("gate", 1), ("m7", 0)], [("clear", 2)])
        out_ready, out_stored = sem("out_ready"), sem("out_stored")

        class OwnProducts:

            def __init__(self, name):
                self.v = Steps(sem(name + "_vector"), [("rest", -1), ("low", -2), ("self", -4)], 0)
                self.s = Steps(sem(name + "_scalar"), [("fetch", 0), ("hT", -2), ("mid", -3)], 0)
                self.t = Steps(sem(name + "_tensor"), [("hT", 0), ("prod", -3)], 0)
        own_products = {l: OwnProducts(f"own{l}") for l in (2, 3, 4)}

        def wide(a):
            return a[:, :].rearrange("p (o d) -> p o d", o=1)

        def rows_of(t):
            return LAST_ROWS if isinstance(t, int) and t == TILES - 1 else P

        def node_rows(a, t, n=P):
            return a[ds(t * P, n), :] if not isinstance(t, int) else a[t * P:t * P + n, :]

        TABLE_TILES = [(TILES + 1) // 2, TILES // 2]

        @block.sync
        def _(sp):
            for a, o in ((src, srcD), (dst, dstD), (edge_type, typD), (w1, w1D)):
                flat = o.rearrange("a b -> (a b)")[0:E].rearrange("(a b) -> a b", a=16)
                sp.dma_start(flat, a.rearrange("(a b) -> a b", a=16)).then_inc(copied, 16)
            sp.wait_ge(padded, 2)
            full, part_row = TAB - CHUNKS, E % P
            for o, rows in ((srcD, pad_i[:, 0, :]), (dstD, pad_i[:, 1, :]), (typD, pad_i[:, 2, :]),
                            (w1D, zeros[:, 0:P]),
                            (by_srcD.rearrange("(a b) f -> a (b f)", b=P), pad_s.rearrange("p e f -> p (e f)"))):
                w = rows.shape[1] // P
                sp.dma_start(o[CHUNKS:TAB, :], rows[0:full, :]).then_inc(copied, 16)
                sp.dma_start(o[CHUNKS - 1:CHUNKS, part_row * w:P * w], rows[0:1, part_row * w:P * w]).then_inc(copied, 16)
            sp.wait_ge(copied, 16 * 14)
            sp.wait_ge(mat_copied, 16 * 5)

            def mat_load(m, b, i):
                if not isinstance(m, int):
                    sp.wait_ge(mat_steps, 4 * m - 4)
                sp.dma_start(mat[b].rearrange("p (k d) -> p k d", k=2),
                             (matD[m:m + 1] if isinstance(m, int) else matD[ds(m, 1)]).rearrange(
                                 "o (k p) d -> p (o k) d", p=P)).then_inc(mat_in[b], 16)

            def mat_store(m):
                sp.wait_ge(mat_steps, 4 * m + 4)
                sp.dma_start((splitD[m:m + 1] if isinstance(m, int) else splitD[ds(m, 1)]).rearrange(
                    "o p s c -> (o p) s c"), mat3).then_inc(mat_out, 16)

            def split_weights():
                mat_load(0, 0, 0)
                mat_load(1, 1, 0)
                with sp.Fori(1, MATS // 2) as i:
                    for b in range(2):
                        mat_store(2 * i + b - 2)
                        mat_load(2 * i + b, b, i)
                mat_store(MATS - 2)
                mat_store(MATS - 1)

            def walk_sp(order, do):
                walk(sp, Steps(None, order), do)

            def stage_in():
                def load_x(t, i, b):
                    n = rows_of(t)
                    if not first(t):
                        sp.wait_ge(A.v.sem, A.v.at("norm", t - 2))
                    sp.dma_start(nx[b][0:n, :], node_rows(x, t, n)).then_inc(A.load[b], 16)

                def put_table(t, i, b):
                    sp.wait_ge(A.v.sem, A.v.at("table", t))
                    sp.dma_start(node_rows(tables[0], t), nt[b][:, :]).then_inc(A.store[b], 16)
                sp.wait_ge(consts, 1)
                walk_sp([("load", 3), ("store", -1)], dict(load=load_x, store=put_table))

            for k in range(2):
                if k == 0:
                    sp.dma_start(last_i, dstD.rearrange("(i p) e -> p i e", p=P)[:, :, P - 1],
                                 allow_slow_non_contiguous=True).then_inc(loaded, 16)
                else:
                    for h in range(2):
                        sp.wait_ge(sorted_out[h], 16 * (SORT_SLOTS // 2) * SORT_LAPS)
                    sp.wait_ge(psem("step_chunk"), 1)
                    sp.dma_start(last_f, by_srcD.rearrange("(i p e) f -> p i (e f)", p=P, e=P)[:, :, FIELDS * P - 2],
                                 allow_slow_non_contiguous=True).then_inc(loaded, 16)
                sp.wait_ge(psem("tile_i"), k + 1)
                sp.dma_start(tileD[k], tile_i).then_inc(tile_out, 16)
                sp.wait_ge(tile_out, 16 * (k + 1))
                sp.dma_start(tile_row[k][0:1, :], tileD[k].rearrange("(o a) b -> o (a b)", o=1)).then_inc(tile_in, 16)
                if k == 0:
                    split_weights()
                    stage_in()

            sp.wait_ge(added, GROUP + STEPS)
            sp.dma_start(tables[1].rearrange("(t p) d -> p t d", p=P), acc[:, :, :]).then_inc(table_out[0], 16)

            sp.wait_ge(added, GROUP + 2 * STEPS)

            def load_x(t, i, b):
                n = rows_of(t)
                if not first(t):
                    sp.wait_ge(C.v.sem, C.v.at("resid", t - 2))
                sp.dma_start(nx[b][0:n, :], node_rows(x, t, n)).then_inc(C.load[b], 16)

            def put_x(t, i, b):
                sp.wait_ge(C.v.sem, C.v.at("resid", t))
                sp.dma_start(node_rows(x1D, t), ny[b][:, :]).then_inc(x1_out[b], 16)

            def put_table(t, i, b):
                sp.wait_ge(C.s.sem, C.s.at("table", t))
                sp.dma_start(node_rows(tables[2], t), nt[b][:, :]).then_inc(C.store[b], 16)
            walk_sp([("load", 3), ("x", 2), ("store", -2)], dict(load=load_x, x=put_x, store=put_table))

            for S, tab in ((D1, tables[3]), (D2, tables[4])):
                def body(t, i, b):
                    sp.wait_ge(S.s.sem, S.s.at("table", t))
                    sp.dma_start(node_rows(tab, t), nt[b][:, :]).then_inc(S.store[b], 16)
                over_tiles(sp, body)

            for b in range(2):
                sp.wait_ge(x1_out[b], 16 * TABLE_TILES[b])
            sp.wait_ge(D2.v.sem, D2.v.at("low", TILES - 1))

            def load_x(t, i, b):
                if not first(t):
                    sp.wait_ge(Es.v.sem, Es.v.at("resid", t - 2))
                sp.dma_start(nx[b][:, :], node_rows(x1D, t)).then_inc(Es.load[b], 16)

            def put_table(t, i, b):
                sp.wait_ge(Es.s.sem, Es.s.at("scaled", t))
                sp.dma_start(node_rows(tables[5], t), nt[b][:, :]).then_inc(Es.store[b], 16)
            walk_sp([("load", 3), ("store", 0)], dict(load=load_x, store=put_table))

            dest = rel_table.rearrange("(r n) d -> n r d", r=RELS)

            def body(t, i, b):
                for u in range(RELS // 2):
                    out_by = Fs.s if u % 2 else Fs.v
                    sp.wait_ge(out_by.sem, out_by.at(f"m{u}", t))
                    to = dest[t * P:(t + 1) * P] if isinstance(t, int) else dest[ds(t * P, P)]
                    sp.dma_start(to[:, 2 * u:2 * u + 2, :], msg[:, u % 4]).then_inc(msgs_out[u % 4], 16)
            over_tiles(sp, body)

            for n, t in enumerate(range(0, TILES, OUT_TILES)):
                sp.wait_ge(out_ready, n + 1)
                whole = min(OUT_TILES, N // P - t)
                sp.dma_start(out[t * P:(t + whole) * P, :].rearrange("(t p) d -> p t d", p=P),
                             keep[:, t:t + whole, :]).then_inc(out_stored, 16)
            sp.dma_start(out[(TILES - 1) * P:N, :], keep[0:LAST_ROWS, TILES - 1, :]).then_inc(out_stored, 16)
            sp.wait_ge(out_stored, 16 * (TILES // OUT_TILES + 1))

        @block.scalar
        def _(act):
            def load_weights(n, *mats):
                for slot, m in enumerate(mats):
                    act.dma_start(W[n % 2][:, :, slot].rearrange("p s k d -> p s (k d)"), splitD[m]
                                  ).then_inc(conv_weights_in if n == 4 else weights_in[n], 16)
            for l in range(3):
                act.dma_start(bias[:, l, :], L1_b[l:l + 1, :].to_broadcast([P, D])).then_inc(hist_in, 16)
            act.dma_start(bias[:, 3, :], L2_b.rearrange("(o d) -> o d", o=1).to_broadcast([P, D])).then_inc(hist_in, 16)
            act.dma_start(hop[:, 0:2], L0_hop.rearrange("(o d) -> o d", o=1).to_broadcast([P, 2])).then_inc(hist_in, 16)
            act.dma_start(hist_src, src.rearrange("(p c) -> p c", p=HIST_ROWS)).then_inc(hist_in, 16)
            act.dma_start(hist_dst, dst.rearrange("(p c) -> p c", p=HIST_ROWS)).then_inc(hist_in, 16)
            act.dma_start(hist_w, w0.rearrange("(p c) -> p c", p=HIST_ROWS)).then_inc(hist_in, 16)
            for k in range(2):
                act.dma_start(gw[:, k, :], L3_g[:, k * P:(k + 1) * P, 0].rearrange("r p -> p r"),
                              allow_slow_non_contiguous=True).then_inc(hist_in, 16)
            act.dma_start(matD[0], L0_w).then_inc(mat_copied, 16)
            act.dma_start(matD[1:7:2], L1_ws).then_inc(mat_copied, 16)
            act.dma_start(matD[2:8:2], L1_wn).then_inc(mat_copied, 16)
            act.dma_start(matD[7], L2_w).then_inc(mat_copied, 16)
            act.dma_start(matD[8:MATS], L3_w).then_inc(mat_copied, 16)
            act.wait_ge(psem("sort_start"), 1)
            def body(k):
                act.wait_ge(sort_counts, k + 1)
                if not isinstance(k, int):
                    act.wait_ge(sort_ranks, k)
                nc.scalar.copy(in_block[:, 0:COL_BLOCKS], ps_h[:, 0:COL_BLOCKS]).then_inc(sort_blocks, 1)
                act.wait_ge(sort_totals, k + 1)
                if not isinstance(k, int):
                    act.wait_ge(sort_begins, k)
                nc.scalar.activation(begin[:, ds(k + 1, 1)], ps_T[0:HIST_ROWS, 0:1], ACT.Identity,
                                     bias=begin[:, ds(k, 1)]).then_inc(sort_begins, 1)
            body(0)
            with act.Fori(1, TILES) as k:
                body(k)
            act.wait_ge(psem("deg"), 1)
            nc.scalar.activation(dinv[:, :], dinv[:, :], ACT.Sqrt).then_inc(misc_act, 1)
            act.wait_ge(psem("hop_logits"), 1)
            nc.scalar.activation(hop[:, 3:5], hop[:, 3:5], ACT.Exp).then_inc(misc_act, 1)

            def std(S):
                def do(t, i, b):
                    act.wait_ge(S.v.sem, S.v.at("moments", t))
                    nc.scalar.activation(mv[:, b, 2:3], mv[:, b, 1:2], ACT.Sqrt, bias=eps[:, :]).then_inc(S.s.sem, 1)
                return do

            def high(S):
                def do(t, i, b):
                    act.wait_ge(S.t.sem, S.t.at("hT", t))
                    if not first(t):
                        act.wait_ge(S.t.sem, S.t.at("prod", t - 2))
                    nc.scalar.copy(nhT[b][:, 0], TT[b]).then_inc(S.s.sem, 1)
                return do

            def mid(S):
                def do(t, i, b):
                    act.wait_ge(S.v.sem, S.v.at("rest", t))
                    nc.scalar.copy(nhT[b][:, 1], nr[b][:, :, :]).then_inc(S.s.sem, 1)
                return do

            def relu(S, after, source):
                def do(t, i, b):
                    act.wait_ge(S.v.sem, S.v.at(after, t))
                    if not first(t):
                        act.wait_ge(S.t.sem, S.t.at("hT", t - 2))
                    nc.scalar.activation(nh[b][:, :], source[b][:, :], ACT.Relu).then_inc(S.s.sem, 1)
                return do

            def table(S):
                def do(t, i, b):
                    act.wait_ge(S.t.sem, S.t.at("prod", t))
                    if not first(t):
                        act.wait_ge(S.store[b], 16 * i)
                    nc.scalar.copy(nt[b][:, :], ps_M[:, b, 0:D]).then_inc(S.s.sem, 1)
                return do

            def keep_h(S, after, source):
                def do(t, i, b):
                    act.wait_ge(after.sem, after.at("relu" if after is S.s else "norm" if S is A else "sum", t))
                    nc.scalar.activation(keep[:, ds(t, 1), :], wide(source[b]), ACT.Relu).then_inc(S.s.sem, 1)
                return do

            def stage_indices(table, l):
                def pair(it, i, c):
                    for k in range(2 * c, 2 * c + 2):
                        act.wait_ge(half_sums, 2 * (l * GROUPS + LAP * i + k + 1))
                        nc.scalar.copy(stage[:, GROUP * k:GROUP * (k + 1)],
                                       table[:, ds(GROUP * LAP * i + GROUP * k, GROUP)]).then_inc(staged, 1)
                if l not in own_products:
                    walk_pairs(act, pair)
                    return
                Q = own_products[l]

                def fetch(t, i, b):
                    if not first(t):
                        act.wait_ge(Q.t.sem, Q.t.at("hT", t - 2))
                    nc.scalar.copy(wide(nh[b]), keep[:, ds(t, 1), :]).then_inc(Q.s.sem, 1)
                walk_pairs(act, pair, Q.s, dict(fetch=fetch, hT=high(Q), mid=mid(Q)), pair_first=True)

            act.wait_ge(consts, 1)
            act.wait_ge(mat_out, 16 * MATS)
            load_weights(0, 0)
            load_weights(1, 1, 2)
            walk(act, A.s, dict(hT=high(A), relu=relu(A, "norm", ny), keep=keep_h(A, A.v, ny), mid=mid(A), std=std(A)))
            act.wait_ge(psem("tables"), 1)
            stage_indices(S_idx, 0)
            stage_indices(S_idx, 1)

            walk(act, C.s, dict(hT=high(C), relu=relu(C, "norm", nh), keep=keep_h(C, C.s, nh), mid=mid(C), table=table(C), std=std(C)))
            load_weights(2, 3, 4)
            act.wait_ge(C.s.sem, C.s.at("keep", TILES - 1))
            stage_indices(D_idx, 2)
            for l, S in ((3, D1), (4, D2)):
                if l == 3:
                    act.wait_ge(own_products[2].t.sem, own_products[2].t.at("prod", TILES - 1))
                    load_weights(3, 5, 6)
                else:
                    act.wait_ge(own_products[3].t.sem, own_products[3].t.at("prod", TILES - 1))
                    load_weights(4, 7)
                walk(act, S.s, dict(hT=high(S), relu=relu(S, "sum", ny), keep=keep_h(S, S.v, ny), mid=mid(S),
                                     table=table(S)))
                act.wait_ge(S.s.sem, S.s.at("keep", TILES - 1))
                stage_indices(D_idx, l)

            def scaled(t, i, b):
                act.wait_ge(Es.v.sem, Es.v.at("norm", t))
                if not first(t):
                    act.wait_ge(Es.store[b], 16 * i)
                nc.scalar.activation(nt[b][:, :], nh[b][:, :], ACT.Relu, scale=dinv[:, ds(t, 1)]).then_inc(Es.s.sem, 1)
            walk(act, Es.s, dict(scaled=scaled, std=std(Es)))
            stage_indices(S_idx, 5)

            act.wait_ge(half_sums, 2 * (LAP + 6 * GROUPS))
            act.wait_ge(added, GROUP + 6 * STEPS)
            for part_n in range(3):
                act.dma_start(W3[part_n].rearrange("p r k d -> p r (k d)"),
                              splitD[8:MATS, :, part_n, :].rearrange("r p c -> p r c")).then_inc(weights_in[4], 16)

            def agg(t, i, b):
                if not first(t):
                    act.wait_ge(Fs.t.sem, Fs.t.at("hT", t - 2))
                nc.scalar.activation(wide(nh[b]), acc[:, ds(t, 1), :], ACT.Copy, scale=dinv[:, ds(t, 1)]
                                     ).then_inc(Fs.s.sem, 1)

            def agg_high(t, i, b):
                act.wait_ge(Fs.t.sem, Fs.t.at("aT", t))
                nc.scalar.copy(naT[:, 0], TT[0]).then_inc(Fs.s.sem, 1)

            def agg_mid(t, i, b):
                act.wait_ge(Fs.v.sem, Fs.v.at("arest", t))
                nc.scalar.copy(naT[:, 1], nr[0][:, :, :]).then_inc(Fs.s.sem, 1)

            def relu_h(t, i, b):
                act.wait_ge(Fs.v.sem, Fs.v.at("norm", t))
                nc.scalar.activation(nh[b][:, :], nh[b][:, :], ACT.Relu).then_inc(Fs.s.sem, 1)

            def h_high(t, i, b):
                act.wait_ge(Fs.t.sem, Fs.t.at("hT", t))
                nc.scalar.copy(nhT[b][:, 0], TT[1]).then_inc(Fs.s.sem, 1)

            def h_mid(t, i, b):
                act.wait_ge(Fs.v.sem, Fs.v.at("rest", t))
                nc.scalar.copy(nhT[b][:, 1], nr[1][:, :, :]).then_inc(Fs.s.sem, 1)

            def gates(t, i, b):
                act.wait_ge(Fs.t.sem, Fs.t.at("gate", t))
                nc.scalar.activation(gate[:, b, :], ps_M[:, 1, 0:RELS], ACT.Sigmoid).then_inc(Fs.s.sem, 1)

            def messages(u):
                def do(t, i, b):
                    act.wait_ge(Fs.s.sem, Fs.s.at("gate", t))
                    act.wait_ge(Fs.t.sem, Fs.t.at(f"m{u}", t))
                    if not (isinstance(t, int) and 2 * t + u // 4 < 1):
                        act.wait_ge(msgs_out[u % 4], 16 * (2 * t + u // 4))
                    nc.scalar.activation(msg[:, u % 4, 0, :], ps_sum[:, 2 * (u % 4), :], ACT.Copy,
                                         scale=gate[:, b, 2 * u:2 * u + 1])
                    nc.scalar.activation(msg[:, u % 4, 1, :], ps_sum[:, 2 * (u % 4) + 1, :], ACT.Copy,
                                         scale=gate[:, b, 2 * u + 1:2 * u + 2]).then_inc(Fs.s.sem, 1)
                return do
            walk(act, Fs.s, dict(agg=agg, aT=agg_high, amid=agg_mid, std=std(Fs), relu=relu_h, hT=h_high, mid=h_mid,
                                 gate=gates, m1=messages(1), m3=messages(3), m5=messages(5), m7=messages(7)))
            stage_indices(D_rel, 6)

        @block.gpsimd
        def _(pool):
            nc.gpsimd.memset(zeros[:, :], 0.0).then_inc(padded, 1)
            nc.gpsimd.iota(iota[:, :], pattern=[[1, P]], base=0, channel_multiplier=0,
                           allow_small_or_imprecise_dtypes=True).then_inc(psem("iota"), 1)
            nc.gpsimd.iota(thr, pattern=[[P, TILES - 1]], base=P, channel_multiplier=0,
                           allow_small_or_imprecise_dtypes=True).then_inc(psem("iota"), 1)
            nc.gpsimd.iota(tnum, pattern=[[1, TILES - 1]], base=1, channel_multiplier=0,
                           allow_small_or_imprecise_dtypes=True).then_inc(psem("iota"), 1)
            nc.gpsimd.iota(snum, pattern=[[P, STEP_TILES]], base=0, channel_multiplier=1,
                           allow_small_or_imprecise_dtypes=True).then_inc(psem("iota"), 1)
            nc.gpsimd.iota(part[:, :], pattern=[[0, 1]], base=0, channel_multiplier=1,
                           allow_small_or_imprecise_dtypes=True).then_inc(psem("iota"), 1)
            nc.gpsimd.iota(columns, pattern=[[1, HIST_COLS]], base=0, channel_multiplier=0,
                           allow_small_or_imprecise_dtypes=True).then_inc(psem("iota"), 1)
            nc.gpsimd.memset(ones[:, :], 1.0).then_inc(psem("ones"), 1)
            pool.wait_ge(psem("ones"), 1)
            nc.gpsimd.affine_select(out=ident[:, :], in_=ones[:, :], compare_op=ALU.is_equal, fill=0.0, base=0,
                                    pattern=[[-1, P]], channel_multiplier=1).then_inc(psem("iota"), 1)
            pool.wait_ge(copied, 16 * 14)
            pool.wait_ge(psem("step_chunk"), 1)
            for i in range(STEP_TILES):
                for to, table in ((raw_i[:, 0, i, :], srcD), (raw_i[:, 1, i, :], dstD), (raw_i[:, 2, i, :], typD),
                                  (raw_f[:, 3, i, :], w1D)):
                    nc.gpsimd.indirect_dma_start(
                        out=to, out_offset=None, in_=table,
                        in_offset=bass.IndirectOffsetOnAxis(ap=step_chunk[:, i:i + 1], axis=0)).then_inc(gath, 16)
            def body(i):
                for h in range(2):
                    if not isinstance(i, int):
                        pool.wait_ge(sorted_out[h], 16 * (SORT_SLOTS // 2) * i)
                    n, at = SORT_SLOTS // 2, SORT_SLOTS * i + SORT_SLOTS // 2 * h
                    nc.gpsimd.tensor_copy(stage[0:HIST_ROWS, n * h:n * (h + 1)], rank_i[:, ds(at, n)]
                                          ).then_inc(sort_staged, 1)
                    nc.gpsimd.tensor_copy(rec_stage[:, n * h:n * (h + 1), :], record[:, ds(at, n), :]
                                          ).then_inc(sort_staged, 1)
                    pool.wait_ge(sort_staged, 4 * i + 2 * h + 2)
                    pool.sem_inc(passed, 1)
                    for j in range(h * SORT_SLOTS // 2, (h + 1) * SORT_SLOTS // 2):
                        nc.gpsimd.indirect_dma_start(
                            out=by_srcD, out_offset=bass.IndirectOffsetOnAxis(ap=stage[0:HIST_ROWS, j:j + 1], axis=0),
                            in_=rec_stage[:, j, :], in_offset=None).then_inc(sorted_out[h], 16)
            pool.wait_ge(psem("records"), 1)
            body(0)
            with pool.Fori(1, SORT_LAPS) as i:
                body(i)
            for h in range(2):
                pool.wait_ge(sorted_out[h], 16 * (SORT_SLOTS // 2) * SORT_LAPS)
            pool.wait_ge(psem("step_chunk"), 2)
            for i in range(STEP_TILES):
                nc.gpsimd.indirect_dma_start(
                    out=raw_s[:, i, :, :].rearrange("p e f -> p (e f)"), out_offset=None,
                    in_=by_srcD.rearrange("(a b) f -> a (b f)", b=P),
                    in_offset=bass.IndirectOffsetOnAxis(ap=step_chunk[:, i:i + 1], axis=0)).then_inc(gath, 16)

            def gathers(table, l, ready):
                for s, v in ready:
                    pool.wait_ge(s, v)
                with pool.Fori(0, LAPS) as i:
                    for k in range(LAP):
                        pool.wait_ge(staged, l * GROUPS + LAP * i + k + 1)
                        pool.sem_inc(passed, 1)
                        for j in range(GROUP):
                            slot = GROUP * k + j
                            nc.gpsimd.indirect_dma_start(
                                out=ring[:, slot, :], out_offset=None, in_=table,
                                in_offset=bass.IndirectOffsetOnAxis(ap=stage[:, slot:slot + 1], axis=0)
                            ).then_inc(gathered[k], 16)

            def stored(S, n=1):
                return [(S.store[b], 16 * n * TABLE_TILES[b]) for b in range(2)]

            def clear(S, by, step):
                def do(t, i, b):
                    pool.wait_ge(by.sem, by.at(step, t))
                    nc.gpsimd.tensor_copy(acc[:, ds(t, 1), :], wide(zeros)).then_inc(S.p.sem, 1)
                walk(pool, S.p, dict(clear=do))

            gathers(tables[0], 0, stored(A))
            gathers(tables[1], 1, [(table_out[0], 16)])
            clear(C, C.v, "resid")
            gathers(tables[2], 2, stored(C))
            clear(D1, D1.v, "sum")
            gathers(tables[3], 3, stored(D1))
            clear(D2, D2.v, "sum")
            gathers(tables[4], 4, stored(D2))
            clear(Es, Es.v, "sum")
            gathers(tables[5], 5, stored(Es))
            clear(Fs, Fs.s, "agg")
            gathers(rel_table, 6, [(q, 16 * 2 * TILES) for q in msgs_out])

        @block.vector
        def _(dve):
            n = [0]

            def step(ins):
                n[0] += 1
                ins.then_inc(prep_dve, 1)
                dve.wait_ge(prep_dve, n[0])

            step(nc.vector.memset(pad_i[:, 0, :], N))
            step(nc.vector.memset(pad_i[:, 1, :], NO_NODE))
            step(nc.vector.memset(pad_i[:, 2, :], 0))
            step(nc.vector.memset(pad_s[:, :, 0], float(N)))
            step(nc.vector.memset(pad_s[:, :, 1], float(NO_NODE)))
            step(nc.vector.memset(pad_s[:, :, 2], 0.0))
            dve.sem_inc(padded, 1)
            step(nc.vector.memset(eps[:, :], LN_EPS))
            step(nc.vector.memset(ones_b[:, :], 1.0))
            step(nc.vector.memset(nx[0][:, :], 0.0))
            step(nc.vector.memset(rank, 0.0))
            step(nc.vector.memset(begin, 0.0))
            for b in range(2):
                step(nc.vector.memset(masks[b], 0.0))
            dve.wait_ge(psem("iota"), 7)
            step(nc.vector.tensor_scalar(before, columns, part[:, 0:1], None, ALU.is_gt))
            m = [0]

            def small(ins):
                m[0] += 1
                ins.then_inc(misc_dve, 1)
                dve.wait_ge(misc_dve, m[0])

            def split(nodes):
                for half, op, by in ((hist_hi, ALU.logical_shift_right, 7), (hist_lo, ALU.bitwise_and, P - 1)):
                    small(nc.vector.tensor_scalar(half.bitcast(I32), nodes, by, None, op))
                    small(nc.vector.tensor_copy(half, half.bitcast(I32)))
            dve.wait_ge(hist_in, 16 * 10)
            split(hist_src)

            def find_steps(k):
                dve.wait_ge(loaded, 16 * (k + 1))
                if k == 0:
                    step(nc.vector.tensor_copy(last_f, last_i))
                step(nc.vector.memset(cnt, 0.0))
                for i in range(STEP_TILES):
                    step(nc.vector.scalar_tensor_tensor(cnt, thr, last_f[:, i:i + 1], cnt, ALU.is_gt, ALU.add))
                dve.sem_inc(psem("cnt"), 1)
                dve.wait_ge(prep_pe, (STEP_TILES + 2) * k + 1)
                step(nc.vector.tensor_tensor(first_step, ps_h[:, 0:TILES - 1], tnum, ALU.add))
                for i in range(STEP_TILES):
                    step(nc.vector.tensor_scalar(cmp[:, i, :], first_step, snum[:, i:i + 1], None, ALU.is_le))
                step(nc.vector.tensor_reduce(step_tile, cmp, AX.X, ALU.add))
                step(nc.vector.tensor_tensor(step_chunk, snum, step_tile, ALU.subtract))
                step(nc.vector.tensor_scalar(step_base, step_tile, float(P), None, ALU.mult))
                dve.sem_inc(psem("step_chunk"), 1)
                dve.wait_ge(prep_pe, (STEP_TILES + 2) * k + 2)
                if k:
                    dve.wait_ge(tile_out, 16)
                nc.vector.tensor_copy(tile_i, ps_h[0:STEP_TILES, 128:128 + P]).then_inc(psem("tile_i"), 1)

            def turned(k, tables):
                for i in range(STEP_TILES):
                    dve.wait_ge(prep_pe, (STEP_TILES + 2) * k + 3 + i)
                    for q, table in enumerate(tables):
                        ins = nc.vector.tensor_copy(table[:, i * P:(i + 1) * P], ps_M[:, i % 2, q * P:(q + 1) * P])
                    ins.then_inc(psem("turned"), 1)
            find_steps(0)

            dve.sem_inc(psem("sort_start"), 1)
            def mask(k, b):
                nc.vector.tensor_scalar(masks[b][:, 0:HIST_COLS], hist_hi, iota[0:HIST_ROWS, ds(k, 1)],
                                        None, ALU.is_equal).then_inc(sort_masks, 1)

            def pick(k, b):
                dve.wait_ge(sort_ranks, k + 1)
                dve.wait_ge(sort_masks, k + 1)
                if not (isinstance(k, int) and k < 1):
                    dve.wait_ge(sort_begins, k)
                    dve.wait_ge(sort_picks, 2 * k)
                ranks = ps_sum[0:HIST_ROWS, 4 * b:4 * b + 4, :].rearrange("p a b -> p (a b)")[:, 0:HIST_COLS]
                nc.vector.scalar_tensor_tensor(picked, ranks, begin[:, ds(k, 1)], masks[b][:, 0:HIST_COLS], ALU.add,
                                               ALU.mult).then_inc(sort_picks, 1)
                dve.wait_ge(sort_picks, 2 * k + 1)
                nc.vector.tensor_tensor(rank, rank, picked, ALU.add).then_inc(sort_picks, 1)
            mask(0, 0)
            mask(1, 1)

            def body(k, b):
                pick(k, b)
                dve.wait_ge(sort_picks, 2 * k + 2)
                mask(k + 2, b)
            body(0, 0)
            body(1, 1)
            with dve.Fori(1, (TILES - 1) // 2) as i:
                body(2 * i, 0)
                body(2 * i + 1, 1)
            pick(TILES - 1, 0)
            dve.wait_ge(sort_picks, 2 * TILES)
            small(nc.vector.tensor_copy(rank_i, rank))
            small(nc.vector.tensor_copy(record[:, :, 0], hist_dst))
            small(nc.vector.tensor_copy(record[:, :, 1], hist_src))
            small(nc.vector.tensor_copy(record[:, :, 2], hist_w))
            dve.sem_inc(psem("records"), 1)

            def hots_of_columns(v):
                def body(i):
                    for b in range(2):
                        g = 2 * i + b
                        if not isinstance(i, int):
                            dve.wait_ge(hist_used, v * (HIST_COLS // GROUP) + g - 1)
                        for hot, digits, n in ((lo_hot, hist_lo, P), (hi_hot, hist_hi, TILES)):
                            nc.vector.tensor_tensor(
                                hot[:, b], iota[0:HIST_ROWS, 0:n].rearrange("p (o e) -> p o e", o=1).to_broadcast(
                                    [HIST_ROWS, GROUP, n]),
                                digits[:, ds(GROUP * g, GROUP)].rearrange("p (j o) -> p j o", o=1).to_broadcast(
                                    [HIST_ROWS, GROUP, n]), ALU.is_equal).then_inc(hist_hots, 1)
                body(0)
                with dve.Fori(1, HIST_COLS // GROUP // 2) as i:
                    body(i)
                dve.wait_ge(hist_used, (v + 1) * (HIST_COLS // GROUP))
            hots_of_columns(0)
            small(nc.vector.tensor_copy(deg_src[:, :], ps_T[:, 0:TILES]))
            split(hist_dst)
            dve.sem_inc(psem("hist_second"), 1)
            hots_of_columns(1)
            small(nc.vector.tensor_copy(dtmp[:, :], ps_T[:, 0:TILES]))
            small(nc.vector.tensor_scalar(inv_deg[:, :], dtmp[:, :], 1.0, None, ALU.max))
            small(nc.vector.reciprocal(inv_deg[:, :], inv_deg[:, :]))
            small(nc.vector.scalar_tensor_tensor(inv_deg[:, :], dtmp[:, :], 0.5, inv_deg[:, :], ALU.is_gt, ALU.mult))
            small(nc.vector.tensor_scalar(dinv[:, :], deg_src[:, :], 1.0, None, ALU.max))
            dve.sem_inc(psem("deg"), 1)

            def parts(x, rest, to, done):
                for n, make in enumerate((lambda: nc.vector.tensor_copy(to[0], x),
                                          lambda: nc.vector.tensor_tensor(rest, x, to[0], ALU.subtract),
                                          lambda: nc.vector.tensor_copy(to[1], rest),
                                          lambda: nc.vector.tensor_tensor(to[2], rest, to[1], ALU.subtract))):
                    done(n, make())

            def split_mat(m, i, b):
                dve.wait_ge(mat_in[b], 16 * i + 16)
                if not (isinstance(m, int) and m < 1):
                    dve.wait_ge(mat_out, 16 * m)

                def done(n, ins):
                    ins.then_inc(mat_steps, 1)
                    dve.wait_ge(mat_steps, 4 * m + n + 1)
                parts(mat[b], mat_rest, [mat3[:, q, :] for q in range(3)], done)
            split_mat(0, 0, 0)
            split_mat(1, 0, 1)
            with dve.Fori(1, MATS // 2) as i:
                split_mat(2 * i, i, 0)
                split_mat(2 * i + 1, i, 1)
            parts(gw[:, :, :], gate_rest, [gw3[:, q] for q in range(3)], lambda n, ins: small(ins))

            dve.wait_ge(gath, 16 * 4 * STEP_TILES)
            for i in range(STEP_TILES):
                step(nc.vector.tensor_copy(raw_f[:, 0, i, :], raw_i[:, 0, i, :]))
                step(nc.vector.tensor_scalar(raw_f[:, 1, i, :], raw_i[:, 1, i, :], step_base[:, i:i + 1], None,
                                             ALU.subtract))
                step(nc.vector.scalar_tensor_tensor(raw_f[:, 2, i, :], raw_i[:, 2, i, :], float(NP),
                                                    raw_f[:, 0, i, :], ALU.mult, ALU.add))
            dve.sem_inc(psem("step_rows"), 1)
            turned(0, (D_idx, D_key, D_rel, D_w))
            small(nc.vector.tensor_tensor(hop[:, 2:3], hop[:, 0:1], hop[:, 1:2], ALU.max))
            small(nc.vector.tensor_scalar(hop[:, 3:5], hop[:, 0:2], hop[:, 2:3], None, ALU.subtract))
            dve.sem_inc(psem("hop_logits"), 1)
            dve.wait_ge(misc_act, 2)
            small(nc.vector.reciprocal(dinv[:, :], dinv[:, :]))
            small(nc.vector.scalar_tensor_tensor(dinv[:, :], deg_src[:, :], 0.5, dinv[:, :], ALU.is_gt, ALU.mult))
            small(nc.vector.tensor_tensor(hop[:, 5:6], hop[:, 3:4], hop[:, 4:5], ALU.add))
            small(nc.vector.reciprocal(hop[:, 5:6], hop[:, 5:6]))
            small(nc.vector.tensor_scalar(hop[:, 3:5], hop[:, 3:5], hop[:, 5:6], None, ALU.mult))

            dve.sem_inc(consts, 1)

            def tile(a, t):
                return a[:, ds(t, 1), :]

            def stats(S, source):
                def do(t, i, b):
                    if not first(t):
                        dve.wait_ge(S.v.sem, S.v.at("norm", t - 2))
                    if "resid" in S.v.names:
                        dve.wait_ge(S.v.sem, S.v.at("resid", t))
                    else:
                        dve.wait_ge(S.load[b], 16 * i + 16)
                    dve.sem_inc(passed, 1)
                    nc.vector.bn_stats(st6[:, b, :], source(t, b)).then_inc(S.v.sem, 1)
                return do

            def moments(S):
                def do(t, i, b):
                    dve.wait_ge(S.v.sem, S.v.at("stats", t))
                    dve.sem_inc(passed, 1)
                    nc.vector.bn_aggr(mv[:, b, 0:2], st6[:, b, :]).then_inc(S.v.sem, 1)
                return do

            def rstd(S):
                def do(t, i, b):
                    dve.wait_ge(S.s.sem, S.s.at("std", t))
                    nc.vector.reciprocal(mv[:, b, 3:4], mv[:, b, 2:3]).then_inc(S.v.sem, 1)
                return do

            def norm(S, source, to, free):
                def do(t, i, b):
                    dve.wait_ge(S.v.sem, S.v.at("rstd", t))
                    for steps, name in free:
                        if not first(t):
                            dve.wait_ge(steps.sem, steps.at(name, t - 2))
                    nc.vector.tensor_scalar(to(b), source(t, b), mv[:, b, 0:1], mv[:, b, 3:4], ALU.subtract,
                                            ALU.mult).then_inc(S.v.sem, 1)
                return do

            def rest(S):
                def do(t, i, b):
                    dve.wait_ge(S.s.sem, S.s.at("hT", t))
                    nc.vector.tensor_tensor(nr[b][:, :, :], TT[b], nhT[b][:, 0], ALU.subtract).then_inc(S.v.sem, 1)
                return do

            def low(S):
                def do(t, i, b):
                    dve.wait_ge(S.s.sem, S.s.at("mid", t))
                    nc.vector.tensor_tensor(nhT[b][:, 2], nr[b][:, :, :], nhT[b][:, 1], ALU.subtract
                                            ).then_inc(S.v.sem, 1)
                return do

            def own(S, l):
                def do(t, i, b):
                    dve.wait_ge(S.t.sem, S.t.at("prod", t))
                    nc.vector.tensor_tensor(tile(keep, t), ps_M[:, b:b + 1, 0:D], bias[:, l:l + 1, :], ALU.add
                                            ).then_inc(S.v.sem, 1)
                return do

            def table(t, i, b):
                dve.wait_ge(A.t.sem, A.t.at("prod", t))
                if not first(t):
                    dve.wait_ge(A.store[b], 16 * i)
                nc.vector.tensor_copy(nt[b][:, :], ps_M[:, b, 0:D]).then_inc(A.v.sem, 1)
            walk(dve, A.v, dict(stats=stats(A, lambda t, b: nx[b][:, :]), moments=moments(A), rstd=rstd(A),
                                norm=norm(A, lambda t, b: nx[b][:, :], lambda b: ny[b][:, :], [(A.s, "keep")]),
                                rest=rest(A), low=low(A), table=table))
            find_steps(1)
            dve.wait_ge(gath, 16 * 5 * STEP_TILES)
            for i in range(STEP_TILES):
                step(nc.vector.tensor_scalar(raw_k[:, i, :], raw_s[:, i, :, 1], step_base[:, i:i + 1], None,
                                             ALU.subtract))
            dve.sem_inc(psem("step_rows"), 1)
            turned(1, (S_idx, S_key, S_w))
            dve.wait_ge(psem("turned"), 2 * STEP_TILES)
            dve.sem_inc(psem("tables"), 1)
            dve.wait_ge(tile_in, 32)
            nc.vector.memset(acc_row, 0.0).then_inc(acc_ready, 1)
            dve.sem_inc(added, GROUP)
            dve.wait_ge(acc_ready, 1)

            tiles_r = [dve.alloc_register(f"step_tile{j}") for j in range(GROUP)]

            def sums(l, key, weight, into=acc):
                row = tile_row[1 if key is S_key else 0]

                def hot(g, k, used):
                    dve.wait_ge(half_sums, 2 * used)
                    for j in range(GROUP):
                        o, s = onehot[:, GROUP * k + j, :], GROUP * g + j
                        if weight is None:
                            ins = nc.vector.tensor_scalar(o, iota[:, :], key[:, ds(s, 1)], None, ALU.is_equal)
                        else:
                            ins = nc.vector.tensor_scalar(o, iota[:, :], key[:, ds(s, 1)], weight[:, ds(s, 1)],
                                                          ALU.is_equal, ALU.mult)
                        ins.then_inc(hots, 1)

                def group(g, k, last):
                    if not last:
                        hot(g + 1, 1 - k, LAP + l * GROUPS + g)
                    dve.load(tiles_r, row[0:1, ds(GROUP * g, GROUP)])
                    for h in range(2):
                        dve.wait_ge(half_sums, 2 * (LAP + l * GROUPS + g) + h + 1)
                        for j in range(h * HALF, (h + 1) * HALF):
                            t = dve.snap(tiles_r[j], min_val=0, max_val=TILES - 1)
                            dve.wait_ge(added, GROUP + l * STEPS + GROUP * g + j)
                            a = tile(into, t)
                            nc.vector.tensor_tensor(a, a, ps_sum[:, j:j + 1, :], ALU.add).then_inc(added, 1)
                def pair(it, i, c):
                    group(2 * it, 0, False)
                    group(2 * it + 1, 1, isinstance(it, int) and it == GROUPS // 2 - 1)
                hot(0, 0, LAP + l * GROUPS)
                if l in own_products:
                    Q = own_products[l]
                    walk_pairs(dve, pair, Q.v, dict(rest=rest(Q), low=low(Q), self=own(Q, l - 2)))
                else:
                    walk_pairs(dve, pair)

            sums(0, S_key, S_w)
            dve.wait_ge(added, GROUP + STEPS)
            dve.wait_ge(A.s.sem, A.s.at("keep", TILES - 1))
            small(nc.vector.scalar_tensor_tensor(keep_row, acc_row, hop[:, 3:4], keep_row, ALU.mult, ALU.add))
            small(nc.vector.tensor_scalar(S_w, S_w, hop[:, 4:5], None, ALU.mult))
            sums(1, S_key, S_w, keep)
            dve.wait_ge(added, GROUP + 2 * STEPS)

            def resid(t, i, b):
                if not first(t):
                    dve.wait_ge(x1_out[b], 16 * i)
                    dve.wait_ge(C.v.sem, C.v.at("norm", t - 2))
                dve.wait_ge(C.load[b], 16 * i + 16)
                nc.vector.scalar_tensor_tensor(wide(ny[b]), tile(keep, t), 0.0, wide(nx[b]), ALU.max, ALU.add
                                               ).then_inc(C.v.sem, 1)
            walk(dve, C.v, dict(resid=resid, stats=stats(C, lambda t, b: ny[b][:, :]), moments=moments(C),
                                rstd=rstd(C), norm=norm(C, lambda t, b: ny[b][:, :], lambda b: nh[b][:, :],
                                                      [(C.t, "hT"), (C.s, "keep")]),
                                rest=rest(C), low=low(C)))
            dve.wait_ge(C.p.sem, C.p.at("clear", TILES - 1))
            sums(2, D_key, None)

            for l, S in ((3, D1), (4, D2)):
                dve.wait_ge(added, GROUP + l * STEPS)
                Q = own_products[l - 1]
                dve.wait_ge(Q.v.sem, Q.v.at("self", TILES - 1))

                def total(t, i, b):
                    if not first(t):
                        dve.wait_ge(S.s.sem, S.s.at("keep", t - 2))
                    nc.vector.scalar_tensor_tensor(wide(ny[b]), tile(acc, t), inv_deg[:, ds(t, 1)], tile(keep, t),
                                                   ALU.mult, ALU.add).then_inc(S.v.sem, 1)
                walk(dve, S.v, dict(sum=total, rest=rest(S), low=low(S)))
                dve.wait_ge(S.p.sem, S.p.at("clear", TILES - 1))
                sums(l, D_key, None)

            dve.wait_ge(added, GROUP + 5 * STEPS)
            dve.wait_ge(own_products[4].v.sem, own_products[4].v.at("self", TILES - 1))

            def total(t, i, b):
                if not first(t):
                    dve.wait_ge(Es.v.sem, Es.v.at("resid", t - 2))
                nc.vector.scalar_tensor_tensor(wide(ny[b]), tile(acc, t), inv_deg[:, ds(t, 1)], tile(keep, t),
                                               ALU.mult, ALU.add).then_inc(Es.v.sem, 1)

            def resid(t, i, b):
                dve.wait_ge(Es.v.sem, Es.v.at("sum", t))
                dve.wait_ge(Es.load[b], 16 * i + 16)
                nc.vector.tensor_tensor(tile(keep, t), wide(ny[b]), wide(nx[b]), ALU.add).then_inc(Es.v.sem, 1)

            def kept(t, b):
                return keep[:, ds(t, 1), :].rearrange("p o d -> p (o d)")
            walk(dve, Es.v, dict(sum=total, resid=resid, stats=stats(Es, kept), moments=moments(Es), rstd=rstd(Es),
                                 norm=norm(Es, kept, lambda b: nh[b][:, :], [(Es.s, "scaled")])))
            dve.wait_ge(Es.p.sem, Es.p.at("clear", TILES - 1))
            sums(5, S_key, None)

            def agg_rest(t, i, b):
                dve.wait_ge(Fs.s.sem, Fs.s.at("aT", t))
                nc.vector.tensor_tensor(nr[0][:, :, :], TT[0], naT[:, 0], ALU.subtract).then_inc(Fs.v.sem, 1)

            def agg_low(t, i, b):
                dve.wait_ge(Fs.s.sem, Fs.s.at("amid", t))
                nc.vector.tensor_tensor(naT[:, 2], nr[0][:, :, :], naT[:, 1], ALU.subtract).then_inc(Fs.v.sem, 1)

            def biased(t, i, b):
                dve.wait_ge(Fs.t.sem, Fs.t.at("prod", t))
                nc.vector.tensor_tensor(nx[b][:, :], ps_M[:, 0, 0:D], bias[:, 3, :], ALU.add).then_inc(Fs.v.sem, 1)

            def leaky(t, i, b):
                dve.wait_ge(Fs.v.sem, Fs.v.at("biased", t))
                nc.vector.scalar_tensor_tensor(nx[b][:, :], nx[b][:, :], LEAK, nx[b][:, :], ALU.mult, ALU.max
                                               ).then_inc(Fs.v.sem, 1)

            def resid(t, i, b):
                dve.wait_ge(Fs.v.sem, Fs.v.at("leaky", t))
                nc.vector.tensor_tensor(tile(keep, t), wide(nx[b]), tile(keep, t), ALU.add).then_inc(Fs.v.sem, 1)

            def h_rest(t, i, b):
                dve.wait_ge(Fs.s.sem, Fs.s.at("hT", t))
                nc.vector.tensor_tensor(nr[1][:, :, :], TT[1], nhT[b][:, 0], ALU.subtract).then_inc(Fs.v.sem, 1)

            def h_low(t, i, b):
                dve.wait_ge(Fs.s.sem, Fs.s.at("mid", t))
                nc.vector.tensor_tensor(nhT[b][:, 2], nr[1][:, :, :], nhT[b][:, 1], ALU.subtract
                                        ).then_inc(Fs.v.sem, 1)

            def messages(u):
                def do(t, i, b):
                    dve.wait_ge(Fs.s.sem, Fs.s.at("gate", t))
                    dve.wait_ge(Fs.t.sem, Fs.t.at(f"m{u}", t))
                    if not (isinstance(t, int) and 2 * t + u // 4 < 1):
                        dve.wait_ge(msgs_out[u % 4], 16 * (2 * t + u // 4))
                    nc.vector.tensor_scalar(msg[:, u % 4, 0, :], ps_sum[:, 2 * (u % 4), :], gate[:, b, 2 * u:2 * u + 1],
                                            None, ALU.mult)
                    nc.vector.tensor_scalar(msg[:, u % 4, 1, :], ps_sum[:, 2 * (u % 4) + 1, :],
                                            gate[:, b, 2 * u + 1:2 * u + 2], None, ALU.mult).then_inc(Fs.v.sem, 1)
                return do
            walk(dve, Fs.v, dict(arest=agg_rest, alow=agg_low, biased=biased, leaky=leaky, resid=resid,
                                 stats=stats(Fs, kept), moments=moments(Fs), rstd=rstd(Fs),
                                 norm=norm(Fs, kept, lambda b: nh[b][:, :], [(Fs.t, "hT")]), rest=h_rest, low=h_low,
                                 m0=messages(0), m2=messages(2), m4=messages(4), m6=messages(6)))
            dve.wait_ge(Fs.p.sem, Fs.p.at("clear", TILES - 1))
            for q in msgs_out:
                dve.wait_ge(q, 16 * 2 * TILES)
            sums(6, D_key, D_w)

            dve.wait_ge(added, GROUP + 7 * STEPS)
            for t in range(0, TILES, OUT_TILES):
                nc.vector.scalar_tensor_tensor(keep[:, t:t + OUT_TILES, :], acc[:, t:t + OUT_TILES, :], 0.0,
                                               keep[:, t:t + OUT_TILES, :], ALU.max, ALU.add).then_inc(out_ready, 1)

        @block.tensor
        def _(pe):
            def find_steps(k):
                pe.wait_ge(psem("cnt"), k + 1)
                nc.tensor.matmul(ps_h[:, 0:TILES - 1], ones[:, :], cnt, start=True, stop=True).then_inc(prep_pe, 1)
                pe.wait_ge(psem("step_chunk"), k + 1)
                nc.tensor.transpose(ps_h[0:STEP_TILES, P:2 * P], step_tile, ident[:, :]).then_inc(prep_pe, 1)

            def turn_rows(k, fields):
                pe.wait_ge(psem("step_rows"), k + 1)
                for i in range(STEP_TILES):
                    if i + k >= 2:
                        pe.wait_ge(psem("turned"), STEP_TILES * k + i - 1)
                    for q, field in enumerate(fields):
                        ins = nc.tensor.transpose(ps_M[:, i % 2, q * P:(q + 1) * P], field(i), ident[:, :])
                    ins.then_inc(prep_pe, 1)
            pe.wait_ge(psem("iota"), 7)
            find_steps(0)

            def body(k, b, first):
                pe.wait_ge(sort_masks, k + 1)
                if not first:
                    pe.wait_ge(sort_blocks, k)
                for i in range(COL_BLOCKS):
                    ins = nc.tensor.matmul(ps_h[:, i:i + 1], masks[b][:, i * P:(i + 1) * P], ones_b[0:HIST_ROWS, :],
                                           start=True, stop=True)
                ins.then_inc(sort_counts, 1)
                if not (isinstance(k, int) and k < 2):
                    pe.wait_ge(sort_picks, 2 * (k - 1))
                to = ps_sum[0:HIST_ROWS, 4 * b:4 * b + 4, :].rearrange("p a b -> p (a b)")
                parts = [(0, 512), (512, HIST_COLS)]
                for lo, hi in parts:
                    nc.tensor.matmul(to[:, lo:hi], before[0:HIST_ROWS, 0:HIST_ROWS], masks[b][:, lo:hi], start=True,
                                     stop=False)
                pe.wait_ge(sort_blocks, k + 1)
                for i in reversed(range(COL_BLOCKS)):
                    block_counts = in_block[:, i:i + 1].to_broadcast([P, HIST_ROWS])
                    for lo, hi in parts:
                        a = max(lo, i * P)
                        if a < hi:
                            ins = nc.tensor.matmul(to[:, a:hi], block_counts, before[:, a - i * P:hi - i * P],
                                                   start=False, stop=(i == 0))
                ins.then_inc(sort_ranks, 1)
                if not first:
                    pe.wait_ge(sort_begins, k)
                for i in range(COL_BLOCKS):
                    ins = nc.tensor.matmul(ps_T[0:HIST_ROWS, 0:1], in_block[:, i:i + 1].to_broadcast([P, HIST_ROWS]),
                                           ones_b[:, :], start=(i == 0), stop=(i == COL_BLOCKS - 1))
                ins.then_inc(sort_totals, 1)
            pe.wait_ge(psem("sort_start"), 1)
            body(0, 0, True)
            body(1, 1, False)
            with pe.Fori(1, TILES // 2) as i:
                body(2 * i, 0, False)
                body(2 * i + 1, 1, False)
            body(TILES - 1, 0, False)

            def turn(S, after="relu"):
                def do(t, i, b):
                    pe.wait_ge(S.s.sem, S.s.at(after, t))
                    if not first(t):
                        pe.wait_ge(S.v.sem, S.v.at("rest", t - 2))
                    for k in range(2):
                        ins = nc.tensor.transpose(TT[b][:, k, :], nh[b][:, k * P:(k + 1) * P], ident[:, :])
                    ins.then_inc(S.t.sem, 1)
                return do

            def product(to, h, w):
                for n, (hp, wp) in enumerate(PAIRS):
                    for k in range(2):
                        ins = nc.tensor.matmul(to, h[:, hp, k, :], w(wp, k), start=(n + k == 0),
                                               stop=(n == len(PAIRS) - 1 and k == 1))
                return ins

            pe.wait_ge(sort_begins, TILES)
            for v in range(2):
                if v:
                    pe.wait_ge(psem("hist_second"), 1)
                nc.tensor.matmul(ps_T[:, 0:TILES], zeros[:, 0:P], zeros[:, 0:TILES], start=True, stop=False,
                                 skip_group_check=True).then_inc(psem("hist_clear"), 1)
                pe.wait_ge(psem("hist_clear"), v + 1)
                with pe.Fori(0, HIST_COLS // GROUP // 2) as i:
                    for b in range(2):
                        pe.wait_ge(hist_hots, 2 * (v * (HIST_COLS // GROUP) + 2 * i + b + 1))
                        for j in range(GROUP):
                            ins = nc.tensor.matmul(ps_T[:, 0:TILES], lo_hot[:, b, j, :], hi_hot[:, b, j, :],
                                                   start=False, stop=False, skip_group_check=True)
                        ins.then_inc(hist_used, 1)
            turn_rows(0, [lambda i, q=q: raw_f[:, q, i, :] for q in range(4)])
            def prod(t, i, b):
                pe.wait_ge(A.v.sem, A.v.at("low", t))
                if not first(t):
                    pe.wait_ge(A.v.sem, A.v.at("table", t - 2))
                product(ps_M[:, b, 0:D], nhT[b], lambda q, k: W[0][:, q, 0, k, :]).then_inc(A.t.sem, 1)
            pe.wait_ge(consts, 1)
            pe.wait_ge(weights_in[0], 16)
            walk(pe, A.t, dict(prod=prod, hT=turn(A)))

            find_steps(1)
            turn_rows(1, [lambda i: raw_s[:, i, :, 0], lambda i: raw_k[:, i, :], lambda i: raw_s[:, i, :, 2]])

            pe.sem_inc(half_sums, 2 * LAP)

            def sums(l):
                def pair(it, i, c):
                    for k in range(2 * c, 2 * c + 2):
                        g = LAP * i + k
                        pe.wait_ge(gathered[k], 16 * GROUP * (l * LAPS + i + 1))
                        for h in range(2):
                            pe.wait_ge(hots, l * STEPS + GROUP * g + HALF * (h + 1))
                            pe.wait_ge(added, l * STEPS + GROUP * g + HALF * (h + 1))
                            for j in range(h * HALF, (h + 1) * HALF):
                                ins = nc.tensor.matmul(ps_sum[:, j, :], onehot[:, GROUP * (k % 2) + j, :],
                                                       ring[:, GROUP * k + j, :], start=True, stop=True)
                            ins.then_inc(half_sums, 1)
                if l not in own_products:
                    walk_pairs(pe, pair)
                    return
                Q = own_products[l]

                def prod(t, i, b):
                    pe.wait_ge(Q.v.sem, Q.v.at("low", t))
                    if not first(t):
                        pe.wait_ge(Q.v.sem, Q.v.at("self", t - 2))
                    product(ps_M[:, b, 0:D], nhT[b], lambda q, k: W[(l - 1) % 2][:, q, 0, k, :]).then_inc(Q.t.sem, 1)
                walk_pairs(pe, pair, Q.t, dict(hT=turn(Q, "fetch"), prod=prod))
            sums(0)
            sums(1)
            for l, (S, n) in enumerate(((C, 1), (D1, 2), (D2, 3))):
                def prod(t, i, b):
                    pe.wait_ge(S.v.sem, S.v.at("low", t))
                    if not first(t):
                        pe.wait_ge(S.s.sem, S.s.at("table", t - 2))
                    product(ps_M[:, b, 0:D], nhT[b], lambda q, k: W[n % 2][:, q, 1, k, :]).then_inc(S.t.sem, 1)
                pe.wait_ge(weights_in[n], 32)
                pe.wait_ge(added, GROUP + (l + 2) * STEPS)
                walk(pe, S.t, dict(prod=prod, hT=turn(S)))
                pe.wait_ge(S.s.sem, S.s.at("table", TILES - 1))
                sums(l + 2)
            sums(5)

            def agg_turn(t, i, b):
                pe.wait_ge(Fs.s.sem, Fs.s.at("agg", t))
                for k in range(2):
                    ins = nc.tensor.transpose(TT[0][:, k, :], nh[b][:, k * P:(k + 1) * P], ident[:, :])
                ins.then_inc(Fs.t.sem, 1)

            def conv(t, i, b):
                pe.wait_ge(Fs.v.sem, Fs.v.at("alow", t))
                product(ps_M[:, 0, 0:D], naT, lambda q, k: W[0][:, q, 0, k, :]).then_inc(Fs.t.sem, 1)

            def h_turn(t, i, b):
                pe.wait_ge(Fs.s.sem, Fs.s.at("relu", t))
                for k in range(2):
                    ins = nc.tensor.transpose(TT[1][:, k, :], nh[b][:, k * P:(k + 1) * P], ident[:, :])
                ins.then_inc(Fs.t.sem, 1)

            def gates(t, i, b):
                pe.wait_ge(Fs.v.sem, Fs.v.at("low", t))
                product(ps_M[:, 1, 0:RELS], nhT[b], lambda q, k: gw3[:, q, k, :]).then_inc(Fs.t.sem, 1)

            def messages(u):
                def do(t, i, b):
                    out_by = Fs.s if u % 2 else Fs.v
                    if u >= 4:
                        pe.wait_ge(out_by.sem, out_by.at(f"m{u - 4}", t))
                    elif not (isinstance(t, int) and t < 1):
                        pe.wait_ge(out_by.sem, out_by.at(f"m{u + 4}", t - 1))
                    if u == 0 and isinstance(t, int) and t == 0:
                        pe.wait_ge(weights_in[4], 48)
                    product(ps_sum[:, 2 * (u % 4):2 * (u % 4) + 2, :], nhT[b],
                            lambda q, k: W3[q][:, 2 * u:2 * u + 2, k, :]).then_inc(Fs.t.sem, 1)
                return do
            pe.wait_ge(conv_weights_in, 16)
            pe.wait_ge(added, GROUP + 6 * STEPS)
            walk(pe, Fs.t, dict(aT=agg_turn, prod=conv, hT=h_turn, gate=gates,
                                **{f"m{u}": messages(u) for u in range(RELS // 2)}))
            sums(6)


_INS = ['x', 'src', 'dst', 'edge_type_16', 'edge_weight', 'edge_weight1', 'L0_gnn_weight', 'L0_gnn_hop_logits',
        'L1_gnn_W_self', 'L1_gnn_W_neigh', 'L1_gnn_bias', 'L2_gnn_W', 'L2_gnn_b', 'L3_gnn_weight',
        'L3_gnn_gate_weight']


def kernel(**inputs):
    import numpy as _np
    import concourse.bacc as _bacc
    from concourse import mybir as _mybir
    from concourse.bass_utils import run_bass_kernel_spmd as _run

    nc = _bacc.Bacc("TRN2", target_bir_lowering=False, num_devices=1)
    arrays, args = {}, []
    for name in _INS:
        a = _np.ascontiguousarray(inputs[name])
        if name == 'edge_weight1':
            a = a.reshape(-1)
        arrays[f"in_{name}_dram"] = a
        args.append(nc.dram_tensor(f"in_{name}_dram", a.shape, _mybir.dt.from_np(a.dtype), kind="ExternalInput").ap())
    args.append(nc.dram_tensor("out_0_dram", (N, D), _mybir.dt.float32, kind="ExternalOutput").ap())
    gnn(nc, *args)
    r = _run(nc, [arrays], core_ids=[0])
    return r.results[0]["out_0_dram"]
```

```python
import concourse.bass as bass
from concourse import mybir
from contextlib import ExitStack

P = 128
N = 6250
E = 100000
D = 256
RELS = 16
TILES = -(-N // P)
NP = TILES * P
LAST_ROWS = N - (TILES - 1) * P
CHUNKS = -(-E // P)
STEP_TILES = -(-(CHUNKS + TILES) // P)
TAB = STEP_TILES * P
GROUP = 8
LAP = 4
LAPS = -(-(CHUNKS + TILES - 1) // (GROUP * LAP))
GROUPS = LAPS * LAP
STEPS = GROUPS * GROUP
HALF = GROUP // 2
OUT_TILES = 7
HIST_ROWS = 125
HIST_COLS = E // HIST_ROWS
NO_NODE = 1 << 20
SORT_SLOTS = 32
SORT_LAPS = HIST_COLS // SORT_SLOTS
EARLY_RANKS = 6
COL_BLOCKS = -(-HIST_COLS // P)
FIELDS = 3
LN_EPS = 1e-5
LEAK = 0.2

F32 = mybir.dt.float32
I32 = mybir.dt.int32
BF16 = mybir.dt.bfloat16
ALU = mybir.AluOpType
ACT = mybir.ActivationFunctionType
AX = mybir.AxisListType
ds = bass.ds


MATS = 8 + RELS
PAIRS = [(2, 0), (0, 2), (1, 1), (1, 0), (0, 1), (0, 0)]
LEAD = 3


class Steps:

    def __init__(self, sem, steps, lead=LEAD):
        self.sem, self.names, self.ahead, self.lead = sem, [n for n, _ in steps], dict(steps), lead

    def at(self, name, t):
        return len(self.names) * (t - self.ahead[name] + self.lead) + self.names.index(name) + 1

    def iteration(self, eng, do, it, i, c):
        for n, name in enumerate(self.names):
            a = self.ahead[name]
            t = it + a
            if isinstance(t, int) and not 0 <= t < TILES:
                if self.sem is not None:
                    before = len(self.names) * (it + self.lead) + n
                    if before:
                        eng.wait_ge(self.sem, before)
                    eng.sem_inc(self.sem, 1)
            else:
                do[name](t, i + (c + a) // 2, (c + a) % 2)


def walk(eng, steps, do):
    def iteration(it, i, c):
        steps.iteration(eng, do, it, i, c)
    for it in range(-LEAD, 4):
        iteration(it, it // 2, it % 2)
    with eng.Fori(2, TILES // 2 - 2) as i:
        for c in range(2):
            iteration(2 * i + c, i, c)
    for it in range(TILES - 5, TILES + 2):
        iteration(it, it // 2, it % 2)


def walk_pairs(eng, pair, steps=None, do=None, pair_first=False):
    def iteration(it, i, c):
        if pair_first:
            pair(it, i, c)
        if steps:
            steps.iteration(eng, do, it, i, c)
        if not pair_first:
            pair(it, i, c)
    head, tail = (6, TILES - 1) if steps else (0, GROUPS // 2 - 2)
    for it in range(head):
        iteration(it, it // 2, it % 2)
    with eng.Fori(head // 2, tail // 2) as i:
        for c in range(2):
            iteration(2 * i + c, i, c)
    for it in range(tail, GROUPS // 2):
        iteration(it, it // 2, it % 2)
    if steps:
        it = GROUPS // 2
        steps.iteration(eng, do, it, it // 2, it % 2)


def over_tiles(eng, body):
    walk(eng, Steps(None, [("body", 0)]), dict(body=body))


def first(t):
    return isinstance(t, int) and t < 2


def gnn(nc, x, src, dst, edge_type, w0, w1, L0_w, L0_hop, L1_ws, L1_wn, L1_b, L2_w, L2_b, L3_w, L3_g, out):
    ctx = ExitStack()
    with ctx:
        def sb(name, shape, dt=F32):
            return ctx.enter_context(nc.sbuf_tensor(name, shape, dt))

        def pb(name, shape, dt=F32):
            return ctx.enter_context(nc.psum_tensor(name, shape, dt))

        def sem(name):
            return ctx.enter_context(nc.semaphore(name))

        def dram(name, shape, dt=F32):
            return nc.dram_tensor(name, shape, dt).ap()

        srcD, dstD, typD = (dram(n, [TAB, P], I32) for n in ("srcD", "dstD", "typD"))
        w1D = dram("w1D", [TAB, P])
        by_srcD = dram("by_srcD", [TAB * P, FIELDS])
        tileD = [dram(f"tileD{k}", [STEP_TILES, P], I32) for k in range(2)]
        tables = [dram(f"table{l}", [NP, D]) for l in range(6)]
        rel_table = dram("rel_table", [RELS * NP, D])
        x1D = dram("x1D", [NP, D])
        matD = dram("matD", [MATS, D, D])
        splitD = dram("splitD", [MATS, P, 3, 2 * D], BF16)

        acc = sb("acc", [P, TILES, D])
        keep = sb("keep", [P, TILES, D])
        ring = sb("ring", [P, LAP * GROUP, D])
        D_idx = sb("D_idx", [P, TAB], I32)
        D_rel = sb("D_rel", [P, TAB], I32)
        D_key = sb("D_key", [P, TAB])
        D_w = sb("D_w", [P, TAB])
        early = sb("early", [P, RELS * D])
        S_idx = early[:, 0:TAB].bitcast(I32)
        S_key = early[:, TAB:2 * TAB]
        S_w = early[:, 2 * TAB:3 * TAB]
        tile_row = [sb("tile_row", [1, TAB], I32), early[0:1, 3 * TAB:4 * TAB].bitcast(I32)]
        onehot = sb("onehot", [P, 2 * GROUP, P])
        stage = sb("stage", [P, LAP * GROUP], I32)
        W = [sb(f"W{b}", [P, 3, 2, 2, D], BF16) for b in range(2)]
        gw = sb("gw", [P, 2, RELS])
        gw3 = sb("gw3", [P, 3, 2, RELS], BF16)
        bias = sb("bias", [P, 4, D])
        ident = sb("ident", [P, P])
        iota = sb("iota", [P, P])
        ones_b = sb("ones_b", [P, 1], BF16)
        zeros = sb("zeros", [P, D])
        deg_src = sb("deg_src", [P, TILES])
        dinv = sb("dinv", [P, TILES])
        inv_deg = sb("inv_deg", [P, TILES])
        dtmp = sb("dtmp", [P, TILES])
        hop = sb("hop", [P, 8])
        eps = sb("eps", [P, 1])
        part = sb("part", [P, 1])
        nx = [sb(f"nx{b}", [P, D]) for b in range(2)]
        ny = [sb(f"ny{b}", [P, D]) for b in range(2)]
        nh = [sb(f"nh{b}", [P, D]) for b in range(2)]
        nhT = [sb(f"nhT{b}", [P, 3, 2, P], BF16) for b in range(2)]
        naT = sb("naT", [P, 3, 2, P], BF16)
        nr = [sb(f"nr{b}", [P, 2, P]) for b in range(2)]
        nt = [sb(f"nt{b}", [P, D]) for b in range(2)]
        st6 = sb("st6", [P, 2, 6])
        mv = sb("mv", [P, 2, 4])
        gate = sb("gate", [P, 2, RELS])
        keep_row = keep[:, :, :].rearrange("p a b -> p (a b)")
        acc_row = acc[:, :, :].rearrange("p a b -> p (a b)")
        ring_row = ring[:, :, :].rearrange("p a b -> p (a b)")

        class Room:

            def __init__(self, row):
                self.row, self.at = row, 0

            def take(self, n, dt=F32):
                a = self.row[:, self.at:self.at + n]
                self.at += n
                return a if dt == F32 else a.bitcast(dt)

        cells = STEP_TILES * P
        room = Room(keep_row)
        raw_i = room.take(3 * cells, I32).rearrange("p (k i e) -> p k i e", k=3, e=P)
        raw_f = room.take(4 * cells).rearrange("p (k i e) -> p k i e", k=4, e=P)
        gate_rest = room.take(2 * RELS).rearrange("p (k r) -> p k r", k=2)
        room = Room(acc_row)
        last_i, last_f = room.take(STEP_TILES, I32), room.take(STEP_TILES)
        thr, tnum = room.take(TILES - 1), room.take(TILES - 1)
        snum = room.take(STEP_TILES)
        step_tile, step_base = room.take(STEP_TILES), room.take(STEP_TILES)
        step_chunk = room.take(STEP_TILES, I32)
        cnt, first_step = room.take(TILES - 1), room.take(TILES - 1)
        cmp = room.take(STEP_TILES * (TILES - 1)).rearrange("p (i t) -> p i t", i=STEP_TILES)
        pad_i = room.take(3 * P, I32).rearrange("p (k e) -> p k e", e=P)
        pad_s = room.take(FIELDS * P).rearrange("p (e f) -> p e f", f=FIELDS)
        tile_i = room.take(P, I32)[0:STEP_TILES, :]
        columns = room.take(HIST_COLS)
        ones = room.take(P)
        before = room.take(HIST_COLS // 2, BF16)
        masks = [room.take(COL_BLOCKS * P // 2, BF16)[0:HIST_ROWS, :] for b in range(2)]
        picked = room.take(HIST_COLS)[0:HIST_ROWS, :]
        rank = room.take(HIST_COLS)[0:HIST_ROWS, :]
        rank_i = room.take(HIST_COLS, I32)[0:HIST_ROWS, :]
        begin = room.take(TILES + 1)[0:HIST_ROWS, :]
        in_block = room.take(8, BF16)
        hist_src = room.take(HIST_COLS, I32)[0:HIST_ROWS, :]
        hist_w = room.take(HIST_COLS)[0:HIST_ROWS, :]
        hist_lo, hist_hi = (room.take(HIST_COLS)[0:HIST_ROWS, :] for _ in range(2))
        hist_dst = room.take(HIST_COLS, I32)[0:HIST_ROWS, :]
        room = Room(ring_row)
        record = room.take(FIELDS * HIST_COLS)[0:HIST_ROWS, :].rearrange("p (c f) -> p c f", f=FIELDS)
        rec_stage = room.take(FIELDS * SORT_SLOTS)[0:HIST_ROWS, :].rearrange("p (c f) -> p c f", f=FIELDS)
        lo_hot = room.take(GROUP * P, BF16)[0:HIST_ROWS, :].rearrange("p (b j e) -> p b j e", b=2, e=P)
        hi_hot = room.take(GROUP * TILES, BF16)[0:HIST_ROWS, :].rearrange("p (b j e) -> p b j e", b=2, e=TILES)
        mat = [room.take(2 * D) for b in range(2)]
        mat_rest = room.take(2 * D)
        mat3 = room.take(3 * D, BF16).rearrange("p (s c) -> p s c", s=3)
        room = Room(ring_row)
        raw_s = room.take(FIELDS * cells).rearrange("p (i e f) -> p i e f", f=FIELDS, e=P)
        raw_k = room.take(cells).rearrange("p (i e) -> p i e", e=P)
        ring_b = ring_row.bitcast(BF16).rearrange("p (s r k d) -> p s r k d", s=2, r=RELS, k=2)
        W3 = [ring_b[:, 0], ring_b[:, 1],
              early[:, :].bitcast(BF16).rearrange("p (r k d) -> p r k d", r=RELS, k=2)]
        msg = onehot[:, :, :].rearrange("p a b -> p (a b)").rearrange("p (u r d) -> p u r d", u=4, r=2)

        ps_sum = pb("ps_sum", [P, GROUP, D])
        ps_T = pb("ps_T", [P, 2 * D])
        ps_M = pb("ps_M", [P, 2, 2 * D])
        ps_h = pb("ps_h", [P, 2 * D])
        TT = [a[:, 0:D].rearrange("p (k e) -> p k e", k=2) for a in (ps_T, ps_h)]

        prep = {}

        def psem(name):
            if name not in prep:
                prep[name] = sem("p_" + name)
            return prep[name]

        copied = sem("inputs_copied")
        padded = sem("pads_ready")
        loaded = sem("prep_loaded")
        gath = sem("step_rows_gathered")
        weights_in = [sem(f"weights_in{n}") for n in range(5)]
        conv_weights_in, rel_weights_in = sem("conv_weights_in"), sem("rel_weights_in")
        consts = sem("consts_ready")
        prep_dve = sem("prep_vector")
        prep_pe = sem("prep_tensor")
        tile_out = sem("tile_row_out")
        tile_in = sem("tile_row_in")
        sort_masks = sem("sort_masks_ready")
        sort_counts = sem("sort_counts_ready")
        sort_blocks = sem("sort_counts_out")
        sort_totals = sem("sort_totals_ready")
        sort_begins = sem("sort_begins_ready")
        sort_ranks = sem("sort_ranks_ready")
        sort_picks = sem("sort_picks")
        sort_staged = sem("sort_slots_staged")
        sorted_out = [sem(f"sorted_rows_out{h}") for h in range(2)]
        hist_in = sem("hist_in")
        hist_used = sem("hist_onehots_used")
        misc_act = sem("small_scalar")
        misc_dve = sem("small_vector")

        passed = sem("waits_passed")
        staged = sem("indices_staged")
        gathered = [sem(f"rows_gathered{k}") for k in range(LAP)]
        hots = sem("onehots_ready")
        hist_hots = sem("hist_onehots_ready")
        half_sums = sem("half_sums_ready")
        added = sem("steps_added")
        acc_ready = sem("acc_ready")
        x1_out = [sem(f"x1_out{b}") for b in range(2)]
        msgs_out = [sem(f"messages_out{j}") for j in range(4)]
        mat_copied, mat_in, mat_out = sem("mats_copied"), [sem(f"mat_in{b}") for b in range(2)], sem("mat_parts_out")
        mat_steps = sem("mat_parts_ready")
        hop_table_out = sem("hop_table_out")

        block = ctx.enter_context(nc.Block())

        class NodeStage:

            def __init__(self, name, vector, scalar, tensor, pool):
                self.v = Steps(sem(name + "_vector"), vector) if vector else None
                self.s = Steps(sem(name + "_scalar"), scalar) if scalar else None
                self.t = Steps(sem(name + "_tensor"), tensor) if tensor else None
                self.p = Steps(sem(name + "_pool"), pool) if pool else None
                self.load = [sem(f"{name}_loaded{b}") for b in range(2)]
                self.store = [sem(f"{name}_stored{b}") for b in range(2)]

        IN = NodeStage("in",
                      [("rstd", 2), ("norm", 2), ("rest", 1), ("stats", 3), ("moments", 3), ("low", 1), ("table", -1)],
                      [("hT", 1), ("relu", 2), ("keep", 2), ("mid", 1), ("std", 3)], [("prod", 0), ("hT", 2)], None)
        HOP = NodeStage("hop",
                      [("rstd", 1), ("stats", 2), ("rest", 0), ("norm", 1), ("moments", 2), ("resid", 3), ("low", 0)],
                      [("hT", 0), ("table", -2), ("mid", 0), ("relu", 1), ("std", 2), ("keep", 1)],
                      [("prod", -1), ("hT", 1)], [("clear", 3)])
        SAGE_V = [("rest", 0), ("sum", 3), ("low", 0)]
        SAGE_S = [("hT", 0), ("table", -2), ("mid", 0), ("relu", 2), ("keep", 2)]
        SAGE1 = NodeStage("sage1", SAGE_V, SAGE_S, [("prod", -1), ("hT", 1)], [("clear", 3)])
        SAGE2 = NodeStage("sage2", SAGE_V, SAGE_S, [("prod", -1), ("hT", 1)], [("clear", 3)])
        SAGE3 = NodeStage("sage3",
                       [("rstd", 1), ("stats", 2), ("sum", 3), ("moments", 2), ("norm", 1), ("resid", 3)],
                       [("std", 2), ("scaled", 1)], None, [("clear", 3)])
        CONV = NodeStage("conv",
                       [("arest", 1), ("alow", 1), ("m0", 0), ("biased", 1), ("leaky", 1), ("resid", 1), ("stats", 1),
                        ("moments", 1), ("m2", 0), ("rstd", 1), ("norm", 1), ("m4", 0), ("rest", 1), ("low", 1),
                        ("m6", 0)],
                       [("aT", 1), ("amid", 1), ("m1", 0), ("std", 1), ("relu", 1), ("agg", 2), ("m3", 0), ("hT", 1),
                        ("mid", 1), ("m5", 0), ("gate", 1), ("m7", 0)],
                       [("aT", 1), ("m0", 0), ("m1", 0), ("prod", 1), ("m2", 0), ("m3", 0), ("m4", 0), ("hT", 1),
                        ("m5", 0), ("m6", 0), ("gate", 1), ("m7", 0)], [("clear", 2)])
        out_ready, out_stored = sem("out_ready"), sem("out_stored")

        class OwnProducts:

            def __init__(self, name):
                self.v = Steps(sem(name + "_vector"), [("rest", -1), ("low", -2), ("self", -4)], 0)
                self.s = Steps(sem(name + "_scalar"), [("fetch", 0), ("hT", -2), ("mid", -3)], 0)
                self.t = Steps(sem(name + "_tensor"), [("hT", 0), ("prod", -3)], 0)
        own_products = {l: OwnProducts(f"own{l}") for l in (2, 3, 4)}

        def wide(a):
            return a[:, :].rearrange("p (o d) -> p o d", o=1)

        def rows_of(t):
            return LAST_ROWS if isinstance(t, int) and t == TILES - 1 else P

        def node_rows(a, t, n=P):
            return a[ds(t * P, n), :] if not isinstance(t, int) else a[t * P:t * P + n, :]

        TABLE_TILES = [(TILES + 1) // 2, TILES // 2]

        @block.sync
        def _(sp):
            for a, o in ((src, srcD), (dst, dstD), (edge_type, typD), (w1, w1D)):
                flat = o.rearrange("a b -> (a b)")[0:E].rearrange("(a b) -> a b", a=16)
                sp.dma_start(flat, a.rearrange("(a b) -> a b", a=16)).then_inc(copied, 16)
            sp.wait_ge(padded, 2)
            full, part_row = TAB - CHUNKS, E % P
            for o, rows in ((srcD, pad_i[:, 0, :]), (dstD, pad_i[:, 1, :]), (typD, pad_i[:, 2, :]),
                            (w1D, zeros[:, 0:P]),
                            (by_srcD.rearrange("(a b) f -> a (b f)", b=P), pad_s.rearrange("p e f -> p (e f)"))):
                w = rows.shape[1] // P
                sp.dma_start(o[CHUNKS:TAB, :], rows[0:full, :]).then_inc(copied, 16)
                sp.dma_start(o[CHUNKS - 1:CHUNKS, part_row * w:P * w], rows[0:1, part_row * w:P * w]).then_inc(copied, 16)
            sp.wait_ge(copied, 16 * 14)
            sp.wait_ge(mat_copied, 16 * 5)

            def mat_load(m, b, i):
                if not isinstance(m, int):
                    sp.wait_ge(mat_steps, 4 * m - 4)
                sp.dma_start(mat[b].rearrange("p (k d) -> p k d", k=2),
                             (matD[m:m + 1] if isinstance(m, int) else matD[ds(m, 1)]).rearrange(
                                 "o (k p) d -> p (o k) d", p=P)).then_inc(mat_in[b], 16)

            def mat_store(m):
                sp.wait_ge(mat_steps, 4 * m + 4)
                sp.dma_start((splitD[m:m + 1] if isinstance(m, int) else splitD[ds(m, 1)]).rearrange(
                    "o p s c -> (o p) s c"), mat3).then_inc(mat_out, 16)

            def split_weights():
                mat_load(0, 0, 0)
                mat_load(1, 1, 0)
                with sp.Fori(1, MATS // 2) as i:
                    for b in range(2):
                        mat_store(2 * i + b - 2)
                        mat_load(2 * i + b, b, i)
                mat_store(MATS - 2)
                mat_store(MATS - 1)

            def walk_sp(order, do):
                walk(sp, Steps(None, order), do)

            def stage_in():
                def load_x(t, i, b):
                    n = rows_of(t)
                    if not first(t):
                        sp.wait_ge(IN.v.sem, IN.v.at("norm", t - 2))
                    sp.dma_start(nx[b][0:n, :], node_rows(x, t, n)).then_inc(IN.load[b], 16)

                def put_table(t, i, b):
                    sp.wait_ge(IN.v.sem, IN.v.at("table", t))
                    sp.dma_start(node_rows(tables[0], t), nt[b][:, :]).then_inc(IN.store[b], 16)
                sp.wait_ge(consts, 1)
                walk_sp([("load", 3), ("store", -1)], dict(load=load_x, store=put_table))

            for k in range(2):
                if k == 0:
                    sp.dma_start(last_i, dstD.rearrange("(i p) e -> p i e", p=P)[:, :, P - 1],
                                 allow_slow_non_contiguous=True).then_inc(loaded, 16)
                else:
                    for h in range(2):
                        sp.wait_ge(sorted_out[h], 16 * (SORT_SLOTS // 2) * SORT_LAPS)
                    sp.wait_ge(psem("step_chunk"), 1)
                    sp.dma_start(last_f, by_srcD.rearrange("(i p e) f -> p i (e f)", p=P, e=P)[:, :, FIELDS * P - 2],
                                 allow_slow_non_contiguous=True).then_inc(loaded, 16)
                sp.wait_ge(psem("tile_i"), k + 1)
                sp.dma_start(tileD[k], tile_i).then_inc(tile_out, 16)
                sp.wait_ge(tile_out, 16 * (k + 1))
                sp.dma_start(tile_row[k][0:1, :], tileD[k].rearrange("(o a) b -> o (a b)", o=1)).then_inc(tile_in, 16)
                if k == 0:
                    split_weights()
                    stage_in()

            sp.wait_ge(added, GROUP + STEPS)
            sp.dma_start(tables[1].rearrange("(t p) d -> p t d", p=P), acc[:, :, :]).then_inc(hop_table_out, 16)

            sp.wait_ge(added, GROUP + 2 * STEPS)

            def load_x(t, i, b):
                n = rows_of(t)
                if not first(t):
                    sp.wait_ge(HOP.v.sem, HOP.v.at("resid", t - 2))
                sp.dma_start(nx[b][0:n, :], node_rows(x, t, n)).then_inc(HOP.load[b], 16)

            def put_x(t, i, b):
                sp.wait_ge(HOP.v.sem, HOP.v.at("resid", t))
                sp.dma_start(node_rows(x1D, t), ny[b][:, :]).then_inc(x1_out[b], 16)

            def put_table(t, i, b):
                sp.wait_ge(HOP.s.sem, HOP.s.at("table", t))
                sp.dma_start(node_rows(tables[2], t), nt[b][:, :]).then_inc(HOP.store[b], 16)
            walk_sp([("load", 3), ("x", 2), ("store", -2)], dict(load=load_x, x=put_x, store=put_table))

            for S, tab in ((SAGE1, tables[3]), (SAGE2, tables[4])):
                def body(t, i, b):
                    sp.wait_ge(S.s.sem, S.s.at("table", t))
                    sp.dma_start(node_rows(tab, t), nt[b][:, :]).then_inc(S.store[b], 16)
                over_tiles(sp, body)

            for b in range(2):
                sp.wait_ge(x1_out[b], 16 * TABLE_TILES[b])
            sp.wait_ge(SAGE2.v.sem, SAGE2.v.at("low", TILES - 1))

            def load_x(t, i, b):
                if not first(t):
                    sp.wait_ge(SAGE3.v.sem, SAGE3.v.at("resid", t - 2))
                sp.dma_start(nx[b][:, :], node_rows(x1D, t)).then_inc(SAGE3.load[b], 16)

            def put_table(t, i, b):
                sp.wait_ge(SAGE3.s.sem, SAGE3.s.at("scaled", t))
                sp.dma_start(node_rows(tables[5], t), nt[b][:, :]).then_inc(SAGE3.store[b], 16)
            walk_sp([("load", 3), ("store", 0)], dict(load=load_x, store=put_table))

            dest = rel_table.rearrange("(r n) d -> n r d", r=RELS)

            def body(t, i, b):
                for u in range(RELS // 2):
                    out_by = CONV.s if u % 2 else CONV.v
                    sp.wait_ge(out_by.sem, out_by.at(f"m{u}", t))
                    to = dest[t * P:(t + 1) * P] if isinstance(t, int) else dest[ds(t * P, P)]
                    sp.dma_start(to[:, 2 * u:2 * u + 2, :], msg[:, u % 4]).then_inc(msgs_out[u % 4], 16)
            over_tiles(sp, body)

            for n, t in enumerate(range(0, TILES, OUT_TILES)):
                sp.wait_ge(out_ready, n + 1)
                whole = min(OUT_TILES, N // P - t)
                sp.dma_start(out[t * P:(t + whole) * P, :].rearrange("(t p) d -> p t d", p=P),
                             keep[:, t:t + whole, :]).then_inc(out_stored, 16)
            sp.dma_start(out[(TILES - 1) * P:N, :], keep[0:LAST_ROWS, TILES - 1, :]).then_inc(out_stored, 16)
            sp.wait_ge(out_stored, 16 * (TILES // OUT_TILES + 1))

        @block.scalar
        def _(act):
            def load_weights(n, *mats):
                for slot, m in enumerate(mats):
                    act.dma_start(W[n % 2][:, :, slot].rearrange("p s k d -> p s (k d)"), splitD[m]
                                  ).then_inc(conv_weights_in if n == 4 else weights_in[n], 16)
            for l in range(3):
                act.dma_start(bias[:, l, :], L1_b[l:l + 1, :].to_broadcast([P, D])).then_inc(hist_in, 16)
            act.dma_start(bias[:, 3, :], L2_b.rearrange("(o d) -> o d", o=1).to_broadcast([P, D])).then_inc(hist_in, 16)
            act.dma_start(hop[:, 0:2], L0_hop.rearrange("(o d) -> o d", o=1).to_broadcast([P, 2])).then_inc(hist_in, 16)
            act.dma_start(hist_src, src.rearrange("(p c) -> p c", p=HIST_ROWS)).then_inc(hist_in, 16)
            act.dma_start(hist_dst, dst.rearrange("(p c) -> p c", p=HIST_ROWS)).then_inc(hist_in, 16)
            act.dma_start(hist_w, w0.rearrange("(p c) -> p c", p=HIST_ROWS)).then_inc(hist_in, 16)
            for k in range(2):
                act.dma_start(gw[:, k, :], L3_g[:, k * P:(k + 1) * P, 0].rearrange("r p -> p r"),
                              allow_slow_non_contiguous=True).then_inc(hist_in, 16)
            act.dma_start(matD[0], L0_w).then_inc(mat_copied, 16)
            act.dma_start(matD[1:7:2], L1_ws).then_inc(mat_copied, 16)
            act.dma_start(matD[2:8:2], L1_wn).then_inc(mat_copied, 16)
            act.dma_start(matD[7], L2_w).then_inc(mat_copied, 16)
            act.dma_start(matD[8:MATS], L3_w).then_inc(mat_copied, 16)
            act.wait_ge(psem("sort_start"), 1)
            def body(k):
                act.wait_ge(sort_counts, k + 1)
                if not isinstance(k, int):
                    act.wait_ge(sort_ranks, k)
                nc.scalar.copy(in_block[:, 0:COL_BLOCKS], ps_h[:, 0:COL_BLOCKS]).then_inc(sort_blocks, 1)
                act.wait_ge(sort_totals, k + 1)
                if not isinstance(k, int):
                    act.wait_ge(sort_begins, k)
                nc.scalar.activation(begin[:, ds(k + 1, 1)], ps_T[0:HIST_ROWS, 0:1], ACT.Identity,
                                     bias=begin[:, ds(k, 1)]).then_inc(sort_begins, 1)
            body(0)
            with act.Fori(1, TILES) as k:
                body(k)
            act.wait_ge(psem("deg"), 1)
            nc.scalar.activation(dinv[:, :], dinv[:, :], ACT.Sqrt).then_inc(misc_act, 1)
            act.wait_ge(psem("hop_logits"), 1)
            nc.scalar.activation(hop[:, 3:5], hop[:, 3:5], ACT.Exp).then_inc(misc_act, 1)

            def std(S):
                def do(t, i, b):
                    act.wait_ge(S.v.sem, S.v.at("moments", t))
                    nc.scalar.activation(mv[:, b, 2:3], mv[:, b, 1:2], ACT.Sqrt, bias=eps[:, :]).then_inc(S.s.sem, 1)
                return do

            def high(S):
                def do(t, i, b):
                    act.wait_ge(S.t.sem, S.t.at("hT", t))
                    if not first(t):
                        act.wait_ge(S.t.sem, S.t.at("prod", t - 2))
                    nc.scalar.copy(nhT[b][:, 0], TT[b]).then_inc(S.s.sem, 1)
                return do

            def mid(S):
                def do(t, i, b):
                    act.wait_ge(S.v.sem, S.v.at("rest", t))
                    nc.scalar.copy(nhT[b][:, 1], nr[b][:, :, :]).then_inc(S.s.sem, 1)
                return do

            def relu(S, after, source):
                def do(t, i, b):
                    act.wait_ge(S.v.sem, S.v.at(after, t))
                    if not first(t):
                        act.wait_ge(S.t.sem, S.t.at("hT", t - 2))
                    nc.scalar.activation(nh[b][:, :], source[b][:, :], ACT.Relu).then_inc(S.s.sem, 1)
                return do

            def table(S):
                def do(t, i, b):
                    act.wait_ge(S.t.sem, S.t.at("prod", t))
                    if not first(t):
                        act.wait_ge(S.store[b], 16 * i)
                    nc.scalar.copy(nt[b][:, :], ps_M[:, b, 0:D]).then_inc(S.s.sem, 1)
                return do

            def keep_h(S, after, source):
                def do(t, i, b):
                    act.wait_ge(after.sem, after.at("relu" if after is S.s else "norm" if S is IN else "sum", t))
                    nc.scalar.activation(keep[:, ds(t, 1), :], wide(source[b]), ACT.Relu).then_inc(S.s.sem, 1)
                return do

            def stage_indices(table, l):
                def pair(it, i, c):
                    for k in range(2 * c, 2 * c + 2):
                        act.wait_ge(half_sums, 2 * (l * GROUPS + LAP * i + k + 1))
                        nc.scalar.copy(stage[:, GROUP * k:GROUP * (k + 1)],
                                       table[:, ds(GROUP * LAP * i + GROUP * k, GROUP)]).then_inc(staged, 1)
                if l not in own_products:
                    walk_pairs(act, pair)
                    return
                Q = own_products[l]

                def fetch(t, i, b):
                    if not first(t):
                        act.wait_ge(Q.t.sem, Q.t.at("hT", t - 2))
                    nc.scalar.copy(wide(nh[b]), keep[:, ds(t, 1), :]).then_inc(Q.s.sem, 1)
                walk_pairs(act, pair, Q.s, dict(fetch=fetch, hT=high(Q), mid=mid(Q)), pair_first=True)

            act.wait_ge(consts, 1)
            act.wait_ge(mat_out, 16 * MATS)
            load_weights(0, 0)
            load_weights(1, 1, 2)
            walk(act, IN.s, dict(hT=high(IN), relu=relu(IN, "norm", ny), keep=keep_h(IN, IN.v, ny), mid=mid(IN),
                                 std=std(IN)))
            act.wait_ge(psem("tables"), 1)
            stage_indices(S_idx, 0)
            stage_indices(S_idx, 1)

            walk(act, HOP.s, dict(hT=high(HOP), relu=relu(HOP, "norm", nh), keep=keep_h(HOP, HOP.s, nh),
                                  mid=mid(HOP), table=table(HOP), std=std(HOP)))
            load_weights(2, 3, 4)
            act.wait_ge(HOP.s.sem, HOP.s.at("keep", TILES - 1))
            stage_indices(D_idx, 2)
            for l, S in ((3, SAGE1), (4, SAGE2)):
                if l == 3:
                    act.wait_ge(own_products[2].t.sem, own_products[2].t.at("prod", TILES - 1))
                    load_weights(3, 5, 6)
                else:
                    act.wait_ge(own_products[3].t.sem, own_products[3].t.at("prod", TILES - 1))
                    load_weights(4, 7)
                walk(act, S.s, dict(hT=high(S), relu=relu(S, "sum", ny), keep=keep_h(S, S.v, ny), mid=mid(S),
                                     table=table(S)))
                act.wait_ge(S.s.sem, S.s.at("keep", TILES - 1))
                stage_indices(D_idx, l)

            def scaled(t, i, b):
                act.wait_ge(SAGE3.v.sem, SAGE3.v.at("norm", t))
                if not first(t):
                    act.wait_ge(SAGE3.store[b], 16 * i)
                nc.scalar.activation(nt[b][:, :], nh[b][:, :], ACT.Relu, scale=dinv[:, ds(t, 1)]).then_inc(SAGE3.s.sem, 1)
            walk(act, SAGE3.s, dict(scaled=scaled, std=std(SAGE3)))
            stage_indices(S_idx, 5)

            act.wait_ge(half_sums, 2 * (LAP + 6 * GROUPS))
            act.wait_ge(added, GROUP + 6 * STEPS)
            for group_in, lo, hi in ((weights_in[4], 0, 2), (rel_weights_in, 2, RELS)):
                for part_n in range(3):
                    act.dma_start(W3[part_n][:, lo:hi].rearrange("p r k d -> p r (k d)"),
                                  splitD[8 + lo:8 + hi, :, part_n, :].rearrange("r p c -> p r c")
                                  ).then_inc(group_in, 16)

            def agg(t, i, b):
                if not first(t):
                    act.wait_ge(CONV.t.sem, CONV.t.at("hT", t - 2))
                nc.scalar.activation(wide(nh[b]), acc[:, ds(t, 1), :], ACT.Copy, scale=dinv[:, ds(t, 1)]
                                     ).then_inc(CONV.s.sem, 1)

            def agg_high(t, i, b):
                act.wait_ge(CONV.t.sem, CONV.t.at("aT", t))
                nc.scalar.copy(naT[:, 0], TT[0]).then_inc(CONV.s.sem, 1)

            def agg_mid(t, i, b):
                act.wait_ge(CONV.v.sem, CONV.v.at("arest", t))
                nc.scalar.copy(naT[:, 1], nr[0][:, :, :]).then_inc(CONV.s.sem, 1)

            def relu_h(t, i, b):
                act.wait_ge(CONV.v.sem, CONV.v.at("norm", t))
                nc.scalar.activation(nh[b][:, :], nh[b][:, :], ACT.Relu).then_inc(CONV.s.sem, 1)

            def h_high(t, i, b):
                act.wait_ge(CONV.t.sem, CONV.t.at("hT", t))
                nc.scalar.copy(nhT[b][:, 0], TT[1]).then_inc(CONV.s.sem, 1)

            def h_mid(t, i, b):
                act.wait_ge(CONV.v.sem, CONV.v.at("rest", t))
                nc.scalar.copy(nhT[b][:, 1], nr[1][:, :, :]).then_inc(CONV.s.sem, 1)

            def gates(t, i, b):
                act.wait_ge(CONV.t.sem, CONV.t.at("gate", t))
                nc.scalar.activation(gate[:, b, :], ps_M[:, 1, 0:RELS], ACT.Sigmoid).then_inc(CONV.s.sem, 1)

            def messages(u):
                def do(t, i, b):
                    act.wait_ge(CONV.s.sem, CONV.s.at("gate", t))
                    act.wait_ge(CONV.t.sem, CONV.t.at(f"m{u}", t))
                    if not (isinstance(t, int) and 2 * t + u // 4 < 1):
                        act.wait_ge(msgs_out[u % 4], 16 * (2 * t + u // 4))
                    nc.scalar.activation(msg[:, u % 4, 0, :], ps_sum[:, 2 * (u % 4), :], ACT.Copy,
                                         scale=gate[:, b, 2 * u:2 * u + 1])
                    nc.scalar.activation(msg[:, u % 4, 1, :], ps_sum[:, 2 * (u % 4) + 1, :], ACT.Copy,
                                         scale=gate[:, b, 2 * u + 1:2 * u + 2]).then_inc(CONV.s.sem, 1)
                return do
            walk(act, CONV.s, dict(agg=agg, aT=agg_high, amid=agg_mid, std=std(CONV), relu=relu_h, hT=h_high, mid=h_mid,
                                 gate=gates, m1=messages(1), m3=messages(3), m5=messages(5), m7=messages(7)))
            stage_indices(D_rel, 6)

        @block.gpsimd
        def _(pool):
            nc.gpsimd.memset(zeros[:, :], 0.0).then_inc(padded, 1)
            nc.gpsimd.iota(iota[:, :], pattern=[[1, P]], base=0, channel_multiplier=0,
                           allow_small_or_imprecise_dtypes=True).then_inc(psem("iota"), 1)
            nc.gpsimd.iota(thr, pattern=[[P, TILES - 1]], base=P, channel_multiplier=0,
                           allow_small_or_imprecise_dtypes=True).then_inc(psem("iota"), 1)
            nc.gpsimd.iota(tnum, pattern=[[1, TILES - 1]], base=1, channel_multiplier=0,
                           allow_small_or_imprecise_dtypes=True).then_inc(psem("iota"), 1)
            nc.gpsimd.iota(snum, pattern=[[P, STEP_TILES]], base=0, channel_multiplier=1,
                           allow_small_or_imprecise_dtypes=True).then_inc(psem("iota"), 1)
            nc.gpsimd.iota(part[:, :], pattern=[[0, 1]], base=0, channel_multiplier=1,
                           allow_small_or_imprecise_dtypes=True).then_inc(psem("iota"), 1)
            nc.gpsimd.iota(columns, pattern=[[1, HIST_COLS]], base=0, channel_multiplier=0,
                           allow_small_or_imprecise_dtypes=True).then_inc(psem("iota"), 1)
            nc.gpsimd.memset(ones[:, :], 1.0).then_inc(psem("ones"), 1)
            pool.wait_ge(psem("ones"), 1)
            nc.gpsimd.affine_select(out=ident[:, :], in_=ones[:, :], compare_op=ALU.is_equal, fill=0.0, base=0,
                                    pattern=[[-1, P]], channel_multiplier=1).then_inc(psem("iota"), 1)
            pool.wait_ge(copied, 16 * 14)
            pool.wait_ge(psem("step_chunk"), 1)
            for i in range(STEP_TILES):
                for to, table in ((raw_i[:, 0, i, :], srcD), (raw_i[:, 1, i, :], dstD), (raw_i[:, 2, i, :], typD),
                                  (raw_f[:, 3, i, :], w1D)):
                    nc.gpsimd.indirect_dma_start(
                        out=to, out_offset=None, in_=table,
                        in_offset=bass.IndirectOffsetOnAxis(ap=step_chunk[:, i:i + 1], axis=0)).then_inc(gath, 16)
            def body(i):
                for h in range(2):
                    if not isinstance(i, int):
                        pool.wait_ge(sorted_out[h], 16 * (SORT_SLOTS // 2) * i)
                    n, at = SORT_SLOTS // 2, SORT_SLOTS * i + SORT_SLOTS // 2 * h
                    nc.gpsimd.tensor_copy(stage[0:HIST_ROWS, n * h:n * (h + 1)], rank_i[:, ds(at, n)]
                                          ).then_inc(sort_staged, 1)
                    nc.gpsimd.tensor_copy(rec_stage[:, n * h:n * (h + 1), :], record[:, ds(at, n), :]
                                          ).then_inc(sort_staged, 1)
                    pool.wait_ge(sort_staged, 4 * i + 2 * h + 2)
                    pool.sem_inc(passed, 1)
                    for j in range(h * SORT_SLOTS // 2, (h + 1) * SORT_SLOTS // 2):
                        nc.gpsimd.indirect_dma_start(
                            out=by_srcD, out_offset=bass.IndirectOffsetOnAxis(ap=stage[0:HIST_ROWS, j:j + 1], axis=0),
                            in_=rec_stage[:, j, :], in_offset=None).then_inc(sorted_out[h], 16)
            pool.wait_ge(psem("records"), 1)
            body(0)
            with pool.Fori(1, SORT_LAPS) as i:
                body(i)
            for h in range(2):
                pool.wait_ge(sorted_out[h], 16 * (SORT_SLOTS // 2) * SORT_LAPS)
            pool.wait_ge(psem("step_chunk"), 2)
            for i in range(STEP_TILES):
                nc.gpsimd.indirect_dma_start(
                    out=raw_s[:, i, :, :].rearrange("p e f -> p (e f)"), out_offset=None,
                    in_=by_srcD.rearrange("(a b) f -> a (b f)", b=P),
                    in_offset=bass.IndirectOffsetOnAxis(ap=step_chunk[:, i:i + 1], axis=0)).then_inc(gath, 16)

            def gathers(table, l, ready):
                for s, v in ready:
                    pool.wait_ge(s, v)
                with pool.Fori(0, LAPS) as i:
                    for k in range(LAP):
                        pool.wait_ge(staged, l * GROUPS + LAP * i + k + 1)
                        pool.sem_inc(passed, 1)
                        for j in range(GROUP):
                            slot = GROUP * k + j
                            nc.gpsimd.indirect_dma_start(
                                out=ring[:, slot, :], out_offset=None, in_=table,
                                in_offset=bass.IndirectOffsetOnAxis(ap=stage[:, slot:slot + 1], axis=0)
                            ).then_inc(gathered[k], 16)

            def stored(S, n=1):
                return [(S.store[b], 16 * n * TABLE_TILES[b]) for b in range(2)]

            def clear(S, by, step):
                def do(t, i, b):
                    pool.wait_ge(by.sem, by.at(step, t))
                    nc.gpsimd.tensor_copy(acc[:, ds(t, 1), :], wide(zeros)).then_inc(S.p.sem, 1)
                walk(pool, S.p, dict(clear=do))

            gathers(tables[0], 0, stored(IN))
            gathers(tables[1], 1, [(hop_table_out, 16)])
            clear(HOP, HOP.v, "resid")
            gathers(tables[2], 2, stored(HOP))
            clear(SAGE1, SAGE1.v, "sum")
            gathers(tables[3], 3, stored(SAGE1))
            clear(SAGE2, SAGE2.v, "sum")
            gathers(tables[4], 4, stored(SAGE2))
            clear(SAGE3, SAGE3.v, "sum")
            gathers(tables[5], 5, stored(SAGE3))
            clear(CONV, CONV.s, "agg")
            gathers(rel_table, 6, [(q, 16 * 2 * TILES) for q in msgs_out])

        @block.vector
        def _(dve):
            n = [0]

            def step(ins):
                n[0] += 1
                ins.then_inc(prep_dve, 1)
                dve.wait_ge(prep_dve, n[0])

            step(nc.vector.memset(pad_i[:, 0, :], N))
            step(nc.vector.memset(pad_i[:, 1, :], NO_NODE))
            step(nc.vector.memset(pad_i[:, 2, :], 0))
            step(nc.vector.memset(pad_s[:, :, 0], float(N)))
            step(nc.vector.memset(pad_s[:, :, 1], float(NO_NODE)))
            step(nc.vector.memset(pad_s[:, :, 2], 0.0))
            dve.sem_inc(padded, 1)
            step(nc.vector.memset(eps[:, :], LN_EPS))
            step(nc.vector.memset(ones_b[:, :], 1.0))
            step(nc.vector.memset(nx[0][:, :], 0.0))
            step(nc.vector.memset(rank, 0.0))
            step(nc.vector.memset(begin, 0.0))
            for b in range(2):
                step(nc.vector.memset(masks[b], 0.0))
            dve.wait_ge(psem("iota"), 7)
            step(nc.vector.tensor_scalar(before, columns, part[:, 0:1], None, ALU.is_gt))
            m = [0]

            def small(ins):
                m[0] += 1
                ins.then_inc(misc_dve, 1)
                dve.wait_ge(misc_dve, m[0])

            def split(nodes):
                for half, op, by in ((hist_hi, ALU.logical_shift_right, 7), (hist_lo, ALU.bitwise_and, P - 1)):
                    small(nc.vector.tensor_scalar(half.bitcast(I32), nodes, by, None, op))
                    small(nc.vector.tensor_copy(half, half.bitcast(I32)))
            dve.wait_ge(hist_in, 16 * 10)
            split(hist_src)

            def find_steps(k):
                dve.wait_ge(loaded, 16 * (k + 1))
                if k == 0:
                    step(nc.vector.tensor_copy(last_f, last_i))
                step(nc.vector.memset(cnt, 0.0))
                for i in range(STEP_TILES):
                    step(nc.vector.scalar_tensor_tensor(cnt, thr, last_f[:, i:i + 1], cnt, ALU.is_gt, ALU.add))
                dve.sem_inc(psem("cnt"), 1)
                dve.wait_ge(prep_pe, (STEP_TILES + 2) * k + 1)
                step(nc.vector.tensor_tensor(first_step, ps_h[:, 0:TILES - 1], tnum, ALU.add))
                for i in range(STEP_TILES):
                    step(nc.vector.tensor_scalar(cmp[:, i, :], first_step, snum[:, i:i + 1], None, ALU.is_le))
                step(nc.vector.tensor_reduce(step_tile, cmp, AX.X, ALU.add))
                step(nc.vector.tensor_tensor(step_chunk, snum, step_tile, ALU.subtract))
                step(nc.vector.tensor_scalar(step_base, step_tile, float(P), None, ALU.mult))
                dve.sem_inc(psem("step_chunk"), 1)
                dve.wait_ge(prep_pe, (STEP_TILES + 2) * k + 2)
                if k:
                    dve.wait_ge(tile_out, 16)
                nc.vector.tensor_copy(tile_i, ps_h[0:STEP_TILES, 128:128 + P]).then_inc(psem("tile_i"), 1)

            def turned(k, tables):
                for i in range(STEP_TILES):
                    dve.wait_ge(prep_pe, (STEP_TILES + 2) * k + 3 + i)
                    for q, table in enumerate(tables):
                        ins = nc.vector.tensor_copy(table[:, i * P:(i + 1) * P], ps_M[:, i % 2, q * P:(q + 1) * P])
                    ins.then_inc(psem("turned"), 1)
            def mask(k, b):
                nc.vector.tensor_scalar(masks[b][:, 0:HIST_COLS], hist_hi, iota[0:HIST_ROWS, ds(k, 1)],
                                        None, ALU.is_equal).then_inc(sort_masks, 1)

            def pick(k, b, more=True):
                dve.wait_ge(sort_ranks, k + 1)
                dve.wait_ge(sort_masks, k + 1)
                if not (isinstance(k, int) and k < 1):
                    dve.wait_ge(sort_begins, k)
                    dve.wait_ge(sort_picks, 2 * k)
                ranks = ps_sum[0:HIST_ROWS, 4 * b:4 * b + 4, :].rearrange("p a b -> p (a b)")[:, 0:HIST_COLS]
                nc.vector.scalar_tensor_tensor(picked, ranks, begin[:, ds(k, 1)], masks[b][:, 0:HIST_COLS], ALU.add,
                                               ALU.mult).then_inc(sort_picks, 1)
                dve.wait_ge(sort_picks, 2 * k + 1)
                if more:
                    mask(k + 2, b)
                nc.vector.tensor_tensor(rank, rank, picked, ALU.add).then_inc(sort_picks, 1)
            dve.sem_inc(psem("sort_start"), 1)
            mask(0, 0)
            mask(1, 1)
            for k in range(EARLY_RANKS):
                pick(k, k % 2)
            find_steps(0)
            with dve.Fori(EARLY_RANKS // 2, (TILES - 1) // 2 - 1) as i:
                pick(2 * i, 0)
                pick(2 * i + 1, 1)
            for k in range(TILES - 3, TILES):
                pick(k, k % 2, more=k < TILES - 2)
            dve.wait_ge(sort_picks, 2 * TILES)
            small(nc.vector.tensor_copy(rank_i, rank))
            small(nc.vector.tensor_copy(record[:, :, 0], hist_dst))
            small(nc.vector.tensor_copy(record[:, :, 1], hist_src))
            small(nc.vector.tensor_copy(record[:, :, 2], hist_w))
            dve.sem_inc(psem("records"), 1)

            def hots_of_columns(v):
                def body(i):
                    for b in range(2):
                        g = 2 * i + b
                        if not isinstance(i, int):
                            dve.wait_ge(hist_used, v * (HIST_COLS // GROUP) + g - 1)
                        for hot, digits, n in ((lo_hot, hist_lo, P), (hi_hot, hist_hi, TILES)):
                            nc.vector.tensor_tensor(
                                hot[:, b], iota[0:HIST_ROWS, 0:n].rearrange("p (o e) -> p o e", o=1).to_broadcast(
                                    [HIST_ROWS, GROUP, n]),
                                digits[:, ds(GROUP * g, GROUP)].rearrange("p (j o) -> p j o", o=1).to_broadcast(
                                    [HIST_ROWS, GROUP, n]), ALU.is_equal).then_inc(hist_hots, 1)
                body(0)
                with dve.Fori(1, HIST_COLS // GROUP // 2) as i:
                    body(i)
                dve.wait_ge(hist_used, (v + 1) * (HIST_COLS // GROUP))
            hots_of_columns(0)
            small(nc.vector.tensor_copy(deg_src[:, :], ps_T[:, 0:TILES]))
            split(hist_dst)
            dve.sem_inc(psem("hist_second"), 1)
            hots_of_columns(1)
            small(nc.vector.tensor_copy(dtmp[:, :], ps_T[:, 0:TILES]))
            small(nc.vector.tensor_scalar(inv_deg[:, :], dtmp[:, :], 1.0, None, ALU.max))
            small(nc.vector.reciprocal(inv_deg[:, :], inv_deg[:, :]))
            small(nc.vector.scalar_tensor_tensor(inv_deg[:, :], dtmp[:, :], 0.5, inv_deg[:, :], ALU.is_gt, ALU.mult))
            small(nc.vector.tensor_scalar(dinv[:, :], deg_src[:, :], 1.0, None, ALU.max))
            dve.sem_inc(psem("deg"), 1)

            def parts(x, rest, to, done):
                for n, make in enumerate((lambda: nc.vector.tensor_copy(to[0], x),
                                          lambda: nc.vector.tensor_tensor(rest, x, to[0], ALU.subtract),
                                          lambda: nc.vector.tensor_copy(to[1], rest),
                                          lambda: nc.vector.tensor_tensor(to[2], rest, to[1], ALU.subtract))):
                    done(n, make())

            def split_mat(m, i, b):
                dve.wait_ge(mat_in[b], 16 * i + 16)
                if not (isinstance(m, int) and m < 1):
                    dve.wait_ge(mat_out, 16 * m)

                def done(n, ins):
                    ins.then_inc(mat_steps, 1)
                    dve.wait_ge(mat_steps, 4 * m + n + 1)
                parts(mat[b], mat_rest, [mat3[:, q, :] for q in range(3)], done)
            split_mat(0, 0, 0)
            split_mat(1, 0, 1)
            with dve.Fori(1, MATS // 2) as i:
                split_mat(2 * i, i, 0)
                split_mat(2 * i + 1, i, 1)
            parts(gw[:, :, :], gate_rest, [gw3[:, q] for q in range(3)], lambda n, ins: small(ins))

            dve.wait_ge(gath, 16 * 4 * STEP_TILES)
            for i in range(STEP_TILES):
                step(nc.vector.tensor_copy(raw_f[:, 0, i, :], raw_i[:, 0, i, :]))
                step(nc.vector.tensor_scalar(raw_f[:, 1, i, :], raw_i[:, 1, i, :], step_base[:, i:i + 1], None,
                                             ALU.subtract))
                step(nc.vector.scalar_tensor_tensor(raw_f[:, 2, i, :], raw_i[:, 2, i, :], float(NP),
                                                    raw_f[:, 0, i, :], ALU.mult, ALU.add))
            dve.sem_inc(psem("step_rows"), 1)
            turned(0, (D_idx, D_key, D_rel, D_w))
            small(nc.vector.tensor_tensor(hop[:, 2:3], hop[:, 0:1], hop[:, 1:2], ALU.max))
            small(nc.vector.tensor_scalar(hop[:, 3:5], hop[:, 0:2], hop[:, 2:3], None, ALU.subtract))
            dve.sem_inc(psem("hop_logits"), 1)
            dve.wait_ge(misc_act, 2)
            small(nc.vector.reciprocal(dinv[:, :], dinv[:, :]))
            small(nc.vector.scalar_tensor_tensor(dinv[:, :], deg_src[:, :], 0.5, dinv[:, :], ALU.is_gt, ALU.mult))
            small(nc.vector.tensor_tensor(hop[:, 5:6], hop[:, 3:4], hop[:, 4:5], ALU.add))
            small(nc.vector.reciprocal(hop[:, 5:6], hop[:, 5:6]))
            small(nc.vector.tensor_scalar(hop[:, 3:5], hop[:, 3:5], hop[:, 5:6], None, ALU.mult))

            dve.sem_inc(consts, 1)

            def tile(a, t):
                return a[:, ds(t, 1), :]

            def stats(S, source):
                def do(t, i, b):
                    if not first(t):
                        dve.wait_ge(S.v.sem, S.v.at("norm", t - 2))
                    if "resid" in S.v.names:
                        dve.wait_ge(S.v.sem, S.v.at("resid", t))
                    else:
                        dve.wait_ge(S.load[b], 16 * i + 16)
                    dve.sem_inc(passed, 1)
                    nc.vector.bn_stats(st6[:, b, :], source(t, b)).then_inc(S.v.sem, 1)
                return do

            def moments(S):
                def do(t, i, b):
                    dve.wait_ge(S.v.sem, S.v.at("stats", t))
                    dve.sem_inc(passed, 1)
                    nc.vector.bn_aggr(mv[:, b, 0:2], st6[:, b, :]).then_inc(S.v.sem, 1)
                return do

            def rstd(S):
                def do(t, i, b):
                    dve.wait_ge(S.s.sem, S.s.at("std", t))
                    nc.vector.reciprocal(mv[:, b, 3:4], mv[:, b, 2:3]).then_inc(S.v.sem, 1)
                return do

            def norm(S, source, to, free):
                def do(t, i, b):
                    dve.wait_ge(S.v.sem, S.v.at("rstd", t))
                    for steps, name in free:
                        if not first(t):
                            dve.wait_ge(steps.sem, steps.at(name, t - 2))
                    nc.vector.tensor_scalar(to(b), source(t, b), mv[:, b, 0:1], mv[:, b, 3:4], ALU.subtract,
                                            ALU.mult).then_inc(S.v.sem, 1)
                return do

            def rest(S):
                def do(t, i, b):
                    dve.wait_ge(S.s.sem, S.s.at("hT", t))
                    nc.vector.tensor_tensor(nr[b][:, :, :], TT[b], nhT[b][:, 0], ALU.subtract).then_inc(S.v.sem, 1)
                return do

            def low(S):
                def do(t, i, b):
                    dve.wait_ge(S.s.sem, S.s.at("mid", t))
                    nc.vector.tensor_tensor(nhT[b][:, 2], nr[b][:, :, :], nhT[b][:, 1], ALU.subtract
                                            ).then_inc(S.v.sem, 1)
                return do

            def own(S, l):
                def do(t, i, b):
                    dve.wait_ge(S.t.sem, S.t.at("prod", t))
                    nc.vector.tensor_tensor(tile(keep, t), ps_M[:, b:b + 1, 0:D], bias[:, l:l + 1, :], ALU.add
                                            ).then_inc(S.v.sem, 1)
                return do

            def table(t, i, b):
                dve.wait_ge(IN.t.sem, IN.t.at("prod", t))
                if not first(t):
                    dve.wait_ge(IN.store[b], 16 * i)
                nc.vector.tensor_copy(nt[b][:, :], ps_M[:, b, 0:D]).then_inc(IN.v.sem, 1)
            walk(dve, IN.v, dict(stats=stats(IN, lambda t, b: nx[b][:, :]), moments=moments(IN), rstd=rstd(IN),
                                norm=norm(IN, lambda t, b: nx[b][:, :], lambda b: ny[b][:, :], [(IN.s, "keep")]),
                                rest=rest(IN), low=low(IN), table=table))
            find_steps(1)
            dve.wait_ge(gath, 16 * 5 * STEP_TILES)
            for i in range(STEP_TILES):
                step(nc.vector.tensor_scalar(raw_k[:, i, :], raw_s[:, i, :, 1], step_base[:, i:i + 1], None,
                                             ALU.subtract))
            dve.sem_inc(psem("step_rows"), 1)
            turned(1, (S_idx, S_key, S_w))
            dve.wait_ge(psem("turned"), 2 * STEP_TILES)
            dve.sem_inc(psem("tables"), 1)
            dve.wait_ge(tile_in, 32)
            nc.vector.memset(acc_row, 0.0).then_inc(acc_ready, 1)
            dve.sem_inc(added, GROUP)
            dve.wait_ge(acc_ready, 1)

            tiles_r = [dve.alloc_register(f"step_tile{j}") for j in range(GROUP)]

            def sums(l, key, weight, into=acc):
                row = tile_row[1 if key is S_key else 0]

                def hot(g, k, used):
                    dve.wait_ge(half_sums, 2 * used)
                    for j in range(GROUP):
                        o, s = onehot[:, GROUP * k + j, :], GROUP * g + j
                        if weight is None:
                            ins = nc.vector.tensor_scalar(o, iota[:, :], key[:, ds(s, 1)], None, ALU.is_equal)
                        else:
                            ins = nc.vector.tensor_scalar(o, iota[:, :], key[:, ds(s, 1)], weight[:, ds(s, 1)],
                                                          ALU.is_equal, ALU.mult)
                        ins.then_inc(hots, 1)

                def group(g, k, last):
                    if not last:
                        hot(g + 1, 1 - k, LAP + l * GROUPS + g)
                    dve.load(tiles_r, row[0:1, ds(GROUP * g, GROUP)])
                    for h in range(2):
                        dve.wait_ge(half_sums, 2 * (LAP + l * GROUPS + g) + h + 1)
                        for j in range(h * HALF, (h + 1) * HALF):
                            t = dve.snap(tiles_r[j], min_val=0, max_val=TILES - 1)
                            dve.wait_ge(added, GROUP + l * STEPS + GROUP * g + j)
                            a = tile(into, t)
                            nc.vector.tensor_tensor(a, a, ps_sum[:, j:j + 1, :], ALU.add).then_inc(added, 1)
                def pair(it, i, c):
                    group(2 * it, 0, False)
                    group(2 * it + 1, 1, isinstance(it, int) and it == GROUPS // 2 - 1)
                hot(0, 0, LAP + l * GROUPS)
                if l in own_products:
                    Q = own_products[l]
                    walk_pairs(dve, pair, Q.v, dict(rest=rest(Q), low=low(Q), self=own(Q, l - 2)))
                else:
                    walk_pairs(dve, pair)

            sums(0, S_key, S_w)
            dve.wait_ge(added, GROUP + STEPS)
            dve.wait_ge(IN.s.sem, IN.s.at("keep", TILES - 1))
            small(nc.vector.scalar_tensor_tensor(keep_row, acc_row, hop[:, 3:4], keep_row, ALU.mult, ALU.add))
            small(nc.vector.tensor_scalar(S_w, S_w, hop[:, 4:5], None, ALU.mult))
            sums(1, S_key, S_w, keep)
            dve.wait_ge(added, GROUP + 2 * STEPS)

            def resid(t, i, b):
                if not first(t):
                    dve.wait_ge(x1_out[b], 16 * i)
                    dve.wait_ge(HOP.v.sem, HOP.v.at("norm", t - 2))
                dve.wait_ge(HOP.load[b], 16 * i + 16)
                nc.vector.scalar_tensor_tensor(wide(ny[b]), tile(keep, t), 0.0, wide(nx[b]), ALU.max, ALU.add
                                               ).then_inc(HOP.v.sem, 1)
            walk(dve, HOP.v, dict(resid=resid, stats=stats(HOP, lambda t, b: ny[b][:, :]), moments=moments(HOP),
                                rstd=rstd(HOP), norm=norm(HOP, lambda t, b: ny[b][:, :], lambda b: nh[b][:, :],
                                                      [(HOP.t, "hT"), (HOP.s, "keep")]),
                                rest=rest(HOP), low=low(HOP)))
            dve.wait_ge(HOP.p.sem, HOP.p.at("clear", TILES - 1))
            sums(2, D_key, None)

            for l, S in ((3, SAGE1), (4, SAGE2)):
                dve.wait_ge(added, GROUP + l * STEPS)
                Q = own_products[l - 1]
                dve.wait_ge(Q.v.sem, Q.v.at("self", TILES - 1))

                def total(t, i, b):
                    if not first(t):
                        dve.wait_ge(S.s.sem, S.s.at("keep", t - 2))
                    nc.vector.scalar_tensor_tensor(wide(ny[b]), tile(acc, t), inv_deg[:, ds(t, 1)], tile(keep, t),
                                                   ALU.mult, ALU.add).then_inc(S.v.sem, 1)
                walk(dve, S.v, dict(sum=total, rest=rest(S), low=low(S)))
                dve.wait_ge(S.p.sem, S.p.at("clear", TILES - 1))
                sums(l, D_key, None)

            dve.wait_ge(added, GROUP + 5 * STEPS)
            dve.wait_ge(own_products[4].v.sem, own_products[4].v.at("self", TILES - 1))

            def total(t, i, b):
                if not first(t):
                    dve.wait_ge(SAGE3.v.sem, SAGE3.v.at("resid", t - 2))
                nc.vector.scalar_tensor_tensor(wide(ny[b]), tile(acc, t), inv_deg[:, ds(t, 1)], tile(keep, t),
                                               ALU.mult, ALU.add).then_inc(SAGE3.v.sem, 1)

            def resid(t, i, b):
                dve.wait_ge(SAGE3.v.sem, SAGE3.v.at("sum", t))
                dve.wait_ge(SAGE3.load[b], 16 * i + 16)
                nc.vector.tensor_tensor(tile(keep, t), wide(ny[b]), wide(nx[b]), ALU.add).then_inc(SAGE3.v.sem, 1)

            def kept(t, b):
                return keep[:, ds(t, 1), :].rearrange("p o d -> p (o d)")
            walk(dve, SAGE3.v, dict(sum=total, resid=resid, stats=stats(SAGE3, kept), moments=moments(SAGE3),
                                    rstd=rstd(SAGE3),
                                 norm=norm(SAGE3, kept, lambda b: nh[b][:, :], [(SAGE3.s, "scaled")])))
            dve.wait_ge(SAGE3.p.sem, SAGE3.p.at("clear", TILES - 1))
            sums(5, S_key, None)

            def agg_rest(t, i, b):
                dve.wait_ge(CONV.s.sem, CONV.s.at("aT", t))
                nc.vector.tensor_tensor(nr[0][:, :, :], TT[0], naT[:, 0], ALU.subtract).then_inc(CONV.v.sem, 1)

            def agg_low(t, i, b):
                dve.wait_ge(CONV.s.sem, CONV.s.at("amid", t))
                nc.vector.tensor_tensor(naT[:, 2], nr[0][:, :, :], naT[:, 1], ALU.subtract).then_inc(CONV.v.sem, 1)

            def biased(t, i, b):
                dve.wait_ge(CONV.t.sem, CONV.t.at("prod", t))
                nc.vector.tensor_tensor(nx[b][:, :], ps_M[:, 0, 0:D], bias[:, 3, :], ALU.add).then_inc(CONV.v.sem, 1)

            def leaky(t, i, b):
                dve.wait_ge(CONV.v.sem, CONV.v.at("biased", t))
                nc.vector.scalar_tensor_tensor(nx[b][:, :], nx[b][:, :], LEAK, nx[b][:, :], ALU.mult, ALU.max
                                               ).then_inc(CONV.v.sem, 1)

            def resid(t, i, b):
                dve.wait_ge(CONV.v.sem, CONV.v.at("leaky", t))
                nc.vector.tensor_tensor(tile(keep, t), wide(nx[b]), tile(keep, t), ALU.add).then_inc(CONV.v.sem, 1)

            def h_rest(t, i, b):
                dve.wait_ge(CONV.s.sem, CONV.s.at("hT", t))
                nc.vector.tensor_tensor(nr[1][:, :, :], TT[1], nhT[b][:, 0], ALU.subtract).then_inc(CONV.v.sem, 1)

            def h_low(t, i, b):
                dve.wait_ge(CONV.s.sem, CONV.s.at("mid", t))
                nc.vector.tensor_tensor(nhT[b][:, 2], nr[1][:, :, :], nhT[b][:, 1], ALU.subtract
                                        ).then_inc(CONV.v.sem, 1)

            def messages(u):
                def do(t, i, b):
                    dve.wait_ge(CONV.s.sem, CONV.s.at("gate", t))
                    dve.wait_ge(CONV.t.sem, CONV.t.at(f"m{u}", t))
                    if not (isinstance(t, int) and 2 * t + u // 4 < 1):
                        dve.wait_ge(msgs_out[u % 4], 16 * (2 * t + u // 4))
                    nc.vector.tensor_scalar(msg[:, u % 4, 0, :], ps_sum[:, 2 * (u % 4), :], gate[:, b, 2 * u:2 * u + 1],
                                            None, ALU.mult)
                    nc.vector.tensor_scalar(msg[:, u % 4, 1, :], ps_sum[:, 2 * (u % 4) + 1, :],
                                            gate[:, b, 2 * u + 1:2 * u + 2], None, ALU.mult).then_inc(CONV.v.sem, 1)
                return do
            walk(dve, CONV.v, dict(arest=agg_rest, alow=agg_low, biased=biased, leaky=leaky, resid=resid,
                                 stats=stats(CONV, kept), moments=moments(CONV), rstd=rstd(CONV),
                                 norm=norm(CONV, kept, lambda b: nh[b][:, :], [(CONV.t, "hT")]), rest=h_rest, low=h_low,
                                 m0=messages(0), m2=messages(2), m4=messages(4), m6=messages(6)))
            dve.wait_ge(CONV.p.sem, CONV.p.at("clear", TILES - 1))
            for q in msgs_out:
                dve.wait_ge(q, 16 * 2 * TILES)
            sums(6, D_key, D_w)

            dve.wait_ge(added, GROUP + 7 * STEPS)
            for t in range(0, TILES, OUT_TILES):
                nc.vector.scalar_tensor_tensor(keep[:, t:t + OUT_TILES, :], acc[:, t:t + OUT_TILES, :], 0.0,
                                               keep[:, t:t + OUT_TILES, :], ALU.max, ALU.add).then_inc(out_ready, 1)

        @block.tensor
        def _(pe):
            def find_steps(k):
                pe.wait_ge(psem("cnt"), k + 1)
                nc.tensor.matmul(ps_h[:, 0:TILES - 1], ones[:, :], cnt, start=True, stop=True).then_inc(prep_pe, 1)
                pe.wait_ge(psem("step_chunk"), k + 1)
                nc.tensor.transpose(ps_h[0:STEP_TILES, P:2 * P], step_tile, ident[:, :]).then_inc(prep_pe, 1)

            def turn_rows(k, fields):
                pe.wait_ge(psem("step_rows"), k + 1)
                for i in range(STEP_TILES):
                    if i + k >= 2:
                        pe.wait_ge(psem("turned"), STEP_TILES * k + i - 1)
                    for q, field in enumerate(fields):
                        ins = nc.tensor.transpose(ps_M[:, i % 2, q * P:(q + 1) * P], field(i), ident[:, :])
                    ins.then_inc(prep_pe, 1)
            pe.wait_ge(psem("iota"), 7)

            def body(k, b, first):
                pe.wait_ge(sort_masks, k + 1)
                if not first:
                    pe.wait_ge(sort_blocks, k)
                for i in range(COL_BLOCKS):
                    ins = nc.tensor.matmul(ps_h[:, i:i + 1], masks[b][:, i * P:(i + 1) * P], ones_b[0:HIST_ROWS, :],
                                           start=True, stop=True)
                ins.then_inc(sort_counts, 1)
                if not (isinstance(k, int) and k < 2):
                    pe.wait_ge(sort_picks, 2 * (k - 1))
                to = ps_sum[0:HIST_ROWS, 4 * b:4 * b + 4, :].rearrange("p a b -> p (a b)")
                parts = [(0, 512), (512, HIST_COLS)]
                for lo, hi in parts:
                    nc.tensor.matmul(to[:, lo:hi], before[0:HIST_ROWS, 0:HIST_ROWS], masks[b][:, lo:hi], start=True,
                                     stop=False)
                pe.wait_ge(sort_blocks, k + 1)
                for i in reversed(range(COL_BLOCKS)):
                    block_counts = in_block[:, i:i + 1].to_broadcast([P, HIST_ROWS])
                    for lo, hi in parts:
                        a = max(lo, i * P)
                        if a < hi:
                            ins = nc.tensor.matmul(to[:, a:hi], block_counts, before[:, a - i * P:hi - i * P],
                                                   start=False, stop=(i == 0))
                ins.then_inc(sort_ranks, 1)
                if not first:
                    pe.wait_ge(sort_begins, k)
                for i in range(COL_BLOCKS):
                    ins = nc.tensor.matmul(ps_T[0:HIST_ROWS, 0:1], in_block[:, i:i + 1].to_broadcast([P, HIST_ROWS]),
                                           ones_b[:, :], start=(i == 0), stop=(i == COL_BLOCKS - 1))
                ins.then_inc(sort_totals, 1)
            pe.wait_ge(psem("sort_start"), 1)
            for k in range(EARLY_RANKS):
                body(k, k % 2, k == 0)
            pe.wait_ge(sort_blocks, EARLY_RANKS)
            find_steps(0)
            pe.wait_ge(psem("tile_i"), 1)
            with pe.Fori(EARLY_RANKS // 2, TILES // 2) as i:
                body(2 * i, 0, False)
                body(2 * i + 1, 1, False)
            body(TILES - 1, 0, False)

            def turn(S, after="relu"):
                def do(t, i, b):
                    pe.wait_ge(S.s.sem, S.s.at(after, t))
                    if not first(t):
                        pe.wait_ge(S.v.sem, S.v.at("rest", t - 2))
                    for k in range(2):
                        ins = nc.tensor.transpose(TT[b][:, k, :], nh[b][:, k * P:(k + 1) * P], ident[:, :])
                    ins.then_inc(S.t.sem, 1)
                return do

            def product(to, h, w):
                for n, (hp, wp) in enumerate(PAIRS):
                    for k in range(2):
                        ins = nc.tensor.matmul(to, h[:, hp, k, :], w(wp, k), start=(n + k == 0),
                                               stop=(n == len(PAIRS) - 1 and k == 1))
                return ins

            pe.wait_ge(sort_begins, TILES)
            for v in range(2):
                if v:
                    pe.wait_ge(psem("hist_second"), 1)
                nc.tensor.matmul(ps_T[:, 0:TILES], zeros[:, 0:P], zeros[:, 0:TILES], start=True, stop=False,
                                 skip_group_check=True).then_inc(psem("hist_clear"), 1)
                pe.wait_ge(psem("hist_clear"), v + 1)
                with pe.Fori(0, HIST_COLS // GROUP // 2) as i:
                    for b in range(2):
                        pe.wait_ge(hist_hots, 2 * (v * (HIST_COLS // GROUP) + 2 * i + b + 1))
                        for j in range(GROUP):
                            ins = nc.tensor.matmul(ps_T[:, 0:TILES], lo_hot[:, b, j, :], hi_hot[:, b, j, :],
                                                   start=False, stop=False, skip_group_check=True)
                        ins.then_inc(hist_used, 1)
            turn_rows(0, [lambda i, q=q: raw_f[:, q, i, :] for q in range(4)])
            def prod(t, i, b):
                pe.wait_ge(IN.v.sem, IN.v.at("low", t))
                if not first(t):
                    pe.wait_ge(IN.v.sem, IN.v.at("table", t - 2))
                product(ps_M[:, b, 0:D], nhT[b], lambda q, k: W[0][:, q, 0, k, :]).then_inc(IN.t.sem, 1)
            pe.wait_ge(consts, 1)
            pe.wait_ge(weights_in[0], 16)
            walk(pe, IN.t, dict(prod=prod, hT=turn(IN)))

            find_steps(1)
            turn_rows(1, [lambda i: raw_s[:, i, :, 0], lambda i: raw_k[:, i, :], lambda i: raw_s[:, i, :, 2]])

            pe.sem_inc(half_sums, 2 * LAP)

            def sums(l):
                def pair(it, i, c):
                    for k in range(2 * c, 2 * c + 2):
                        g = LAP * i + k
                        pe.wait_ge(gathered[k], 16 * GROUP * (l * LAPS + i + 1))
                        for h in range(2):
                            pe.wait_ge(hots, l * STEPS + GROUP * g + HALF * (h + 1))
                            pe.wait_ge(added, l * STEPS + GROUP * g + HALF * (h + 1))
                            for j in range(h * HALF, (h + 1) * HALF):
                                ins = nc.tensor.matmul(ps_sum[:, j, :], onehot[:, GROUP * (k % 2) + j, :],
                                                       ring[:, GROUP * k + j, :], start=True, stop=True)
                            ins.then_inc(half_sums, 1)
                if l not in own_products:
                    walk_pairs(pe, pair)
                    return
                Q = own_products[l]

                def prod(t, i, b):
                    pe.wait_ge(Q.v.sem, Q.v.at("low", t))
                    if not first(t):
                        pe.wait_ge(Q.v.sem, Q.v.at("self", t - 2))
                    product(ps_M[:, b, 0:D], nhT[b], lambda q, k: W[(l - 1) % 2][:, q, 0, k, :]).then_inc(Q.t.sem, 1)
                walk_pairs(pe, pair, Q.t, dict(hT=turn(Q, "fetch"), prod=prod))
            sums(0)
            sums(1)
            for l, (S, n) in enumerate(((HOP, 1), (SAGE1, 2), (SAGE2, 3))):
                def prod(t, i, b):
                    pe.wait_ge(S.v.sem, S.v.at("low", t))
                    if not first(t):
                        pe.wait_ge(S.s.sem, S.s.at("table", t - 2))
                    product(ps_M[:, b, 0:D], nhT[b], lambda q, k: W[n % 2][:, q, 1, k, :]).then_inc(S.t.sem, 1)
                pe.wait_ge(weights_in[n], 32)
                pe.wait_ge(added, GROUP + (l + 2) * STEPS)
                walk(pe, S.t, dict(prod=prod, hT=turn(S)))
                pe.wait_ge(S.s.sem, S.s.at("table", TILES - 1))
                sums(l + 2)
            sums(5)

            def agg_turn(t, i, b):
                pe.wait_ge(CONV.s.sem, CONV.s.at("agg", t))
                for k in range(2):
                    ins = nc.tensor.transpose(TT[0][:, k, :], nh[b][:, k * P:(k + 1) * P], ident[:, :])
                ins.then_inc(CONV.t.sem, 1)

            def conv(t, i, b):
                pe.wait_ge(CONV.v.sem, CONV.v.at("alow", t))
                product(ps_M[:, 0, 0:D], naT, lambda q, k: W[0][:, q, 0, k, :]).then_inc(CONV.t.sem, 1)

            def h_turn(t, i, b):
                pe.wait_ge(CONV.s.sem, CONV.s.at("relu", t))
                for k in range(2):
                    ins = nc.tensor.transpose(TT[1][:, k, :], nh[b][:, k * P:(k + 1) * P], ident[:, :])
                ins.then_inc(CONV.t.sem, 1)

            def gates(t, i, b):
                pe.wait_ge(CONV.v.sem, CONV.v.at("low", t))
                product(ps_M[:, 1, 0:RELS], nhT[b], lambda q, k: gw3[:, q, k, :]).then_inc(CONV.t.sem, 1)

            def messages(u):
                def do(t, i, b):
                    out_by = CONV.s if u % 2 else CONV.v
                    if u >= 4:
                        pe.wait_ge(out_by.sem, out_by.at(f"m{u - 4}", t))
                    elif not (isinstance(t, int) and t < 1):
                        pe.wait_ge(out_by.sem, out_by.at(f"m{u + 4}", t - 1))
                    if u < 2 and isinstance(t, int) and t == 0:
                        pe.wait_ge((weights_in[4], rel_weights_in)[u], 48)
                    product(ps_sum[:, 2 * (u % 4):2 * (u % 4) + 2, :], nhT[b],
                            lambda q, k: W3[q][:, 2 * u:2 * u + 2, k, :]).then_inc(CONV.t.sem, 1)
                return do
            pe.wait_ge(conv_weights_in, 16)
            pe.wait_ge(added, GROUP + 6 * STEPS)
            walk(pe, CONV.t, dict(aT=agg_turn, prod=conv, hT=h_turn, gate=gates,
                                **{f"m{u}": messages(u) for u in range(RELS // 2)}))
            sums(6)


_INS = ['x', 'src', 'dst', 'edge_type_16', 'edge_weight', 'edge_weight1', 'L0_gnn_weight', 'L0_gnn_hop_logits',
        'L1_gnn_W_self', 'L1_gnn_W_neigh', 'L1_gnn_bias', 'L2_gnn_W', 'L2_gnn_b', 'L3_gnn_weight',
        'L3_gnn_gate_weight']


def kernel(**inputs):
    import numpy as _np
    import concourse.bacc as _bacc
    from concourse import mybir as _mybir
    from concourse.bass_utils import run_bass_kernel_spmd as _run

    nc = _bacc.Bacc("TRN2", target_bir_lowering=False, num_devices=1)
    arrays, args = {}, []
    for name in _INS:
        a = _np.ascontiguousarray(inputs[name])
        if name == 'edge_weight1':
            a = a.reshape(-1)
        arrays[f"in_{name}_dram"] = a
        args.append(nc.dram_tensor(f"in_{name}_dram", a.shape, _mybir.dt.from_np(a.dtype), kind="ExternalInput").ap())
    args.append(nc.dram_tensor("out_0_dram", (N, D), _mybir.dt.float32, kind="ExternalOutput").ap())
    gnn(nc, *args)
    r = _run(nc, [arrays], core_ids=[0])
    return r.results[0]["out_0_dram"]
```
